# Optimizing a Trainium2 kernel written in Bass

```python
import numpy as np
import jax
import jax.numpy as jnp

def _softmax(x, axis=-1):
    return jax.nn.softmax(x, axis=axis)

def _gelu(x):
    return jax.nn.gelu(x, approximate=True)

def _silu(x):
    return jax.nn.silu(x)

def _sigmoid(x):
    return jax.nn.sigmoid(x)

def _layernorm(x, axis=-1, eps=1e-05):
    m = jnp.mean(x, axis=axis, keepdims=True)
    v = jnp.var(x, axis=axis, keepdims=True)
    return (x - m) / jnp.sqrt(v + eps)

def _scatter_add(tgt, idx, src, axis=0):
    return tgt.at[idx].add(src)

def _segment_sum(src, seg, n):
    return jax.ops.segment_sum(src, seg, n)
kernel_name = 'mk_flamingo_gated_d1_seqx_r4_f37d0c'

def setup_inputs(seed: int=0):
    np.random.seed(seed)
    _w = jnp.asarray

    def _rec_inputs():
        import jax
        import jax.numpy as jnp
        _rk = jax.random.key(seed)
        x = -0.0002928 + 1 * jax.random.normal(jax.random.fold_in(_rk, 1), (32, 128, 256), jnp.float32)
        _lenS = 128 - jax.random.randint(jax.random.fold_in(_rk, 7), (32,), 0, max(1, 128 // 4) + 1, jnp.int32)
        _lenS2 = 128 - jax.random.randint(jax.random.fold_in(_rk, 8), (32,), 0, max(1, 128 // 4) + 1, jnp.int32)
        _ctx_1024P = jax.random.normal(jax.random.fold_in(_rk, 11), (32, 16, 256), jnp.float32)
        _ctx_1024c = jax.random.dirichlet(jax.random.fold_in(_rk, 511), 0.3 * jnp.ones((16,), jnp.float32), (32, 128))
        _ctx_1024t = jnp.einsum('bsk,bkd->bsd', _ctx_1024c, _ctx_1024P)
        _ctx_1024t = _ctx_1024t * jax.lax.rsqrt(jnp.mean(jnp.square(_ctx_1024t)) + 1e-12) * 0.953939
        ctx_1024 = -1.39393e-06 + 0.999914 * (_ctx_1024t + 0.3 * jax.random.normal(jax.random.fold_in(_rk, 611), (32, 128, 256), jnp.float32))
        _g = jax.random.normal(jax.random.fold_in(_rk, 9001), (2, 1), jnp.float32)
        _g = jnp.sign(_g) * jnp.maximum(jnp.abs(_g), 1.0) + (_g == 0) * 1.0
        g_xattn = _g[0]
        g_ffn = _g[1]
        return (x, ctx_1024, g_xattn, g_ffn)
    x, ctx_1024, g_xattn, g_ffn = _rec_inputs()

    def _L0_xattn_setup():
        import jax, jax.numpy as jnp
        import numpy as np
        D_MODEL = 256
        N_HEADS = 16
        D_K = D_MODEL // N_HEADS
        LOCAL_WINDOW = 128
        GLOBAL_TOKENS = 16

        def sparse_mask(seq_len):
            i = jnp.arange(seq_len)[:, None]
            j = jnp.arange(seq_len)[None, :]
            local = jnp.abs(i - j) <= LOCAL_WINDOW
            glob = (i < GLOBAL_TOKENS) | (j < GLOBAL_TOKENS)
            causal = j <= i
            return ((local | glob) & causal)[None, None]
        key = jax.random.key(seed)
        ks = jax.random.split(key, 11)
        B, S = (2, 512)
        std = 1.0 / np.sqrt(D_MODEL)
        inp = {'query': jax.random.normal(ks[0], (B, S, D_MODEL), jnp.float32), 'key': jax.random.normal(ks[1], (B, S, D_MODEL), jnp.float32), 'value': jax.random.normal(ks[2], (B, S, D_MODEL), jnp.float32), 'w_q': jax.random.normal(ks[3], (D_MODEL, D_MODEL), jnp.float32) * std, 'b_q': jnp.zeros((D_MODEL,), jnp.float32), 'w_k': jax.random.normal(ks[4], (D_MODEL, D_MODEL), jnp.float32) * std, 'b_k': jnp.zeros((D_MODEL,), jnp.float32), 'w_v': jax.random.normal(ks[5], (D_MODEL, D_MODEL), jnp.float32) * std, 'b_v': jnp.zeros((D_MODEL,), jnp.float32), 'w_o': jax.random.normal(ks[6], (D_MODEL, D_MODEL), jnp.float32) * std, 'b_o': jnp.zeros((D_MODEL,), jnp.float32)}
        return inp
    _L0_xattn_all = _L0_xattn_setup()
    _L0_xattn_in = {k: v for k, v in _L0_xattn_all.items() if k in ('w_q', 'b_q', 'w_k', 'b_k', 'w_v', 'b_v', 'w_o', 'b_o')}
    del _L0_xattn_all

    def _L0_ffn_setup():
        import jax, jax.numpy as jnp
        import numpy as np
        from jax import lax
        D = 256
        H = 1024
        E = 8
        TOPK = 2
        key = jax.random.key(seed)
        ks = jax.random.split(key, 7)
        s = 0.02
        return {'x': jax.random.normal(ks[0], (2, 512, D), dtype=jnp.float32), 'W1': jax.random.normal(ks[1], (E, D, H), dtype=jnp.float32) * s, 'b1': jnp.zeros((E, H), dtype=jnp.float32), 'W2': jax.random.normal(ks[2], (E, H, D), dtype=jnp.float32) * s, 'b2': jnp.zeros((E, D), dtype=jnp.float32), 'Wr': jax.random.normal(ks[3], (D, E), dtype=jnp.float32) * s, 'br': jnp.zeros((E,), dtype=jnp.float32)}
    _L0_ffn_all = _L0_ffn_setup()
    _L0_ffn_in = {k: v for k, v in _L0_ffn_all.items() if k in ('W1', 'b1', 'W2', 'b2', 'Wr', 'br')}
    del _L0_ffn_all
    return {'x': x, 'ctx_1024': ctx_1024, 'g_xattn': g_xattn, 'g_ffn': g_ffn, 'L0_xattn_w_q': _L0_xattn_in['w_q'], 'L0_xattn_b_q': _L0_xattn_in['b_q'], 'L0_xattn_w_k': _L0_xattn_in['w_k'], 'L0_xattn_b_k': _L0_xattn_in['b_k'], 'L0_xattn_w_v': _L0_xattn_in['w_v'], 'L0_xattn_b_v': _L0_xattn_in['b_v'], 'L0_xattn_w_o': _L0_xattn_in['w_o'], 'L0_xattn_b_o': _L0_xattn_in['b_o'], 'L0_ffn_W1': _L0_ffn_in['W1'], 'L0_ffn_b1': _L0_ffn_in['b1'], 'L0_ffn_W2': _L0_ffn_in['W2'], 'L0_ffn_b2': _L0_ffn_in['b2'], 'L0_ffn_Wr': _L0_ffn_in['Wr'], 'L0_ffn_br': _L0_ffn_in['br']}

def reference(x, ctx_1024, g_xattn, g_ffn, L0_xattn_w_q, L0_xattn_b_q, L0_xattn_w_k, L0_xattn_b_k, L0_xattn_w_v, L0_xattn_b_v, L0_xattn_w_o, L0_xattn_b_o, L0_ffn_W1, L0_ffn_b1, L0_ffn_W2, L0_ffn_b2, L0_ffn_Wr, L0_ffn_br):
    import jax
    import jax.numpy as jnp

    def _L0_xattn_ref(query, key, value, w_q, b_q, w_k, b_k, w_v, b_v, w_o, b_o):
        import jax, jax.numpy as jnp
        import numpy as np
        D_MODEL = 256
        N_HEADS = 16
        D_K = D_MODEL // N_HEADS
        LOCAL_WINDOW = 128
        GLOBAL_TOKENS = 16

        def sparse_mask(seq_len):
            i = jnp.arange(seq_len)[:, None]
            j = jnp.arange(seq_len)[None, :]
            local = jnp.abs(i - j) <= LOCAL_WINDOW
            glob = (i < GLOBAL_TOKENS) | (j < GLOBAL_TOKENS)
            causal = j <= i
            return ((local | glob) & causal)[None, None]
        B, S, _ = query.shape

        def proj(x, w, b):
            y = x @ w.T + b
            return y.reshape(B, S, N_HEADS, D_K).transpose(0, 2, 1, 3)
        q = proj(query, w_q, b_q)
        k = proj(key, w_k, b_k)
        v = proj(value, w_v, b_v)
        scores = jnp.einsum('bhqd,bhkd->bhqk', q, k) / np.sqrt(D_K).astype(np.float32)
        mask = sparse_mask(S)
        scores = jnp.where(mask, scores, -jnp.inf)
        attn = jax.nn.softmax(scores, axis=-1)
        out = jnp.einsum('bhqk,bhkd->bhqd', attn, v)
        out = out.transpose(0, 2, 1, 3).reshape(B, S, D_MODEL)
        return out @ w_o.T + b_o

    def _L0_ffn_ref(x, W1, b1, W2, b2, Wr, br):
        import jax, jax.numpy as jnp
        import numpy as np
        from jax import lax
        D = 256
        H = 1024
        E = 8
        TOPK = 2
        B, S, _ = x.shape
        xf = x.reshape(-1, D)
        logits = xf @ Wr + br
        topv, _ = lax.top_k(logits, TOPK)
        thresh = topv[:, TOPK - 1:TOPK]
        masked = jnp.where(logits >= thresh, logits, -jnp.inf)
        weights = jax.nn.softmax(masked, axis=-1)
        h = jax.nn.gelu(jnp.einsum('td,edh->eth', xf, W1) + b1[:, None, :], approximate=False)
        expert_out = jnp.einsum('eth,ehd->etd', h, W2) + b2[:, None, :]
        out = jnp.einsum('etd,te->td', expert_out, weights)
        return out.reshape(B, S, D)
    x = x + jnp.tanh(g_xattn[0]) * _L0_xattn_ref(_layernorm(x, axis=-1), ctx_1024, ctx_1024, L0_xattn_w_q, L0_xattn_b_q, L0_xattn_w_k, L0_xattn_b_k, L0_xattn_w_v, L0_xattn_b_v, L0_xattn_w_o, L0_xattn_b_o)
    x = x + jnp.tanh(g_ffn[0]) * _L0_ffn_ref(_layernorm(x, axis=-1), L0_ffn_W1, L0_ffn_b1, L0_ffn_W2, L0_ffn_b2, L0_ffn_Wr, L0_ffn_br)
    return x

_drawn_inputs = setup_inputs


def setup_inputs(seed=0):
    import zlib

    import numpy as np

    out = dict(_drawn_inputs(seed))
    spreads = {'L0_xattn_b_q': (0.0, 0.38),
     'L0_xattn_b_k': (0.0, 0.8),
     'L0_xattn_b_v': (0.0, 0.1),
     'L0_xattn_b_o': (0.0, 0.1),
     'L0_ffn_b1': (0.0, 0.369),
     'L0_ffn_b2': (0.0, 0.1),
     'L0_ffn_br': (0.0, 0.1)}
    factors = {}
    for name, (base, spread) in spreads.items():
        noise = np.random.default_rng([zlib.crc32(name.encode()), seed]).standard_normal(out[name].shape)
        drawn = base * np.exp(spread * noise) if base else spread * noise
        out[name] = jnp.asarray(drawn.astype(out[name].dtype))
    for name, factor in factors.items():
        out[name] = (out[name] * factor).astype(out[name].dtype)
    return out
```

```python
import concourse.bass as bass
from concourse import mybir
from contextlib import ExitStack

F32 = mybir.dt.float32
F32R = mybir.dt.float32r
F16 = mybir.dt.float16
BF16 = mybir.dt.bfloat16
I32 = mybir.dt.int32
ALU = mybir.AluOpType
ACT = mybir.ActivationFunctionType
AX = mybir.AxisListType.X
ADD_ALL = bass.bass_isa.ReduceOp.add
MAX_ALL = bass.bass_isa.ReduceOp.max

P = 128
B, S, D = 32, 128, 256
T = B * S
HEADS, DK = 16, 16
KC = D // P
H = 1024
HC = H // P
E = 8
GT = 2
NG = B // GT
PAIRS = HEADS // 2
VA = DK + 1
QUADS = 4 * GT
EPS = 1e-5
MASKED = -1e30

REG = T + P
ROW = D + E + 8
MAIN_TILES = (2 * T + E * (P - 1)) // P
ALL_TILES = E * T // P
EARLY = 4
X_SCALE = 1024.0
OFF_BIG = 1.0e6


class Links:

    def __init__(self, eng, sem):
        self.eng, self.sem, self.k = eng, sem, 0

    def __call__(self, ins):
        self.k += 1
        ins.then_inc(self.sem, 1)
        self.eng.wait_ge(self.sem, self.k)

    def later(self, ins):
        self.k += 1
        ins.then_inc(self.sem, 1)

    def wait(self):
        self.eng.wait_ge(self.sem, self.k)

    def restart(self):
        if self.k:
            self.eng.sem_clear(self.sem)
        self.k = 0


def there(g):
    return 0 <= g < NG if isinstance(g, int) else True


def bass_flamingo(nc, x, ctx_in, g_xattn, g_ffn, w_q, b_q, w_k, b_k, w_v, b_v, w_o, b_o,
                  W1, b1, W2, b2, Wr, br, out):
    xs_dram = nc.dram_tensor("token_rows", [E * REG + P, ROW], F32, kind="Internal").ap()
    w_dram = nc.dram_tensor("split_weights", [E, 2, P, 2 * 2048], F16, kind="Internal").ap()

    with ExitStack() as stack:
        def sb(name, shape, dt=F32):
            return stack.enter_context(nc.sbuf_tensor(name, shape, dt))

        def sem(name):
            return stack.enter_context(nc.semaphore(name))

        wts = sb("wts", [P, E, 4 * 2048], F16)
        stacked = wts[:, E - 2:E, :].rearrange("p e n -> p (e n)").bitcast(F32)
        stacked = stacked.rearrange("p (w a j t) -> p w a j t", w=2, a=2, j=PAIRS)
        qst = [stacked[:, 0, i] for i in range(2)]
        kst = [stacked[:, 1, i] for i in range(2)]
        passing = wts[:, E - 4:E - 2, :].rearrange("p e n -> p (e n)")
        stage = [passing[:, 4096 * i:4096 * (i + 1)].bitcast(F32) for i in range(2)]
        split = [passing[:, 8192 + 4096 * i:8192 + 4096 * (i + 1)].rearrange("p (a n) -> p a n", a=2)
                 for i in range(2)]

        ident = sb("ident", [P, P])
        negident = sb("negident", [P, P], F32R)
        ident16 = sb("ident16", [P, P], BF16)
        mask4 = sb("mask4", [P, 4, P], BF16)
        earlier = sb("earlier", [P, P], BF16)
        ones16 = sb("ones16", [P, P], BF16)
        rank1 = sb("rank1", [P, 8])
        rank0 = sb("rank0", [P, 8])
        ones8 = sb("ones8", [P, 8])
        region0 = sb("region0", [P, 8])
        base = sb("base", [P, 8])
        mostsel = sb("mostsel", [P, GT])
        tgx = sb("tgx", [P, 1])
        tgf = sb("tgf", [P, 1])
        gates_in = sb("gates_in", [P, 2])
        power = sb("power", [P, GT])
        wscale = sb("wscale", [P, 2, 8])
        wsquares = sb("wsquares", [P, 2, 8])
        padrow = sb("padrow", [P, ROW])
        all_slots = sb("all_slots", [P, B, 8], I32)
        b1t = sb("b1t", [P, E, HC])
        bank = [stack.enter_context(nc.psum_tensor(f"bank{i}", [P, 512], F32)) for i in range(8)]

        env = dict(locals())
        attention_and_routing(nc, env)
        experts(nc, env)


def attention_and_routing(nc, env):
    (x, ctx_in, g_xattn, g_ffn, w_q, b_q, w_k, b_k, w_v, b_v, w_o, b_o, W1, b1, W2, Wr, br, out,
     xs_dram, w_dram, bank, qst, kst, ident, negident, ident16, mask4, earlier, ones16, rank1,
     rank0, ones8, region0, base, mostsel, tgx, tgf, gates_in, power, wscale, wsquares, padrow,
     b1t, stage, split, all_slots, wts) = (env[k] for k in (
         "x", "ctx_in", "g_xattn", "g_ffn", "w_q", "b_q", "w_k", "b_k", "w_v", "b_v", "w_o", "b_o",
         "W1", "b1", "W2", "Wr", "br", "out", "xs_dram", "w_dram", "bank", "qst", "kst", "ident",
         "negident", "ident16", "mask4", "earlier", "ones16", "rank1", "rank0", "ones8", "region0",
         "base", "mostsel", "tgx", "tgf", "gates_in", "power", "wscale", "wsquares", "padrow",
         "b1t", "stage", "split", "all_slots", "wts"))
    with ExitStack() as stack:
        def sb(name, shape, dt=F32):
            return stack.enter_context(nc.sbuf_tensor(name, shape, dt))

        def sem(name):
            return stack.enter_context(nc.semaphore(name))

        wq, wk, wv, wo = (sb(f"w{c}_sb", [P, KC, D]) for c in "qkvo")
        wr = sb("wr_sb", [P, KC, E])
        bqk = sb("bqk", [P, 2, 2])
        bv_all, bo_all = sb("bv_all", [P, D]), sb("bo_all", [P, D])
        br_all = sb("br_all", [P, E])
        xin = [sb(f"xin{i}", [P, GT, D]) for i in range(2)]
        cin = [sb(f"cin{i}", [P, GT, D]) for i in range(2)]
        xn = sb("xn", [P, GT, D])
        xT, cT = sb("xT", [P, KC, GT * P]), sb("cT", [P, KC, GT * P])
        xb = [sb(f"xb{i}", [P, GT, D]) for i in range(2)]
        queries, keys = sb("queries", [P, 2, GT * P]), sb("keys", [P, 2, GT * P])
        va = [sb(f"va{i}", [P, GT, HEADS, VA]) for i in range(2)]
        rowmax = [sb(f"rowmax{i}", [P, 4], F32R) for i in range(2)]
        probs = [sb(f"probs{i}", [P, 4, P]) for i in range(4)]
        rden = sb("rden", [P, HEADS])
        ao = [sb(f"ao{i}", [P, HEADS, DK]) for i in range(2)]
        aoT = [sb(f"aoT{i}", [P, KC, P]) for i in range(2)]
        x2 = [sb(f"x2_{i}", [P, GT, D]) for i in range(2)]
        pay = [sb(f"pay{i}", [P, GT, ROW]) for i in range(2)]
        x2T = sb("x2T", [P, KC, GT * P])
        bn, bn1 = sb("bn", [P, GT, 6]), sb("bn1", [P, GT, 6])
        mv1, mv2 = sb("mv1", [P, GT, 2]), sb("mv2", [P, GT, 2])
        rs1, rs2 = sb("rs1", [P, GT]), sb("rs2", [P, GT])
        partsum = sb("partsum", [P, 1])
        ebits = sb("ebits", [P, 1], I32)
        wsum, wnow = sb("wsum", [P, 2]), sb("wnow", [P, 2])
        ints = sb("ints", [P, 3, 8], I32)
        lg, mx, lgs = sb("lg", [P, GT, E]), sb("mx", [P, GT, 8]), sb("lgs", [P, GT, E])
        msk, msk16 = sb("msk", [P, GT, E]), sb("msk16", [P, GT, E], BF16)
        ex, em, esum, erec = sb("ex", [P, GT, E]), sb("em", [P, GT, E]), sb("esum", [P, GT]), sb("erec", [P, GT])
        cnt, cm, inv = sb("cnt", [P, GT, E]), sb("cm", [P, GT, E]), sb("inv", [P, GT, E])
        pos, slotf = sb("pos", [P, GT, E]), sb("slotf", [P, GT, E])
        sel, selpos = sb("sel", [P, GT, 8, E]), sb("selpos", [P, GT, 8, E])
        slots = sb("slots", [P, GT, 8], I32)

        BT = bank[0]
        PJA, PJB = bank[1], bank[2]
        SB = [bank[3], bank[4]]
        TB = [bank[5], bank[6]]
        OB = bank[7]

        consts, const_steps = sem("consts"), sem("const_steps")
        params = sem("params")
        tanh_ready, bias_ready = sem("tanh_ready"), sem("bias_ready")
        x_loaded, c_loaded, kst_ready, qst_ready, x2_stored, scattered, w_staged, w_stored = (
            [sem(f"{name}{i}") for i in range(2)] for name in (
                "x_loaded", "c_loaded", "kst_ready", "qst_ready", "x2_stored", "scattered",
                "w_staged", "w_stored"))
        var1_ready, rstd1_ready, xn_ready = sem("var1_ready"), sem("rstd1_ready"), sem("xn_ready")
        cT_psum, cT_ready = sem("cT_psum"), sem("cT_ready")
        xT_psum, xT_ready = sem("xT_psum"), sem("xT_ready")
        k_psum, keys_ready = sem("k_psum"), sem("keys_ready")
        q_psum, queries_ready = sem("q_psum"), sem("queries_ready")
        v_psum, va_ready = sem("v_psum"), sem("va_ready")
        s_psum, max_ready = sem("s_psum"), sem("max_ready")
        st_psum, exp_ready, probs_ready = sem("st_psum"), sem("exp_ready"), sem("probs_ready")
        pv_psum, ao_ready = sem("pv_psum"), sem("ao_ready")
        aoT_psum, aoT_ready = sem("aoT_psum"), sem("aoT_ready")
        o_psum, x2_ready = sem("o_psum"), sem("x2_ready")
        xb_ready = sem("xb_ready")
        var2_ready, rstd2_ready, xn2_ready = sem("var2_ready"), sem("rstd2_ready"), sem("xn2_ready")
        x2T_psum, x2T_ready = sem("x2T_psum"), sem("x2T_ready")
        r_psum, logits_read, shifted_ready = sem("r_psum"), sem("logits_read"), sem("shifted_ready")
        ex_ready, pos_psum, pos_read = sem("ex_ready"), sem("pos_psum"), sem("pos_read")
        slots_ready = sem("slots_ready")
        w_sums, w_total, w_scaled = sem("w_sums"), sem("w_total"), sem("w_scaled")
        w_high, w_low = sem("w_high"), sem("w_low")
        mask_ready = sem("mask_ready")
        early_weights = sem("early_weights")
        dve_consts, waits_taken = sem("dve_consts"), sem("waits_taken")
        dve_steps, pool_steps = sem("dve_steps"), sem("pool_steps")


        def bt_before(g, k):
            order = [(cT_ready, 1, lambda i: i + 1), (xT_ready, 1, lambda i: i + 1),
                     (x2T_ready, -1, lambda i: 2 * i + 1), (aoT_ready, -1, lambda i: 2 * i + 2),
                     (x2T_ready, -1, lambda i: 2 * i + 2), (aoT_ready, 0, lambda i: 2 * i + 1)]
            while True:
                k -= 1
                if k < 0:
                    g, k = g - 1, 5
                s, d, count = order[k]
                if there(g + d):
                    return s, count(g + d)
                if isinstance(g, int) and g < -2:
                    return None

        def free_bt(pe, g, k):
            w = bt_before(g, k)
            if w:
                pe.wait_ge(*w)

        def loop_over_groups(eng, it):
            for g in (-2, -1, 0, 1):
                it(g, g % 2, g // 2)
            with eng.Fori(0, (NG - 4) // 2) as u:
                it(u * 2 + 2, 0, u + 1)
                it(u * 2 + 3, 1, u + 1)
            for g in range(NG - 2, NG + 2):
                it(g, g % 2, g // 2)

        def arrived(eng, sems, g, par, dmas=1, ok=True):
            if ok:
                eng.wait_ge(sems[par], (g - par) * (8 * dmas) + 16 * dmas)

        def settled(eng):
            eng.sem_inc(waits_taken, 1)

        def when(eng, ok, s, value):
            if ok:
                eng.wait_ge(s, value)

        with nc.Block() as block:

            @block.sync
            def _(sp):
                def load(dst, src):
                    sp.dma_start(dst, src).then_inc(params, 16)

                def group_rows(a, g):
                    return a[bass.ds(g * (GT * P), GT * P), :].rearrange("(b p) d -> p b d", p=P)

                def it(g, par, half):
                    if there(g + 2):
                        when(sp, there(g), xn_ready, g + 1)
                        settled(sp)
                        when(sp, there(g), xb_ready, g + 1)
                        settled(sp)
                        when(sp, there(g), cT_psum, g + 1)
                        settled(sp)
                        sp.dma_start(xin[par][:, :, :], group_rows(x, g + 2)).then_inc(x_loaded[par], 16)
                        sp.dma_start(cin[par][:, :, :], group_rows(ctx_in, g + 2)).then_inc(c_loaded[par], 16)
                    if isinstance(g, int) and g == -2:
                        load(wk[:, :, :], w_k.rearrange("(k p) n -> p k n", p=P))
                        load(bqk[:, 0, :], b_q)
                        load(bqk[:, 1, :], b_k)
                        load(wq[:, :, :], w_q.rearrange("(k p) n -> p k n", p=P))
                        load(wv[:, :, :], w_v.rearrange("(k p) n -> p k n", p=P))
                        load(bv_all[:, :], b_v.partition_broadcast(P))
                        load(wo[:, :, :], w_o.rearrange("(k p) n -> p k n", p=P))
                        load(bo_all[:, :], b_o.partition_broadcast(P))
                        load(wr[:, :, :], Wr.rearrange("(k p) n -> p k n", p=P))
                        load(br_all[:, :], br.partition_broadcast(P))
                        load(gates_in[:, 0:1], g_xattn.partition_broadcast(P))
                        load(gates_in[:, 1:2], g_ffn.partition_broadcast(P))
                        load(b1t[:, :, :], b1)
                        sp.wait_ge(consts, 2)
                        load(out[T:T + P, :], padrow[:, 0:D])
                        load(xs_dram[E * REG:E * REG + P, :], padrow[:, :])
                    if there(g):
                        when(sp, there(g - 2), w_low, (g - 1) * 4)
                        settled(sp)
                        e = half
                        if par == 0:
                            src = W1[bass.ds(e, 1), :, :].rearrange("a (k p) n -> p (a k) n", p=P)
                            dst = stage[0].rearrange("p (k n) -> p k n", k=KC)
                        else:
                            src = W2[bass.ds(e, 1), :, :].rearrange("a (k p) n -> p (a k) n", p=P)
                            dst = stage[1].rearrange("p (k n) -> p k n", k=HC)
                        sp.dma_start(dst, src).then_inc(w_staged[par], 16)
                    if there(g + 1):
                        for src, st, src_ready, dst_ready in ((keys, kst, keys_ready, kst_ready),
                                                              (queries, qst, queries_ready, qst_ready)):
                            sp.wait_ge(src_ready, g + 2)
                            settled(sp)
                            when(sp, there(g - 1), st_psum, g * QUADS)
                            settled(sp)
                            for odd in range(2):
                                sp.dma_start(st[1 - par][64 * odd:64 * odd + DK, :, :],
                                             src[:, odd, :]).then_inc(dst_ready[1 - par], 16)
                    if there(g - 1):
                        sp.wait_ge(x2_ready, g * GT)
                        settled(sp)
                        sp.dma_start(group_rows(out, g - 1), x2[1 - par][:, :, :]).then_inc(x2_stored[1 - par], 16)
                        sp.wait_ge(w_low, g * 4)
                        settled(sp)
                        e = half - (1 - par)
                        rows = w_dram[bass.ds(e, 1), 1 - par, :, :].rearrange("a p n -> p (a n)")
                        sp.dma_start(rows, split[1 - par].rearrange("p a n -> p (a n)")).then_inc(w_stored[1 - par], 16)
                    if isinstance(g, int) and g == NG - 2:
                        for i in range(2):
                            arrived(sp, w_stored, 2 * (EARLY - 1) + i, i)
                            settled(sp)
                        for e in range(EARLY):
                            sp.dma_start(wts[:, e, :].rearrange("p (a n) -> p a n", a=2),
                                         w_dram[e].rearrange("a p n -> p a n")).then_inc(early_weights, 16)

                loop_over_groups(sp, it)
                for i in range(2):
                    arrived(sp, x2_stored, NG - 2 + i, i)
                    settled(sp)
                    arrived(sp, w_stored, NG - 2 + i, i)
                    settled(sp)
                sp.wait_ge(params, 16 * 15)
                sp.wait_ge(early_weights, 16 * EARLY)

            @block.gpsimd
            def _(pool):
                step = Links(pool, pool_steps)
                step.later(pool.memset(ident[:, :], 0.0))
                step.later(pool.memset(mask4[:, :, :], 0.0))
                step.later(pool.memset(earlier[:, :], 1.0))
                step.later(pool.memset(padrow[:, :], 0.0))
                for i in range(2):
                    step.later(pool.memset(pay[i][:, :, D + E:], 0.0))
                step(pool.memset(power[:, :], -0.5))
                pool.iota(padrow[:, D + E:D + E + 1].bitcast(I32), pattern=[[0, 1]], base=T,
                          channel_multiplier=1).then_inc(consts, 1)
                pool.affine_select(out=ident[:, :], in_=ident[:, :], compare_op=ALU.not_equal,
                                   fill=1.0, base=0, pattern=[[-1, P]], channel_multiplier=1).then_inc(consts, 1)
                pool.affine_select(out=mask4[:, :, :], in_=mask4[:, :, :], compare_op=ALU.is_ge,
                                   fill=MASKED, base=0, pattern=[[0, 4], [-1, P]],
                                   channel_multiplier=1).then_inc(consts, 1)
                pool.affine_select(out=earlier[:, :], in_=earlier[:, :], compare_op=ALU.is_gt,
                                   fill=0.0, base=0, pattern=[[1, P]], channel_multiplier=-1).then_inc(consts, 1)
                pool.iota(ints[:, 0, :], pattern=[[1, 8]], base=0, channel_multiplier=0).then_inc(consts, 1)
                pool.iota(ints[:, 1, :], pattern=[[1, 8]], base=1, channel_multiplier=0).then_inc(consts, 1)
                pool.iota(ints[:, 2, :], pattern=[[REG, 8]], base=0, channel_multiplier=0).then_inc(consts, 1)
                for i in range(2):
                    pool.iota(pay[i][:, :, D + E:D + E + 1].bitcast(I32), pattern=[[P, GT], [0, 1]],
                              base=(i - 2) * GT * P, channel_multiplier=1).then_inc(consts, 1)

                def it(g, par, half):
                    for n in range(QUADS):
                        q, pg = (QUADS - 1, g - 1) if n == 0 else (n - 1, g)
                        if there(pg):
                            pool.wait_ge(exp_ready, pg * QUADS + q + 1)
                            settled(pool)
                            pool.affine_select(out=probs[q % 4][:, :, :], in_=probs[q % 4][:, :, :],
                                               compare_op=ALU.is_ge, fill=0.0, base=0,
                                               pattern=[[0, 4], [1, P]],
                                               channel_multiplier=-1).then_inc(probs_ready, 1)
                        if n in (1, 5) and there(g - 1):
                            b = n // 4
                            pool.wait_ge(var2_ready, (g - 1) * GT + b + 1)
                            pool.tensor_tensor(rs2[:, b:b + 1], mv2[:, b, 1:2], power[:, 0:1],
                                               ALU.pow).then_inc(rstd2_ready, 1)
                        if n == 5 and there(g + 1):
                            arrived(pool, x_loaded, g + 1, 1 - par)
                            when(pool, there(g - 1), x2_ready, g * GT)
                            pool.wait_ge(bias_ready, 1)
                            pool.tensor_tensor(xb[1 - par][:, :, :], xin[1 - par][:, :, :],
                                               bo_all[:, :].unsqueeze(1).to_broadcast([P, GT, D]),
                                               ALU.add).then_inc(xb_ready, 1)
                        if n == 5 and there(g):
                            pool.wait_ge(w_sums, g + 1)
                            when(pool, there(g - 1), w_scaled, g)
                            settled(pool)
                            pool.partition_all_reduce(wsum[:, par:par + 1], partsum[:, :], P,
                                                      ADD_ALL).then_inc(w_total, 1)
                        if n >= 4 and there(g - 2):
                            b, r = (n - 4) // 2, n % 2
                            if n == 4:
                                pool.wait_ge(slots_ready, g - 1)
                                settled(pool)
                            pool.indirect_dma_start(
                                out=xs_dram[:, :],
                                out_offset=bass.IndirectOffsetOnAxis(ap=slots[:, b, r:r + 1], axis=0),
                                in_=pay[par][:, b, :], in_offset=None,
                                bounds_check=E * REG - 1, oob_is_err=False).then_inc(scattered[par], 16)
                        if n == 7 and there(g + 2):
                            pool.wait_ge(var1_ready, g + 3)
                            when(pool, there(g + 1), xn_ready, g + 2)
                            pool.tensor_tensor(rs1[:, :], mv1[:, :, 1], power[:, 0:GT],
                                               ALU.pow).then_inc(rstd1_ready, 1)

                loop_over_groups(pool, it)
                for i in range(2):
                    arrived(pool, scattered, NG - 2 + i, i, 4)

            @block.scalar
            def _(act):
                act.wait_ge(params, 16 * 15)
                act.activation(tgx[:, :], gates_in[:, 0:1], ACT.Tanh).then_inc(tanh_ready, 1)
                act.activation(tgf[:, :], gates_in[:, 1:2], ACT.Tanh).then_inc(tanh_ready, 1)

                def it(g, par, half):
                    g1, p1 = g + 1, 1 - par
                    for n in range(QUADS):
                        q, pg = (QUADS - 1, g - 1) if n == 0 else (n - 1, g)
                        if there(pg):
                            act.wait_ge(st_psum, pg * QUADS + q + 1)
                            before = there(pg - 1) if q < 4 else True
                            when(act, before, pv_psum, pg * QUADS + q - 3)
                            act.activation(probs[q % 4][:, :, :].rearrange("p a q -> p (a q)"), TB[q % 2][:, :],
                                           ACT.Exp, scale=float(DK) ** -0.5).then_inc(exp_ready, 1)
                        if n == 0 and there(g1):
                            act.wait_ge(cT_psum, g1 + 1)
                            when(act, there(g), v_psum, g + 1)
                            act.activation(cT[:, :, :].rearrange("p k t -> p (k t)"), BT[:, :],
                                           ACT.Copy).then_inc(cT_ready, 1)
                        if n == 0 and there(g - 2):
                            act.wait_ge(shifted_ready, g - 1)
                            when(act, there(g - 3), slots_ready, g - 2)
                            act.activation(ex[:, :, :], lgs[:, :, :], ACT.Exp).then_inc(ex_ready, 1)
                        if n in (1, 3) and there(g1):
                            w, dst, ps, psum, done, restacked = (
                                (1, keys, k_psum, PJB, keys_ready, kst_ready) if n == 1 else
                                (0, queries, q_psum, PJA, queries_ready, qst_ready))
                            act.wait_ge(ps, g1 + 1)
                            arrived(act, restacked, g, par, 2, there(g))
                            for odd in range(2):
                                last = act.activation(dst[:, odd, :], psum[:, 256 * odd:256 * odd + 256],
                                                      ACT.Identity, bias=bqk[:, w, odd:odd + 1])
                            last.then_inc(done, 1)
                        if n == 1 and there(g1):
                            act.wait_ge(xT_psum, g1 + 1)
                            when(act, there(g), q_psum, g + 1)
                            act.activation(xT[:, :, :].rearrange("p k t -> p (k t)"), BT[:, :],
                                           ACT.Copy).then_inc(xT_ready, 1)
                        if n in (2, 6) and there(g - 1):
                            b = n // 4
                            act.wait_ge(x2T_psum, (g - 1) * GT + b + 1)
                            when(act, there(g - 2), r_psum, g - 1)
                            act.activation(x2T[:, :, b * P:(b + 1) * P],
                                           BT[:, 0:D].rearrange("p (k t) -> p k t", k=KC),
                                           ACT.Copy).then_inc(x2T_ready, 1)
                        if (n == 3 and there(g - 1)) or (n == 7 and there(g)):
                            b, tg = (1, g - 1) if n == 3 else (0, g)
                            act.wait_ge(aoT_psum, tg * GT + b + 1)
                            when(act, there(tg - 1), o_psum, (tg - 1) * GT + b + 1)
                            act.activation(aoT[b][:, :, :].rearrange("p k t -> p (k t)"), BT[:, 0:D],
                                           ACT.Copy).then_inc(aoT_ready, 1)
                        if n == 4 and there(g):
                            arrived(act, w_staged, g, par)
                            when(act, there(g - 1), w_total, g)
                            arrived(act, w_stored, g - 2, par, 1, there(g - 2))
                            act.activation(split[par][:, 1, :].bitcast(BF16), stage[par][:, :], ACT.Square,
                                           accum_out=partsum[:, :]).then_inc(w_sums, 1)
                        if n == 7 and there(g):
                            act.wait_ge(w_scaled, g + 1)
                            act.activation(split[par][:, 0, :], stage[par][:, :], ACT.Copy,
                                           scale=wnow[:, par:par + 1]).then_inc(w_high, 1)

                loop_over_groups(act, it)

            @block.vector
            def _(dve):
                step = Links(dve, dve_steps)
                for i in range(2):
                    step.later(dve.memset(va[i][:, :, :, DK:DK + 1], 1.0))
                step.later(dve.memset(mostsel[:, :], 0.0))
                step.later(dve.memset(ones8[:, :], 1.0))
                step.later(dve.memset(ones16[:, :], 1.0))
                dve.wait_ge(consts, 9)
                step.later(dve.tensor_copy(rank0[:, :], ints[:, 0, :]))
                step.later(dve.tensor_copy(rank1[:, :], ints[:, 1, :]))
                step.later(dve.tensor_copy(region0[:, :], ints[:, 2, :]))
                step.later(dve.tensor_copy(base[:, :], ints[:, 2, :]))
                step.later(dve.tensor_scalar(negident[:, :], ident[:, :], -1.0, None, ALU.mult))
                dve.tensor_copy(ident16[:, :], ident[:, :]).then_inc(dve_consts, 1)
                step.wait()
                dve.wait_ge(tanh_ready, 2)
                dve.tensor_scalar(bo_all[:, :], bo_all[:, :], tgx[:, 0:1], None, ALU.mult).then_inc(bias_ready, 1)

                def variance(src, bn_, mv, done):
                    step(dve.bn_stats(bn_, src))
                    step(dve.bn_aggr(mv, bn_))
                    dve.tensor_scalar_add(mv[:, 1:2], mv[:, 1:2], EPS).then_inc(done, 1)

                def normalise(g, b):
                    t = g * GT + b
                    dve.wait_ge(pv_psum, (t + 1) * 4)
                    when(dve, there(g - 1), aoT_psum, t - 1)
                    o = OB[:, 0:HEADS * VA].rearrange("p (h v) -> p h v", h=HEADS)
                    step(dve.reciprocal(rden[:, :], o[:, :, DK]))
                    dve.tensor_tensor(ao[b][:, :, :], o[:, :, 0:DK],
                                      rden[:, :].unsqueeze(2).to_broadcast([P, HEADS, DK]),
                                      ALU.mult).then_inc(ao_ready, 1)

                def residual(g, b, psum, i):
                    t = g * GT + b
                    dve.wait_ge(o_psum, t + 1)
                    dve.wait_ge(xb_ready, g + 1)
                    arrived(dve, x2_stored, g - 2, i, 1, there(g - 2))
                    dve.scalar_tensor_tensor(out=x2[i][:, b, :], in0=psum[:, 0:D], scalar=tgx[:, 0:1],
                                             in1=xb[i][:, b, :], op0=ALU.mult, op1=ALU.add).then_inc(x2_ready, 1)
                    dve.wait_ge(x2_ready, t + 1)
                    variance(x2[i][:, b, :], bn[:, b, :], mv2[:, b, :], var2_ready)

                def norm2(g, b, i):
                    dve.wait_ge(rstd2_ready, g * GT + b + 1)
                    arrived(dve, scattered, g - 2, i, 4, there(g - 2))
                    dve.tensor_scalar(pay[i][:, b, 0:D], x2[i][:, b, :], mv2[:, b, 0:1], rs2[:, b:b + 1],
                                      ALU.subtract, ALU.mult).then_inc(xn2_ready, 1)

                def over_ranks(a):
                    return a.unsqueeze(2).to_broadcast([P, GT, 8, E])

                def it(g, par, half):
                    settled(dve)
                    step.restart()
                    g1, p1 = g + 1, 1 - par
                    for n in range(QUADS):
                        if there(g):
                            dve.wait_ge(s_psum, g * QUADS + n + 1)
                            when(dve, n >= 2 or there(g - 1), st_psum, g * QUADS + n - 1)
                            dve.tensor_reduce(rowmax[n % 2][:, :], SB[n % 2][:, :].rearrange("p (a k) -> p a k", a=4),
                                              AX, ALU.max).then_inc(max_ready, 1)
                        if n % 2 == 0 and there(g - 1):
                            c = slice(256 * n, 256 * n + 512)
                            if n == 0:
                                dve.wait_ge(w_high, g)
                            dve.scalar_tensor_tensor(out=split[p1][:, 1, c], in0=stage[p1][:, c],
                                                     scalar=wnow[:, p1:p1 + 1], in1=split[p1][:, 0, c],
                                                     op0=ALU.mult, op1=ALU.subtract).then_inc(w_low, 1)
                        if n == 0 and there(g1):
                            dve.wait_ge(rstd1_ready, g1 + 1)
                            when(dve, there(g), xT_psum, g + 1)
                            for b in range(GT):
                                last = dve.tensor_scalar(xn[:, b, :], xin[p1][:, b, :], mv1[:, b, 0:1],
                                                         rs1[:, b:b + 1], ALU.subtract, ALU.mult)
                            last.then_inc(xn_ready, 1)
                        if n == 0 and there(g - 1):
                            residual(g - 1, 0, PJA, p1)
                        if n == 1 and there(g - 1):
                            norm2(g - 1, 0, p1)
                        if n == 1 and there(g - 2):
                            dve.wait_ge(ex_ready, g - 1)
                            step(dve.tensor_tensor(em[:, :, :], ex[:, :, :], msk[:, :, :], ALU.mult))
                            for b in range(GT):
                                step.later(dve.tensor_tensor_scan(cnt[:, b, :], ones8[:, :], msk[:, b, :], 0.0,
                                                                  ALU.mult, ALU.add))
                            step(dve.tensor_reduce(esum[:, :], em[:, :, :], AX, ALU.add))
                            step.later(dve.reciprocal(erec[:, :], esum[:, :]))
                            step.later(dve.tensor_tensor(cm[:, :, :], cnt[:, :, :], msk[:, :, :], ALU.mult))
                            step(dve.tensor_tensor(mostsel[:, :], mostsel[:, :], cnt[:, :, E - 1], ALU.max))
                            step.later(dve.scalar_tensor_tensor(
                                out=pay[par][:, :, D:D + E], in0=em[:, :, :], scalar=tgf[:, 0:1],
                                in1=erec[:, :].unsqueeze(2).to_broadcast([P, GT, E]), op0=ALU.mult, op1=ALU.mult))
                            if True:
                                numbers = pay[par][:, :, D + E:D + E + 1].bitcast(I32)
                                step.later(dve.tensor_scalar(numbers, numbers, float(2 * GT * P), None, ALU.add))
                            step.later(dve.tensor_tensor(inv[:, :, :], rank0[:, :].unsqueeze(1).to_broadcast([P, GT, 8]),
                                                         cnt[:, :, E - 1:E].to_broadcast([P, GT, 8]), ALU.is_ge))
                            step(dve.tensor_tensor(sel[:, :, :, :], over_ranks(cm[:, :, :]),
                                                   rank1[:, :].unsqueeze(1).unsqueeze(3).to_broadcast([P, GT, 8, E]),
                                                   ALU.is_equal))
                        if n == 2 and there(g - 2):
                            dve.wait_ge(pos_psum, g - 1)
                            step(dve.tensor_tensor(pos[:, :, :], PJA[:, 0:GT * E].rearrange("p (b e) -> p b e", b=GT),
                                                   base[:, :].unsqueeze(1).to_broadcast([P, GT, E]), ALU.add))
                            dve.tensor_tensor(base[:, :], base[:, :], PJA[:, GT * E:GT * E + E],
                                              ALU.add).then_inc(pos_read, 1)
                            step(dve.tensor_tensor(selpos[:, :, :, :], sel[:, :, :, :], over_ranks(pos[:, :, :]), ALU.mult))
                            step(dve.tensor_reduce(slotf[:, :, :], selpos[:, :, :, :], AX, ALU.add))
                            arrived(dve, scattered, g - 3, p1, 4, there(g - 3))
                            dve.scalar_tensor_tensor(out=slots[:, :, :], in0=inv[:, :, :], scalar=OFF_BIG,
                                                     in1=slotf[:, :, :], op0=ALU.mult,
                                                     op1=ALU.add).then_inc(slots_ready, 1)
                            dve.wait_ge(slots_ready, g - 1)
                            step.later(dve.tensor_copy(all_slots[:, bass.ds((g - 2) * GT, GT), :], slots[:, :, :]))
                        if n == 3 and there(g1):
                            dve.wait_ge(v_psum, g1 + 1)
                            when(dve, there(g - 1), pv_psum, g * QUADS)
                            dve.tensor_tensor(va[p1][:, :, :, 0:DK],
                                              PJB[:, :].rearrange("p (b h v) -> p b h v", b=GT, h=HEADS),
                                              bv_all[:, :].rearrange("p (h v) -> p h v", h=HEADS).unsqueeze(1)
                                              .to_broadcast([P, GT, HEADS, DK]), ALU.add).then_inc(va_ready, 1)
                        if n == 3 and there(g - 1):
                            normalise(g - 1, 1)
                        if n == 4 and there(g - 1):
                            residual(g - 1, 1, PJB, p1)
                        if n == 5 and there(g - 1):
                            norm2(g - 1, 1, p1)
                        if n == 6 and there(g + 2):
                            arrived(dve, x_loaded, g + 2, par)
                            for b in range(GT):
                                step.later(dve.bn_stats(bn1[:, b, :], xin[par][:, b, :]))
                            when(dve, there(g1), xn_ready, g1 + 1)
                            step.wait()
                            settled(dve)
                            for b in range(GT):
                                step.later(dve.bn_aggr(mv1[:, b, :], bn1[:, b, :]))
                            step.wait()
                            dve.tensor_scalar_add(mv1[:, :, 1:2], mv1[:, :, 1:2], EPS).then_inc(var1_ready, 1)
                        if n == 6 and there(g):
                            dve.wait_ge(w_total, g + 1)
                            step(dve.tensor_scalar(ebits[:, :], wsum[:, par:par + 1].bitcast(I32), 24, None,
                                                   ALU.logical_shift_right))
                            dve.tensor_scalar(wnow[:, par:par + 1].bitcast(I32), ebits[:, :], -float(1 << 23),
                                              204.0 * (1 << 23), ALU.mult, ALU.add).then_inc(w_scaled, 1)
                            dve.wait_ge(w_scaled, g + 1)
                            e = half
                            dve.tensor_copy(wscale[:, par, bass.ds(e, 1)], wnow[:, par:par + 1])
                            step(dve.tensor_copy(wsquares[:, par, bass.ds(e, 1)], wsum[:, par:par + 1]))
                        if n == 7 and there(g):
                            normalise(g, 0)
                        if n == 7 and there(g - 1):
                            dve.wait_ge(r_psum, g)
                            dve.tensor_tensor(lg[:, :, :], PJA[:, 0:GT * E].rearrange("p (b e) -> p b e", b=GT),
                                              br_all[:, :].unsqueeze(1).to_broadcast([P, GT, E]),
                                              ALU.add).then_inc(logits_read, 1)
                            dve.wait_ge(logits_read, g)
                            settled(dve)
                            for b in range(GT):
                                last = dve.max(mx[:, b, :], lg[:, b, :])
                            step(last)
                            step.later(dve.tensor_tensor(msk[:, :, :], lg[:, :, :],
                                                         mx[:, :, 1:2].to_broadcast([P, GT, E]), ALU.is_ge))
                            dve.tensor_tensor(msk16[:, :, :], lg[:, :, :],
                                              mx[:, :, 1:2].to_broadcast([P, GT, E]), ALU.is_ge).then_inc(mask_ready, 1)
                            dve.tensor_tensor(lgs[:, :, :], lg[:, :, :], mx[:, :, 0:1].to_broadcast([P, GT, E]),
                                              ALU.subtract).then_inc(shifted_ready, 1)
                            dve.wait_ge(shifted_ready, g)

                loop_over_groups(dve, it)

            @block.tensor
            def _(pe):
                pe.wait_ge(dve_consts, 1)
                pe.wait_ge(params, 16 * 15)

                def transposes(parts, done):
                    for i, (src, n) in enumerate(parts):
                        last = pe.transpose(BT[:, i * P:(i + 1) * P], src, ident[:, :])
                    last.then_inc(done, 1)

                def product(psum, lhsT, rhs):
                    for k in range(KC):
                        last = pe.matmul(psum, lhsT(k), rhs(k), start=k == 0, stop=k == KC - 1)
                    return last

                def it(g, par, half):
                    g1, p1 = g + 1, 1 - par
                    for n in range(QUADS):
                        idx = g * QUADS + n
                        odd, pairs = n % 2, range(4 * ((n % 4) // 2), 4 * ((n % 4) // 2) + 4)
                        if there(g):
                            if n == 0:
                                arrived(pe, kst_ready, g, par, 2)
                                arrived(pe, qst_ready, g, par, 2)
                            when(pe, n >= 2 or there(g - 1), max_ready, idx - 1)
                            ps, rows = SB[n % 2], slice(64 * odd, 64 * odd + DK)
                            tok = slice((n // 4) * P, (n // 4) * P + P)
                            pe.matmul(ps[:, :], ident16[:, :], mask4[:, :, :].rearrange("p a k -> p (a k)"),
                                      start=True, stop=False)
                            for i, j in enumerate(pairs):
                                last = pe.matmul(ps[:, i * P:(i + 1) * P], qst[par][rows, j, tok],
                                                 kst[par][rows, j, tok], start=False, stop=i == 3)
                            last.then_inc(s_psum, 1)
                        if n == 0 and there(g - 1):
                            pe.wait_ge(aoT_ready, (g - 1) * GT + 1)
                            when(pe, there(g - 2), logits_read, g - 1)
                            product(PJA[:, 0:D], lambda k: aoT[0][:, k, :], lambda k: wo[:, k, :]).then_inc(o_psum, 1)
                        if n == 0 and there(g1):
                            arrived(pe, c_loaded, g1, p1)
                            free_bt(pe, g, 0)
                            transposes([(cin[p1][:, b, k * P:(k + 1) * P], 0) for k in range(KC) for b in range(GT)],
                                       cT_psum)
                        if n == 1 and there(g - 2):
                            pe.wait_ge(mask_ready, g - 1)
                            when(pe, there(g - 1), x2_ready, (g - 1) * GT + 1)
                            pe.matmul(PJA[:, 0:E], earlier[:, :], msk16[:, 0, :], start=True, stop=True)
                            pe.matmul(PJA[:, E:2 * E], earlier[:, :], msk16[:, 1, :], start=True, stop=False)
                            pe.matmul(PJA[:, E:2 * E], ones16[:, :], msk16[:, 0, :], start=False, stop=True)
                            pe.matmul(PJA[:, 2 * E:3 * E], ones16[:, :], msk16[:, 0, :], start=True, stop=False)
                            pe.matmul(PJA[:, 2 * E:3 * E], ones16[:, :], msk16[:, 1, :], start=False,
                                      stop=True).then_inc(pos_psum, 1)
                        if n == 1 and there(g1):
                            pe.wait_ge(cT_ready, g1 + 1)
                            when(pe, there(g), va_ready, g + 1)
                            when(pe, there(g - 2), x2_ready, (g - 1) * GT)
                            for o in range(2):
                                last = product(PJB[:, 256 * o:256 * o + 256], lambda k: wk[:, k, o * P:(o + 1) * P],
                                               lambda k: cT[:, k, :])
                            last.then_inc(k_psum, 1)
                            pe.wait_ge(xn_ready, g1 + 1)
                            free_bt(pe, g, 1)
                            transposes([(xn[:, b, k * P:(k + 1) * P], 0) for k in range(KC) for b in range(GT)],
                                       xT_psum)
                        if n == 2 and there(g1):
                            pe.wait_ge(keys_ready, g1 + 1)
                            for b in range(GT):
                                last = product(PJB[:, 256 * b:256 * b + 256], lambda k: cT[:, k, b * P:(b + 1) * P],
                                               lambda k: wv[:, k, :])
                            last.then_inc(v_psum, 1)
                        if n in (2, 6) and there(g - 1):
                            b = n // 4
                            pe.wait_ge(xn2_ready, (g - 1) * GT + b + 1)
                            free_bt(pe, g, 2 if n == 2 else 4)
                            transposes([(pay[p1][:, b, k * P:(k + 1) * P], 0) for k in range(KC)], x2T_psum)
                        if n == 3 and there(g1):
                            pe.wait_ge(xT_ready, g1 + 1)
                            when(pe, there(g - 1), x2_ready, (g - 1) * GT + 1)
                            when(pe, there(g - 2), pos_read, g - 1)
                            when(pe, there(g), queries_ready, g + 1)
                            for o in range(2):
                                last = product(PJA[:, 256 * o:256 * o + 256], lambda k: wq[:, k, o * P:(o + 1) * P],
                                               lambda k: xT[:, k, :])
                            last.then_inc(q_psum, 1)
                        if there(g if n >= 1 else g - 1):
                            tg, m, i = (g, n - 1, par) if n >= 1 else (g - 1, QUADS - 1, p1)
                            odd, pairs = m % 2, range(4 * ((m % 4) // 2), 4 * ((m % 4) // 2) + 4)
                            rows, tok = slice(64 * odd, 64 * odd + DK), slice((m // 4) * P, (m // 4) * P + P)
                            pe.wait_ge(max_ready, tg * QUADS + m + 1)
                            when(pe, m >= 2 or there(tg - 1), exp_ready, tg * QUADS + m - 1)
                            ps = TB[m % 2]
                            for a in range(4):
                                pe.matmul(ps[:, a * P:(a + 1) * P], rowmax[m % 2][:, a:a + 1].to_broadcast([P, P]),
                                          negident[:, :], start=a == 0, stop=False)
                            for a, j in enumerate(pairs):
                                last = pe.matmul(ps[:, a * P:(a + 1) * P], kst[i][rows, j, tok],
                                                 qst[i][rows, j, tok], start=False, stop=a == 3)
                            last.then_inc(st_psum, 1)
                        if there(g if n >= 3 else g - 1):
                            tg, m, i = (g, n - 3, par) if n >= 3 else (g - 1, n + 5, p1)
                            b, odd, pairs = m // 4, m % 2, range(4 * ((m % 4) // 2), 4 * ((m % 4) // 2) + 4)
                            pe.wait_ge(probs_ready, tg * QUADS + m + 1)
                            if m == 0:
                                pe.wait_ge(va_ready, tg + 1)
                            if m % 4 == 0:
                                when(pe, b == 1 or there(tg - 1), ao_ready, tg * GT + b)
                            for a, j in enumerate(pairs):
                                h = 2 * j + odd
                                last = pe.matmul(OB[:, h * VA:(h + 1) * VA], probs[m % 4][:, a, :],
                                                 va[i][:, b, h, :], start=True, stop=True)
                            last.then_inc(pv_psum, 1)
                        if (n == 3 and there(g - 1)) or (n == 7 and there(g)):
                            b, tg = (1, g - 1) if n == 3 else (0, g)
                            pe.wait_ge(ao_ready, tg * GT + b + 1)
                            free_bt(pe, g, 3 if n == 3 else 5)
                            flat = ao[b][:, :, :].rearrange("p h v -> p (h v)")
                            transposes([(flat[:, k * P:(k + 1) * P], 0) for k in range(KC)], aoT_psum)
                        if n == 4 and there(g - 1):
                            pe.wait_ge(aoT_ready, (g - 1) * GT + 2)
                            when(pe, there(g1), va_ready, g1 + 1)
                            when(pe, there(g - 2), x2_ready, (g - 1) * GT)
                            product(PJB[:, 0:D], lambda k: aoT[1][:, k, :], lambda k: wo[:, k, :]).then_inc(o_psum, 1)
                        if n == 7 and there(g - 1):
                            pe.wait_ge(x2T_ready, g * GT)
                            when(pe, there(g1), queries_ready, g1 + 1)
                            when(pe, there(g - 2), pos_read, g - 1)
                            pe.wait_ge(x2_ready, g * GT)
                            for b in range(GT):
                                last = product(PJA[:, b * E:(b + 1) * E], lambda k: x2T[:, k, b * P:(b + 1) * P],
                                               lambda k: wr[:, k, :])
                            last.then_inc(r_psum, 1)

                loop_over_groups(pe, it)


def experts(nc, env):
    (out, b2, xs_dram, w_dram, bank, wts, ident, region0, base, mostsel, wscale, wsquares, padrow,
     b1t, all_slots) = (env[k] for k in (
         "out", "b2", "xs_dram", "w_dram", "bank", "wts", "ident", "region0", "base", "mostsel",
         "wscale", "wsquares", "padrow", "b1t", "all_slots"))
    with ExitStack() as stack:
        def sb(name, shape, dt=F32):
            return stack.enter_context(nc.sbuf_tensor(name, shape, dt))

        def sem(name):
            return stack.enter_context(nc.semaphore(name))

        b2_all = sb("b2_all", [P, E, D])
        xs = [sb(f"xs{i}", [P, ROW]) for i in range(4)]
        xh = [sb(f"xh{i}", [P, 2, KC, P], F16) for i in range(2)]
        hf = [sb(f"hf{i}", [P, HC, P]) for i in range(2)]
        hh = [sb(f"hh{i}", [P, 2, HC, P], F16) for i in range(2)]
        yb = [sb(f"yb{i}", [P, D]) for i in range(2)]
        yg = [sb(f"yg{i}", [P, D]) for i in range(2)]
        gscale, hscale, yscale = sb("gscale", [P, E]), sb("hscale", [P, E]), sb("yscale", [P, E])
        small = sb("small", [P, 6, E])
        smallint = sb("smallint", [P, 3, E], I32)
        b1sq = sb("b1sq", [P, E, HC])
        pcol, minus_T = sb("pcol", [P, 1]), sb("minus_T", [P, E])
        padidx = sb("padidx", [P, E], I32)
        most = sb("most", [P, 2])
        mostint = sb("mostint", [P, 1], I32)
        tile_no_int, tile_no = sb("tile_no_int", [1, ALL_TILES], I32), sb("tile_no", [1, ALL_TILES])
        past, pastn = sb("past", [1, ALL_TILES, E]), sb("pastn", [1, ALL_TILES, E])
        te, ts = sb("te", [1, ALL_TILES]), sb("ts", [1, ALL_TILES])
        tile_expert, tile_row = sb("tile_expert", [1, ALL_TILES], I32), sb("tile_row", [1, ALL_TILES], I32)
        tie_idx = sb("tie_idx", [P, 8], I32)
        tie_row = sb("tie_row", [P, ROW])

        XT = bank[0]
        HB = [(bank[1], bank[2]), (bank[3], bank[4])]
        YB = [bank[5], bank[6]]

        weights_in, b2_in, pads_in, ties_in = sem("weights_in"), sem("b2_in"), sem("pads_in"), sem("ties_in")
        numbers_made, pad_rows_ready, table_ready = sem("numbers_made"), sem("pad_rows_ready"), sem("table_ready")
        b1_sums, b1_total, most_ready, most_total = sem("b1_sums"), sem("b1_total"), sem("most_ready"), sem("most_total")
        scales_ready, rows_placed = sem("scales_ready"), sem("rows_placed")
        row_in = [sem(f"row_in{i}") for i in range(4)]
        added = [sem(f"added{i}") for i in range(2)]
        xT_psum, xhi_ready, xlo_ready = sem("xT_psum"), sem("xhi_ready"), sem("xlo_ready")
        h_psum, gelu_ready, split_ready = sem("h_psum"), sem("gelu_ready"), sem("split_ready")
        y_psum, yb_ready, yg_ready = sem("y_psum"), sem("yb_ready"), sem("yg_ready")
        dve_steps, pool_steps, waits_taken = sem("dve_steps"), sem("pool_steps"), sem("waits_taken")

        def settled(eng):
            eng.sem_inc(waits_taken, 1)

        def pipeline(eng, it, lo, hi):
            def peeled(a, b):
                for i in range(a, b):
                    it(i, i % 4, lambda k, i=i: lo <= i + k < hi)

            first = -(-(lo + 1) // 4) * 4
            rounds = (hi - 3 - first) // 4
            peeled(lo - 2, first)
            with eng.Fori(0, rounds) as u:
                for m in range(4):
                    it(u * 4 + (first + m), m, lambda k: True)
            peeled(first + 4 * rounds, hi)

        def all_tiles(eng, it):
            pipeline(eng, it, 0, MAIN_TILES)
            ties = eng.value_load(mostint[0:1, 0:1], min_val=0, max_val=E)
            with eng.If(ties > 2):
                pipeline(eng, it, MAIN_TILES, ALL_TILES)

        def when(eng, ok, s, value):
            if ok:
                eng.wait_ge(s, value)

        def before(i, n):
            return i >= n if isinstance(i, int) else True

        def expert_of(eng, i):
            return eng.value_load(tile_expert[0:1, bass.ds(i, 1)], min_val=0, max_val=E - 1)

        def added_value(i, m):
            return (i - m % 2) * 8 + 16

        with nc.Block() as block:

            @block.sync
            def _(sp):
                for e in range(EARLY, E):
                    sp.dma_start(wts[:, e, :].rearrange("p (a n) -> p a n", a=2),
                                 w_dram[e].rearrange("a p n -> p a n")).then_inc(weights_in, 16)
                sp.dma_start(b2_all[:, :, :].rearrange("p e d -> p (e d)"), b2.partition_broadcast(P)).then_inc(b2_in, 16)
                sp.wait_ge(rows_placed, 1)
                sp.wait_ge(table_ready, 1)

                def it(i, m, there):
                    if there(2):
                        j = i + 2
                        when(sp, before(j, 4), added[m % 2], added_value(i - 2, (m + 2) % 4))
                        settled(sp)
                        row = sp.value_load(tile_row[0:1, bass.ds(j, 1)], min_val=0, max_val=E * REG)
                        sp.dma_start(xs[(m + 2) % 4][:, :], xs_dram[bass.ds(row, P), :]).then_inc(row_in[(m + 2) % 4], 16)

                all_tiles(sp, it)
                sp.wait_ge(weights_in, 16 * (E - EARLY))
                sp.wait_ge(b2_in, 16)

            @block.gpsimd
            def _(pool):
                step = Links(pool, pool_steps)
                pool.iota(tile_no_int[:, :], pattern=[[1, ALL_TILES]], base=0, channel_multiplier=0).then_inc(numbers_made, 1)
                pool.wait_ge(most_ready, 1)
                pool.partition_all_reduce(most[:, 1:2], most[:, 0:1], P, MAX_ALL).then_inc(most_total, 1)
                pool.wait_ge(b1_sums, 1)
                pool.partition_all_reduce(small[:, 1, :], small[:, 0, :], P, ADD_ALL).then_inc(b1_total, 1)
                pool.wait_ge(pad_rows_ready, 1)
                for e in range(E):
                    pool.indirect_dma_start(out=xs_dram[:, :],
                                            out_offset=bass.IndirectOffsetOnAxis(ap=padidx[:, e:e + 1], axis=0),
                                            in_=padrow[:, :], in_offset=None).then_inc(pads_in, 16)
                pool.wait_ge(pads_in, 16 * E)
                pool.wait_ge(table_ready, 1)
                ties = pool.value_load(mostint[0:1, 0:1], min_val=0, max_val=E)
                with pool.If(ties > 2):
                    with pool.Fori(0, B) as t:
                        step(pool.tensor_copy(tie_idx[:, :], all_slots[:, bass.ds(t, 1), :].rearrange("p a r -> p (a r)")))
                        pool.indirect_dma_start(out=tie_row[:, :], out_offset=None, in_=xs_dram[:, :],
                                                in_offset=bass.IndirectOffsetOnAxis(ap=tie_idx[:, 0:1], axis=0)
                                                ).then_inc(ties_in, 16)
                        pool.wait_ge(ties_in, 16)
                        for r in range(2, 8):
                            pool.indirect_dma_start(out=xs_dram[:, :],
                                                    out_offset=bass.IndirectOffsetOnAxis(ap=tie_idx[:, r:r + 1], axis=0),
                                                    in_=tie_row[:, :], in_offset=None, bounds_check=E * REG - 1,
                                                    oob_is_err=False).then_inc(ties_in, 16)
                        pool.wait_ge(ties_in, 16 * 7)
                        pool.sem_clear(ties_in)
                        step.restart()
                pool.sem_inc(rows_placed, 1)

                def it(i, m, there):
                    if there(0):
                        pool.wait_ge(yg_ready, i + 1)
                        when(pool, before(i, 1), added[(m + 1) % 2], added_value(i - 1, (m + 3) % 4))
                        settled(pool)
                        pool.indirect_dma_start(
                            out=out[:, :],
                            out_offset=bass.IndirectOffsetOnAxis(ap=xs[m][:, D + E:D + E + 1].bitcast(I32), axis=0),
                            in_=yg[m % 2][:, :], in_offset=None, compute_op=ALU.add).then_inc(added[m % 2], 16)

                def last(tiles):
                    for i in (tiles - 2, tiles - 1):
                        pool.wait_ge(added[i % 2], added_value(i, i % 4))

                pipeline(pool, it, 0, MAIN_TILES)
                last(MAIN_TILES)
                ties = pool.value_load(mostint[0:1, 0:1], min_val=0, max_val=E)
                with pool.If(ties > 2):
                    pipeline(pool, it, MAIN_TILES, ALL_TILES)
                    last(ALL_TILES)

            @block.scalar
            def _(act):
                act.wait_ge(scales_ready, 1)
                act.wait_ge(table_ready, 1)

                def it(i, m, there):
                    if there(2):
                        act.wait_ge(xT_psum, i + 3)
                        when(act, before(i + 2, 2), h_psum, (i + 1) * 2)
                        act.activation(xh[m % 2][:, 0, :, :], XT[:, 0:D].rearrange("p (k t) -> p k t", k=KC), ACT.Copy,
                                       scale=X_SCALE).then_inc(xhi_ready, 1)
                    if there(1):
                        e = expert_of(act, i + 1)
                        for half in range(2):
                            act.wait_ge(h_psum, (i + 1) * 2 + half + 1)
                            when(act, half == 0 and before(i + 1, 2), split_ready, i * 2)
                            for c in range(4):
                                last = act.activation(
                                    hf[(m + 1) % 2][:, 4 * half + c, :], HB[(m + 1) % 2][half][:, c * P:(c + 1) * P],
                                    ACT.Gelu, bias=b1t[:, bass.ds(e, 1), 4 * half + c], scale=gscale[:, bass.ds(e, 1)])
                            last.then_inc(gelu_ready, 1)
                    if there(0):
                        e = expert_of(act, i)
                        act.wait_ge(yb_ready, i + 1)
                        when(act, before(i, 2), added[m % 2], added_value(i - 2, (m + 2) % 4))
                        act.activation(yg[m % 2][:, :], yb[m % 2][:, :], ACT.Copy,
                                       scale=xs[m][:, bass.ds(e + D, 1)]).then_inc(yg_ready, 1)

                all_tiles(act, it)

            @block.vector
            def _(dve):
                step = Links(dve, dve_steps)
                dve.tensor_reduce(most[:, 0:1], mostsel[:, :], AX, ALU.max).then_inc(most_ready, 1)
                step.later(dve.memset(minus_T[:, :], -float(T)))
                step.later(dve.tensor_copy(pcol[:, :], padrow[:, D + E:D + E + 1].bitcast(I32)))
                step(dve.tensor_tensor(b1sq[:, :, :], b1t[:, :, :], b1t[:, :, :], ALU.mult))
                dve.tensor_reduce(small[:, 0, :], b1sq[:, :, :], AX, ALU.add).then_inc(b1_sums, 1)
                dve.scalar_tensor_tensor(out=padidx[:, :], in0=base[:, :], scalar=pcol[:, 0:1],
                                         in1=minus_T[:, :], op0=ALU.add, op1=ALU.add).then_inc(pad_rows_ready, 1)
                step(dve.tensor_tensor(small[:, 2, :], base[:, :], region0[:, :], ALU.subtract))
                step(dve.tensor_scalar(smallint[:, 0, :], small[:, 2, :], float(P - 1), None, ALU.add))
                step(dve.tensor_scalar(smallint[:, 1, :], smallint[:, 0, :], 7, None, ALU.logical_shift_right))
                step.later(dve.memset(small[:, 4, :], 1.0))
                step(dve.tensor_copy(small[:, 3, :], smallint[:, 1, :]))
                step.later(dve.tensor_tensor_scan(small[:, 5, :], small[:, 4, :], small[:, 3, :], 0.0, ALU.mult, ALU.add))
                dve.wait_ge(numbers_made, 1)
                step(dve.tensor_copy(tile_no[:, :], tile_no_int[:, :]))

                def by_tile(a):
                    return a.unsqueeze(1).to_broadcast([1, ALL_TILES, E])

                step(dve.tensor_tensor(past[:, :, :], tile_no[:, :].unsqueeze(2).to_broadcast([1, ALL_TILES, E]),
                                       by_tile(small[0:1, 5, :]), ALU.is_ge))
                step.later(dve.tensor_tensor(pastn[:, :, :], past[:, :, :], by_tile(small[0:1, 3, :]), ALU.mult))
                step(dve.tensor_reduce(te[:, :], past[:, :, :], AX, ALU.add))
                step.later(dve.tensor_scalar(tile_expert[:, :], te[:, :], float(E - 1), None, ALU.min))
                step(dve.tensor_reduce(ts[:, :], pastn[:, :, :], AX, ALU.add))
                step(dve.tensor_tensor(ts[:, :], tile_no[:, :], ts[:, :], ALU.subtract))
                step.later(dve.tensor_scalar(te[:, :], te[:, :], float(REG), None, ALU.mult))
                step(dve.tensor_scalar(ts[:, :], ts[:, :], float(P), None, ALU.mult))
                step(dve.tensor_tensor(ts[:, :], ts[:, :], te[:, :], ALU.add))
                step(dve.tensor_scalar(tile_row[:, :], ts[:, :], float(E * REG), None, ALU.min))
                dve.wait_ge(most_total, 1)
                dve.tensor_copy(mostint[:, :], most[:, 1:2]).then_inc(table_ready, 1)

                one = float(1 << 23)
                dve.tensor_scalar(gscale[:, :].bitcast(I32), wscale[:, 0, :].bitcast(I32), -1.0, 244 * one,
                                  ALU.mult, ALU.add)
                dve.wait_ge(b1_total, 1)
                step(dve.scalar_tensor_tensor(out=small[:, 0, :], in0=wsquares[:, 0, :], scalar=256.0,
                                              in1=small[:, 1, :], op0=ALU.mult, op1=ALU.add))
                step(dve.tensor_scalar(small[:, 0, :], small[:, 0, :], 2.0, None, ALU.mult))
                step(dve.tensor_scalar(smallint[:, 0, :], small[:, 0, :].bitcast(I32), 24, None, ALU.logical_shift_right))
                step(dve.tensor_scalar(hscale[:, :].bitcast(I32), smallint[:, 0, :], -one, 204 * one,
                                       ALU.mult, ALU.add))
                step.later(dve.tensor_scalar(small[:, 0, :].bitcast(I32), hscale[:, :].bitcast(I32), -1.0, 254 * one,
                                             ALU.mult, ALU.add))
                step(dve.tensor_scalar(small[:, 1, :].bitcast(I32), wscale[:, 1, :].bitcast(I32), -1.0, 254 * one,
                                       ALU.mult, ALU.add))
                dve.tensor_tensor(yscale[:, :], small[:, 0, :], small[:, 1, :], ALU.mult).then_inc(scales_ready, 1)
                dve.wait_ge(scales_ready, 1)
                dve.wait_ge(b2_in, 16)

                def it(i, m, there):
                    if there(2):
                        dve.wait_ge(xhi_ready, i + 3)
                        dve.scalar_tensor_tensor(out=xh[m % 2][:, 1, :, :].rearrange("p k t -> p (k t)"),
                                                 in0=XT[:, 0:D], scalar=X_SCALE,
                                                 in1=xh[m % 2][:, 0, :, :].rearrange("p k t -> p (k t)"),
                                                 op0=ALU.mult, op1=ALU.subtract).then_inc(xlo_ready, 1)
                    if there(0):
                        e = expert_of(dve, i)
                        dve.wait_ge(y_psum, i + 1)
                        when(dve, before(i, 2), yg_ready, i - 1)
                        dve.scalar_tensor_tensor(out=yb[m % 2][:, :], in0=YB[m % 2][:, 0:D],
                                                 scalar=yscale[:, bass.ds(e, 1)],
                                                 in1=b2_all[:, bass.ds(e, 1), :].rearrange("p a d -> p (a d)"),
                                                 op0=ALU.mult, op1=ALU.add).then_inc(yb_ready, 1)
                    if there(1):
                        e = expert_of(dve, i + 1)
                        b = (m + 1) % 2
                        for half in range(2):
                            c = slice(4 * half, 4 * half + 4)
                            dve.wait_ge(gelu_ready, (i + 1) * 2 + half + 1)
                            when(dve, half == 0 and before(i + 1, 2), y_psum, i)
                            high = hh[b][:, 0, c, :].rearrange("p c t -> p (c t)")
                            full = hf[b][:, c, :].rearrange("p c t -> p (c t)")
                            step(dve.tensor_scalar(high, full, hscale[:, bass.ds(e, 1)], None, ALU.mult))
                            dve.scalar_tensor_tensor(out=hh[b][:, 1, c, :].rearrange("p c t -> p (c t)"), in0=full,
                                                     scalar=hscale[:, bass.ds(e, 1)], in1=high,
                                                     op0=ALU.mult, op1=ALU.subtract).then_inc(split_ready, 1)
                    settled(dve)
                    step.restart()

                settled(dve)
                step.restart()
                all_tiles(dve, it)

            @block.tensor
            def _(pe):
                pe.wait_ge(weights_in, 16 * (E - EARLY))
                pe.wait_ge(table_ready, 1)

                def it(i, m, there):
                    if there(2):
                        pe.wait_ge(row_in[(m + 2) % 4], row_value(i + 2, (m + 2) % 4))
                        when(pe, before(i + 2, 1), xlo_ready, i + 2)
                        for k in range(KC):
                            last = pe.transpose(XT[:, k * P:(k + 1) * P], xs[(m + 2) % 4][:, k * P:(k + 1) * P],
                                                ident[:, :])
                        last.then_inc(xT_psum, 1)
                    if there(1):
                        e = expert_of(pe, i + 1)
                        b = (m + 1) % 2
                        pe.wait_ge(xlo_ready, i + 2)
                        for half in range(2):
                            when(pe, before(i + 1, 2), gelu_ready, i * 2 + half - 1)
                            for c in range(4):
                                terms = [(wp, xp, k) for wp, xp in ((0, 0), (0, 1), (1, 0)) for k in range(KC)]
                                for q, (wp, xp, k) in enumerate(terms):
                                    at = wp * 2048 + k * H + (4 * half + c) * P
                                    last = pe.matmul(HB[b][half][:, c * P:(c + 1) * P], wts[:, bass.ds(e, 1), at:at + P],
                                                     xh[b][:, xp, k, :], start=q == 0, stop=q == 5)
                            last.then_inc(h_psum, 1)
                    if there(0):
                        e = expert_of(pe, i)
                        b = m % 2
                        when(pe, before(i, 2), yb_ready, i - 1)
                        terms = [(hp, wp, c) for half in range(2) for hp, wp in ((0, 0), (1, 0), (0, 1))
                                 for c in range(4 * half, 4 * half + 4)]
                        for q, (hp, wp, c) in enumerate(terms):
                            if q in (0, 12):
                                pe.wait_ge(split_ready, i * 2 + (1 if q == 0 else 2))
                            at = 4096 + wp * 2048 + c * D
                            last = pe.matmul(YB[b][:, 0:D], hh[b][:, hp, c, :], wts[:, bass.ds(e, 1), at:at + D],
                                             start=q == 0, stop=q == 23)
                        last.then_inc(y_psum, 1)

                def row_value(i, m):
                    return (i - m) * 4 + 16

                all_tiles(pe, it)


def kernel(**inputs):
    import numpy as np
    import concourse.bacc as bacc
    from concourse.bass_utils import run_bass_kernel_spmd as run

    a = {k: np.asarray(v) for k, v in inputs.items()}
    order = np.arange(D).reshape(PAIRS, 2, DK).transpose(1, 2, 0).reshape(D)

    def w(name):
        return a["L0_xattn_w_" + name].T

    def bias(name):
        return a["L0_xattn_b_" + name]

    arrays = {
        "x": a["x"].reshape(T, D),
        "ctx_in": a["ctx_1024"].reshape(T, D),
        "g_xattn": a["g_xattn"], "g_ffn": a["g_ffn"],
        "w_q": w("q")[:, order], "b_q": bias("q")[order].reshape(2, P).T,
        "w_k": w("k")[:, order], "b_k": bias("k")[order].reshape(2, P).T,
        "w_v": w("v"), "b_v": bias("v"), "w_o": w("o"), "b_o": bias("o"),
        "W1": a["L0_ffn_W1"], "b1": a["L0_ffn_b1"].reshape(E, HC, P).transpose(2, 0, 1),
        "W2": a["L0_ffn_W2"], "b2": a["L0_ffn_b2"].reshape(E * D),
        "Wr": a["L0_ffn_Wr"], "br": a["L0_ffn_br"],
    }
    arrays = {k: np.ascontiguousarray(v) for k, v in arrays.items()}
    nc = bacc.Bacc("TRN2", target_bir_lowering=False, num_devices=1)
    aps = [nc.dram_tensor(f"in_{k}", v.shape, mybir.dt.from_np(v.dtype), kind="ExternalInput").ap()
           for k, v in arrays.items()]
    out = nc.dram_tensor("out_rows", [T + P, D], F32, kind="ExternalOutput").ap()
    bass_flamingo(nc, *aps, out)
    r = run(nc, [{f"in_{k}": v for k, v in arrays.items()}], core_ids=[0])
    return r.results[0]["out_rows"][:T].reshape(B, S, D)
```

```python
import concourse.bass as bass
from concourse import mybir
from contextlib import ExitStack

F32 = mybir.dt.float32
F32R = mybir.dt.float32r
F16 = mybir.dt.float16
BF16 = mybir.dt.bfloat16
I32 = mybir.dt.int32
ALU = mybir.AluOpType
ACT = mybir.ActivationFunctionType
AX = mybir.AxisListType.X
ADD_ALL = bass.bass_isa.ReduceOp.add
MAX_ALL = bass.bass_isa.ReduceOp.max

P = 128
B, S, D = 32, 128, 256
T = B * S
HEADS, DK = 16, 16
KC = D // P
H = 1024
HC = H // P
E = 8
GT = 2
NG = B // GT
PAIRS = HEADS // 2
VA = DK + 1
PRODUCTS = ((0, 0), (0, 1), (1, 0), (0, 2), (2, 0), (1, 1))
STACK = len(PRODUCTS) * DK
QUADS = 4 * GT
EPS = 1e-5
MASKED = -1e30

TILE = 2 * P
REG = T + TILE
ROW = D + E + 8
MAIN_TILES = (2 * T + E * (TILE - 1)) // TILE
ALL_TILES = E * T // TILE
EARLY = 4
X_SCALE = 1024.0
OFF_BIG = 1.0e6


class Links:

    def __init__(self, eng, sem):
        self.eng, self.sem, self.k = eng, sem, 0

    def __call__(self, ins):
        self.k += 1
        ins.then_inc(self.sem, 1)
        self.eng.wait_ge(self.sem, self.k)

    def later(self, ins):
        self.k += 1
        ins.then_inc(self.sem, 1)

    def wait(self):
        self.eng.wait_ge(self.sem, self.k)

    def restart(self):
        if self.k:
            self.eng.sem_clear(self.sem)
        self.k = 0


def there(g):
    return 0 <= g < NG if isinstance(g, int) else True


def bass_flamingo(nc, x, ctx_in, g_xattn, g_ffn, w_q, b_q, w_k, b_k, w_v, b_v, w_o, b_o,
                  W1, b1, W2, b2, Wr, br, out):
    xs_dram = nc.dram_tensor("token_rows", [E * REG + TILE, ROW], F32, kind="Internal").ap()
    w_dram = nc.dram_tensor("split_weights", [E, 2, P, 2 * 2048], F16, kind="Internal").ap()

    with ExitStack() as stack:
        def sb(name, shape, dt=F32):
            return stack.enter_context(nc.sbuf_tensor(name, shape, dt))

        def sem(name):
            return stack.enter_context(nc.semaphore(name))

        wts = sb("wts", [P, E, 4 * 2048], F16)
        stacked = wts[:, E - 2:E, :].rearrange("p e n -> p (e n)").bitcast(BF16)
        stacked = stacked.rearrange("p (w a h t) -> p w a h t", w=2, a=2, h=HEADS)
        qst = [stacked[0:STACK, 0, i] for i in range(2)]
        kst = [stacked[0:STACK, 1, i] for i in range(2)]
        passing = wts[:, E - 4:E - 2, :].rearrange("p e n -> p (e n)")
        stage = [passing[:, 4096 * i:4096 * (i + 1)].bitcast(F32) for i in range(2)]
        split = [passing[:, 8192 + 4096 * i:8192 + 4096 * (i + 1)].rearrange("p (a n) -> p a n", a=2)
                 for i in range(2)]

        ident = sb("ident", [P, P])
        negident = sb("negident", [P, P], F32R)
        ident16 = sb("ident16", [P, P], BF16)
        mask4 = sb("mask4", [P, 4, P], BF16)
        earlier = sb("earlier", [P, P], BF16)
        ones16 = sb("ones16", [P, P], BF16)
        rank1 = sb("rank1", [P, 8])
        rank0 = sb("rank0", [P, 8])
        ones8 = sb("ones8", [P, 8])
        region0 = sb("region0", [P, 8])
        base = sb("base", [P, 8])
        mostsel = sb("mostsel", [P, GT])
        tgx = sb("tgx", [P, 1])
        tgf = sb("tgf", [P, 1])
        gates_in = sb("gates_in", [P, 2])
        power = sb("power", [P, GT])
        wscale = sb("wscale", [P, 2, 8])
        wsquares = sb("wsquares", [P, 2, 8])
        padrow = sb("padrow", [P, ROW])
        all_slots = sb("all_slots", [P, B, 8], I32)
        b1t = sb("b1t", [P, E, HC])
        bank = [stack.enter_context(nc.psum_tensor(f"bank{i}", [P, 512], F32)) for i in range(8)]

        env = dict(locals())
        attention_and_routing(nc, env)
        experts(nc, env)


def attention_and_routing(nc, env):
    (x, ctx_in, g_xattn, g_ffn, w_q, b_q, w_k, b_k, w_v, b_v, w_o, b_o, W1, b1, W2, Wr, br, out,
     xs_dram, w_dram, bank, qst, kst, ident, negident, ident16, mask4, earlier, ones16, rank1,
     rank0, ones8, region0, base, mostsel, tgx, tgf, gates_in, power, wscale, wsquares, padrow,
     b1t, stage, split, all_slots, wts) = (env[k] for k in (
         "x", "ctx_in", "g_xattn", "g_ffn", "w_q", "b_q", "w_k", "b_k", "w_v", "b_v", "w_o", "b_o",
         "W1", "b1", "W2", "Wr", "br", "out", "xs_dram", "w_dram", "bank", "qst", "kst", "ident",
         "negident", "ident16", "mask4", "earlier", "ones16", "rank1", "rank0", "ones8", "region0",
         "base", "mostsel", "tgx", "tgf", "gates_in", "power", "wscale", "wsquares", "padrow",
         "b1t", "stage", "split", "all_slots", "wts"))
    with ExitStack() as stack:
        def sb(name, shape, dt=F32):
            return stack.enter_context(nc.sbuf_tensor(name, shape, dt))

        def sem(name):
            return stack.enter_context(nc.semaphore(name))

        wq, wk, wv, wo = (sb(f"w{c}_sb", [P, KC, D]) for c in "qkvo")
        wr = sb("wr_sb", [P, KC, E])
        bqk = sb("bqk", [P, 2, 2])
        bv_all, bo_all = sb("bv_all", [P, D]), sb("bo_all", [P, D])
        br_all = sb("br_all", [P, E])
        xin = [sb(f"xin{i}", [P, GT, D]) for i in range(2)]
        cin = [sb(f"cin{i}", [P, GT, D]) for i in range(2)]
        xn = sb("xn", [P, GT, D])
        xT, cT = sb("xT", [P, KC, GT * P]), sb("cT", [P, KC, GT * P])
        xb = [sb(f"xb{i}", [P, GT, D]) for i in range(2)]
        queries, keys = (sb(name, [P, 3, 2, GT * P], BF16) for name in ("queries", "keys"))
        q_rest, k_rest = (sb(name, [P, 2, GT * P]) for name in ("q_rest", "k_rest"))
        va = [sb(f"va{i}", [P, GT, HEADS, VA]) for i in range(2)]
        rowmax = [sb(f"rowmax{i}", [P, 4], F32R) for i in range(2)]
        probs = [sb(f"probs{i}", [P, 4, P]) for i in range(4)]
        rden = sb("rden", [P, HEADS])
        ao = [sb(f"ao{i}", [P, HEADS, DK]) for i in range(2)]
        aoT = [sb(f"aoT{i}", [P, KC, P]) for i in range(2)]
        x2 = [sb(f"x2_{i}", [P, GT, D]) for i in range(2)]
        pay = [sb(f"pay{i}", [P, GT, ROW]) for i in range(2)]
        x2T = sb("x2T", [P, KC, GT * P])
        bn, bn1 = sb("bn", [P, GT, 6]), sb("bn1", [P, GT, 6])
        mv1, mv2 = sb("mv1", [P, GT, 2]), sb("mv2", [P, GT, 2])
        rs1, rs2 = sb("rs1", [P, GT]), sb("rs2", [P, GT])
        partsum = sb("partsum", [P, 1])
        ebits = sb("ebits", [P, 1], I32)
        wsum, wnow = sb("wsum", [P, 2]), sb("wnow", [P, 2])
        ints = sb("ints", [P, 3, 8], I32)
        lg, mx, lgs = sb("lg", [P, GT, E]), sb("mx", [P, GT, 8]), sb("lgs", [P, GT, E])
        msk, msk16 = sb("msk", [P, GT, E]), sb("msk16", [P, GT, E], BF16)
        ex, em, esum, erec = sb("ex", [P, GT, E]), sb("em", [P, GT, E]), sb("esum", [P, GT]), sb("erec", [P, GT])
        cnt, cm, inv = sb("cnt", [P, GT, E]), sb("cm", [P, GT, E]), sb("inv", [P, GT, E])
        pos, slotf = sb("pos", [P, GT, E]), sb("slotf", [P, GT, E])
        sel, selpos = sb("sel", [P, GT, 8, E]), sb("selpos", [P, GT, 8, E])
        slots = sb("slots", [P, GT, 8], I32)

        BT = bank[0]
        PJA, PJB = bank[1], bank[2]
        SB = [bank[3], bank[4]]
        TB = [bank[5], bank[6]]
        OB = bank[7]

        consts, const_steps = sem("consts"), sem("const_steps")
        params = sem("params")
        tanh_ready, bias_ready = sem("tanh_ready"), sem("bias_ready")
        x_loaded, c_loaded, kst_ready, qst_ready, x2_stored, scattered, w_staged, w_stored = (
            [sem(f"{name}{i}") for i in range(2)] for name in (
                "x_loaded", "c_loaded", "kst_ready", "qst_ready", "x2_stored", "scattered",
                "w_staged", "w_stored"))
        var1_ready, rstd1_ready, xn_ready = sem("var1_ready"), sem("rstd1_ready"), sem("xn_ready")
        cT_psum, cT_ready = sem("cT_psum"), sem("cT_ready")
        xT_psum, xT_ready = sem("xT_psum"), sem("xT_ready")
        k_psum, keys_ready = sem("k_psum"), sem("keys_ready")
        k_first, k_left, k_second = sem("k_first"), sem("k_left"), sem("k_second")
        q_first, q_left, q_second = sem("q_first"), sem("q_left"), sem("q_second")
        q_psum, queries_ready = sem("q_psum"), sem("queries_ready")
        v_psum, va_ready = sem("v_psum"), sem("va_ready")
        s_psum, max_ready = sem("s_psum"), sem("max_ready")
        st_psum, exp_ready, probs_ready = sem("st_psum"), sem("exp_ready"), sem("probs_ready")
        pv_psum, ao_ready = sem("pv_psum"), sem("ao_ready")
        aoT_psum, aoT_ready = sem("aoT_psum"), sem("aoT_ready")
        o_psum, x2_ready = sem("o_psum"), sem("x2_ready")
        xb_ready = sem("xb_ready")
        var2_ready, rstd2_ready, xn2_ready = sem("var2_ready"), sem("rstd2_ready"), sem("xn2_ready")
        x2T_psum, x2T_ready = sem("x2T_psum"), sem("x2T_ready")
        r_psum, logits_read, shifted_ready = sem("r_psum"), sem("logits_read"), sem("shifted_ready")
        ex_ready, pos_psum, pos_read = sem("ex_ready"), sem("pos_psum"), sem("pos_read")
        slots_ready = sem("slots_ready")
        w_sums, w_total, w_scaled = sem("w_sums"), sem("w_total"), sem("w_scaled")
        w_high, w_low = sem("w_high"), sem("w_low")
        mask_ready = sem("mask_ready")
        early_weights = sem("early_weights")
        dve_consts, waits_taken = sem("dve_consts"), sem("waits_taken")
        dve_steps, pool_steps = sem("dve_steps"), sem("pool_steps")


        def bt_before(g, k):
            order = [(cT_ready, 1, lambda i: i + 1), (xT_ready, 1, lambda i: i + 1),
                     (x2T_ready, -1, lambda i: 2 * i + 1), (aoT_ready, -1, lambda i: 2 * i + 2),
                     (x2T_ready, -1, lambda i: 2 * i + 2), (aoT_ready, 0, lambda i: 2 * i + 1)]
            while True:
                k -= 1
                if k < 0:
                    g, k = g - 1, 5
                s, d, count = order[k]
                if there(g + d):
                    return s, count(g + d)
                if isinstance(g, int) and g < -2:
                    return None

        def free_bt(pe, g, k):
            w = bt_before(g, k)
            if w:
                pe.wait_ge(*w)

        def loop_over_groups(eng, it):
            for g in (-2, -1, 0, 1):
                it(g, g % 2, g // 2)
            with eng.Fori(0, (NG - 4) // 2) as u:
                it(u * 2 + 2, 0, u + 1)
                it(u * 2 + 3, 1, u + 1)
            for g in range(NG - 2, NG + 2):
                it(g, g % 2, g // 2)

        def arrived(eng, sems, g, par, dmas=1, ok=True):
            if ok:
                eng.wait_ge(sems[par], (g - par) * (8 * dmas) + 16 * dmas)

        def settled(eng):
            eng.sem_inc(waits_taken, 1)

        def when(eng, ok, s, value):
            if ok:
                eng.wait_ge(s, value)

        with nc.Block() as block:

            @block.sync
            def _(sp):
                def load(dst, src):
                    sp.dma_start(dst, src).then_inc(params, 16)

                def group_rows(a, g):
                    return a[bass.ds(g * (GT * P), GT * P), :].rearrange("(b p) d -> p b d", p=P)

                def it(g, par, half):
                    if there(g + 2):
                        when(sp, there(g), xn_ready, g + 1)
                        settled(sp)
                        when(sp, there(g), xb_ready, g + 1)
                        settled(sp)
                        when(sp, there(g), cT_psum, g + 1)
                        settled(sp)
                        sp.dma_start(xin[par][:, :, :], group_rows(x, g + 2)).then_inc(x_loaded[par], 16)
                        sp.dma_start(cin[par][:, :, :], group_rows(ctx_in, g + 2)).then_inc(c_loaded[par], 16)
                    if isinstance(g, int) and g == -2:
                        load(wk[:, :, :], w_k.rearrange("(k p) n -> p k n", p=P))
                        load(bqk[:, 0, :], b_q)
                        load(bqk[:, 1, :], b_k)
                        load(wq[:, :, :], w_q.rearrange("(k p) n -> p k n", p=P))
                        load(wv[:, :, :], w_v.rearrange("(k p) n -> p k n", p=P))
                        load(bv_all[:, :], b_v.partition_broadcast(P))
                        load(wo[:, :, :], w_o.rearrange("(k p) n -> p k n", p=P))
                        load(bo_all[:, :], b_o.partition_broadcast(P))
                        load(wr[:, :, :], Wr.rearrange("(k p) n -> p k n", p=P))
                        load(br_all[:, :], br.partition_broadcast(P))
                        load(gates_in[:, 0:1], g_xattn.partition_broadcast(P))
                        load(gates_in[:, 1:2], g_ffn.partition_broadcast(P))
                        load(b1t[:, :, :], b1)
                        sp.wait_ge(consts, 2)
                        load(out[T:T + P, :], padrow[:, 0:D])
                        for half in range(2):
                            at = E * REG + half * P
                            load(xs_dram[at:at + P, :], padrow[:, :])
                    if there(g):
                        when(sp, there(g - 2), w_low, (g - 1) * 4)
                        settled(sp)
                        e = half
                        if par == 0:
                            src = W1[bass.ds(e, 1), :, :].rearrange("a (k p) n -> p (a k) n", p=P)
                            dst = stage[0].rearrange("p (k n) -> p k n", k=KC)
                        else:
                            src = W2[bass.ds(e, 1), :, :].rearrange("a (k p) n -> p (a k) n", p=P)
                            dst = stage[1].rearrange("p (k n) -> p k n", k=HC)
                        sp.dma_start(dst, src).then_inc(w_staged[par], 16)
                    if there(g + 1):
                        for w, src, st, src_ready, dst_ready in ((1, keys, kst, keys_ready, kst_ready),
                                                                 (0, queries, qst, queries_ready, qst_ready)):
                            sp.wait_ge(src_ready, g + 2)
                            settled(sp)
                            when(sp, there(g - 1), st_psum, g * QUADS)
                            settled(sp)
                            for at, parts in enumerate(PRODUCTS):
                                sp.dma_start(st[1 - par][DK * at:DK * at + DK, :, :],
                                             src[:, parts[1 if w else 0], :, :]).then_inc(dst_ready[1 - par], 16)
                    if there(g - 1):
                        sp.wait_ge(x2_ready, g * GT)
                        settled(sp)
                        sp.dma_start(group_rows(out, g - 1), x2[1 - par][:, :, :]).then_inc(x2_stored[1 - par], 16)
                        sp.wait_ge(w_low, g * 4)
                        settled(sp)
                        e = half - (1 - par)
                        rows = w_dram[bass.ds(e, 1), 1 - par, :, :].rearrange("a p n -> p (a n)")
                        sp.dma_start(rows, split[1 - par].rearrange("p a n -> p (a n)")).then_inc(w_stored[1 - par], 16)
                    if isinstance(g, int) and g == NG - 2:
                        for i in range(2):
                            arrived(sp, w_stored, 2 * (EARLY - 1) + i, i)
                            settled(sp)
                        for e in range(EARLY):
                            sp.dma_start(wts[:, e, :].rearrange("p (a n) -> p a n", a=2),
                                         w_dram[e].rearrange("a p n -> p a n")).then_inc(early_weights, 16)

                loop_over_groups(sp, it)
                for i in range(2):
                    arrived(sp, x2_stored, NG - 2 + i, i)
                    settled(sp)
                    arrived(sp, w_stored, NG - 2 + i, i)
                    settled(sp)
                sp.wait_ge(params, 16 * 16)
                sp.wait_ge(early_weights, 16 * EARLY)

            @block.gpsimd
            def _(pool):
                step = Links(pool, pool_steps)
                step.later(pool.memset(ident[:, :], 0.0))
                step.later(pool.memset(mask4[:, :, :], 0.0))
                step.later(pool.memset(earlier[:, :], 1.0))
                step.later(pool.memset(padrow[:, :], 0.0))
                for i in range(2):
                    step.later(pool.memset(pay[i][:, :, D + E:], 0.0))
                step(pool.memset(power[:, :], -0.5))
                pool.iota(padrow[:, D + E:D + E + 1].bitcast(I32), pattern=[[0, 1]], base=T,
                          channel_multiplier=1).then_inc(consts, 1)
                pool.affine_select(out=ident[:, :], in_=ident[:, :], compare_op=ALU.not_equal,
                                   fill=1.0, base=0, pattern=[[-1, P]], channel_multiplier=1).then_inc(consts, 1)
                pool.affine_select(out=mask4[:, :, :], in_=mask4[:, :, :], compare_op=ALU.is_ge,
                                   fill=MASKED, base=0, pattern=[[0, 4], [-1, P]],
                                   channel_multiplier=1).then_inc(consts, 1)
                pool.affine_select(out=earlier[:, :], in_=earlier[:, :], compare_op=ALU.is_gt,
                                   fill=0.0, base=0, pattern=[[1, P]], channel_multiplier=-1).then_inc(consts, 1)
                pool.iota(ints[:, 0, :], pattern=[[1, 8]], base=0, channel_multiplier=0).then_inc(consts, 1)
                pool.iota(ints[:, 1, :], pattern=[[1, 8]], base=1, channel_multiplier=0).then_inc(consts, 1)
                pool.iota(ints[:, 2, :], pattern=[[REG, 8]], base=0, channel_multiplier=0).then_inc(consts, 1)
                for i in range(2):
                    pool.iota(pay[i][:, :, D + E:D + E + 1].bitcast(I32), pattern=[[P, GT], [0, 1]],
                              base=(i - 2) * GT * P, channel_multiplier=1).then_inc(consts, 1)

                def it(g, par, half):
                    for n in range(QUADS):
                        q, pg = (QUADS - 1, g - 1) if n == 0 else (n - 1, g)
                        if there(pg):
                            pool.wait_ge(exp_ready, pg * QUADS + q + 1)
                            settled(pool)
                            pool.affine_select(out=probs[q % 4][:, :, :], in_=probs[q % 4][:, :, :],
                                               compare_op=ALU.is_ge, fill=0.0, base=0,
                                               pattern=[[0, 4], [1, P]],
                                               channel_multiplier=-1).then_inc(probs_ready, 1)
                        if n in (1, 5) and there(g - 1):
                            b = n // 4
                            pool.wait_ge(var2_ready, (g - 1) * GT + b + 1)
                            pool.tensor_tensor(rs2[:, b:b + 1], mv2[:, b, 1:2], power[:, 0:1],
                                               ALU.pow).then_inc(rstd2_ready, 1)
                        if n == 5 and there(g + 1):
                            arrived(pool, x_loaded, g + 1, 1 - par)
                            when(pool, there(g - 1), x2_ready, g * GT)
                            pool.wait_ge(bias_ready, 1)
                            pool.tensor_tensor(xb[1 - par][:, :, :], xin[1 - par][:, :, :],
                                               bo_all[:, :].unsqueeze(1).to_broadcast([P, GT, D]),
                                               ALU.add).then_inc(xb_ready, 1)
                        if n == 5 and there(g):
                            pool.wait_ge(w_sums, g + 1)
                            when(pool, there(g - 1), w_scaled, g)
                            settled(pool)
                            pool.partition_all_reduce(wsum[:, par:par + 1], partsum[:, :], P,
                                                      ADD_ALL).then_inc(w_total, 1)
                        if n >= 4 and there(g - 2):
                            b, r = (n - 4) // 2, n % 2
                            if n == 4:
                                pool.wait_ge(slots_ready, g - 1)
                                settled(pool)
                            pool.indirect_dma_start(
                                out=xs_dram[:, :],
                                out_offset=bass.IndirectOffsetOnAxis(ap=slots[:, b, r:r + 1], axis=0),
                                in_=pay[par][:, b, :], in_offset=None,
                                bounds_check=E * REG - 1, oob_is_err=False).then_inc(scattered[par], 16)
                        if n == 7 and there(g + 2):
                            pool.wait_ge(var1_ready, g + 3)
                            when(pool, there(g + 1), xn_ready, g + 2)
                            pool.tensor_tensor(rs1[:, :], mv1[:, :, 1], power[:, 0:GT],
                                               ALU.pow).then_inc(rstd1_ready, 1)

                loop_over_groups(pool, it)
                for i in range(2):
                    arrived(pool, scattered, NG - 2 + i, i, 4)

            @block.scalar
            def _(act):
                act.wait_ge(params, 16 * 16)
                act.activation(tgx[:, :], gates_in[:, 0:1], ACT.Tanh).then_inc(tanh_ready, 1)
                act.activation(tgf[:, :], gates_in[:, 1:2], ACT.Tanh).then_inc(tanh_ready, 1)

                def it(g, par, half):
                    g1, p1 = g + 1, 1 - par
                    for n in range(QUADS):
                        q, pg = (QUADS - 1, g - 1) if n == 0 else (n - 1, g)
                        if there(pg):
                            act.wait_ge(st_psum, pg * QUADS + q + 1)
                            before = there(pg - 1) if q < 4 else True
                            when(act, before, pv_psum, pg * QUADS + q - 3)
                            act.activation(probs[q % 4][:, :, :].rearrange("p a q -> p (a q)"), TB[q % 2][:, :],
                                           ACT.Exp, scale=float(DK) ** -0.5).then_inc(exp_ready, 1)
                        if n == 0 and there(g1):
                            act.wait_ge(cT_psum, g1 + 1)
                            when(act, there(g), v_psum, g + 1)
                            act.activation(cT[:, :, :].rearrange("p k t -> p (k t)"), BT[:, :],
                                           ACT.Copy).then_inc(cT_ready, 1)
                        if n == 0 and there(g - 2):
                            act.wait_ge(shifted_ready, g - 1)
                            when(act, there(g - 3), slots_ready, g - 2)
                            act.activation(ex[:, :, :], lgs[:, :, :], ACT.Exp).then_inc(ex_ready, 1)
                        if n in (1, 3) and there(g1):
                            w, dst, ps, psum, done, restacked = (
                                (1, keys, k_psum, PJB, k_first, kst_ready) if n == 1 else
                                (0, queries, q_psum, PJA, q_first, qst_ready))
                            act.wait_ge(ps, g1 + 1)
                            arrived(act, restacked, g, par, 6, there(g))
                            for odd in range(2):
                                last = act.activation(dst[:, 0, odd, :], psum[:, 256 * odd:256 * odd + 256],
                                                      ACT.Identity, bias=bqk[:, w, odd:odd + 1])
                            last.then_inc(done, 1)
                        if n in (2, 4) and there(g1):
                            dst, rest, left, done = ((keys, k_rest, k_left, k_second) if n == 2 else
                                                     (queries, q_rest, q_left, q_second))
                            act.wait_ge(left, g1 + 1)
                            act.activation(dst[:, 1, :, :], rest[:, :, :], ACT.Copy).then_inc(done, 1)
                        if n == 1 and there(g1):
                            act.wait_ge(xT_psum, g1 + 1)
                            when(act, there(g), q_psum, g + 1)
                            act.activation(xT[:, :, :].rearrange("p k t -> p (k t)"), BT[:, :],
                                           ACT.Copy).then_inc(xT_ready, 1)
                        if n in (2, 6) and there(g - 1):
                            b = n // 4
                            act.wait_ge(x2T_psum, (g - 1) * GT + b + 1)
                            when(act, there(g - 2), r_psum, g - 1)
                            act.activation(x2T[:, :, b * P:(b + 1) * P],
                                           BT[:, 0:D].rearrange("p (k t) -> p k t", k=KC),
                                           ACT.Copy).then_inc(x2T_ready, 1)
                        if (n == 3 and there(g - 1)) or (n == 7 and there(g)):
                            b, tg = (1, g - 1) if n == 3 else (0, g)
                            act.wait_ge(aoT_psum, tg * GT + b + 1)
                            when(act, there(tg - 1), o_psum, (tg - 1) * GT + b + 1)
                            act.activation(aoT[b][:, :, :].rearrange("p k t -> p (k t)"), BT[:, 0:D],
                                           ACT.Copy).then_inc(aoT_ready, 1)
                        if n == 4 and there(g):
                            arrived(act, w_staged, g, par)
                            when(act, there(g - 1), w_total, g)
                            arrived(act, w_stored, g - 2, par, 1, there(g - 2))
                            act.activation(split[par][:, 1, :].bitcast(BF16), stage[par][:, :], ACT.Square,
                                           accum_out=partsum[:, :]).then_inc(w_sums, 1)
                        if n == 7 and there(g):
                            act.wait_ge(w_scaled, g + 1)
                            act.activation(split[par][:, 0, :], stage[par][:, :], ACT.Copy,
                                           scale=wnow[:, par:par + 1]).then_inc(w_high, 1)

                loop_over_groups(act, it)

            @block.vector
            def _(dve):
                step = Links(dve, dve_steps)
                for i in range(2):
                    step.later(dve.memset(va[i][:, :, :, DK:DK + 1], 1.0))
                step.later(dve.memset(mostsel[:, :], 0.0))
                step.later(dve.memset(ones8[:, :], 1.0))
                step.later(dve.memset(ones16[:, :], 1.0))
                dve.wait_ge(consts, 9)
                step.later(dve.tensor_copy(rank0[:, :], ints[:, 0, :]))
                step.later(dve.tensor_copy(rank1[:, :], ints[:, 1, :]))
                step.later(dve.tensor_copy(region0[:, :], ints[:, 2, :]))
                step.later(dve.tensor_copy(base[:, :], ints[:, 2, :]))
                step.later(dve.tensor_scalar(negident[:, :], ident[:, :], -1.0, None, ALU.mult))
                dve.tensor_copy(ident16[:, :], ident[:, :]).then_inc(dve_consts, 1)
                step.wait()
                dve.wait_ge(tanh_ready, 2)
                dve.tensor_scalar(bo_all[:, :], bo_all[:, :], tgx[:, 0:1], None, ALU.mult).then_inc(bias_ready, 1)

                def variance(src, bn_, mv, done):
                    step(dve.bn_stats(bn_, src))
                    step(dve.bn_aggr(mv, bn_))
                    dve.tensor_scalar_add(mv[:, 1:2], mv[:, 1:2], EPS).then_inc(done, 1)

                def rest(g1, n):
                    w, dst, left, psum, first, done = ((1, keys, k_rest, PJB, k_first, k_left) if n == 1 else
                                                       (0, queries, q_rest, PJA, q_first, q_left))
                    dve.wait_ge(first, g1 + 1)
                    when(dve, there(g1 - 1), queries_ready if w == 0 else keys_ready, g1)
                    for odd in range(2):
                        last = dve.scalar_tensor_tensor(
                            out=left[:, odd, :], in0=psum[:, 256 * odd:256 * odd + 256],
                            scalar=bqk[:, w, odd:odd + 1], in1=dst[:, 0, odd, :], op0=ALU.add, op1=ALU.subtract)
                    last.then_inc(done, 1)

                def third(g1, p1, n):
                    dst, left, second, done, restacked = (
                        (keys, k_rest, k_second, keys_ready, kst_ready) if n == 2 else
                        (queries, q_rest, q_second, queries_ready, qst_ready))
                    dve.wait_ge(second, g1 + 1)
                    arrived(dve, restacked, g1 - 1, 1 - p1, 6, there(g1 - 1))
                    dve.tensor_tensor(dst[:, 2, :, :], left[:, :, :], dst[:, 1, :, :], ALU.subtract).then_inc(done, 1)

                def normalise(g, b):
                    t = g * GT + b
                    dve.wait_ge(pv_psum, (t + 1) * 4)
                    when(dve, there(g - 1), aoT_psum, t - 1)
                    o = OB[:, 0:HEADS * VA].rearrange("p (h v) -> p h v", h=HEADS)
                    step(dve.reciprocal(rden[:, :], o[:, :, DK]))
                    dve.tensor_tensor(ao[b][:, :, :], o[:, :, 0:DK],
                                      rden[:, :].unsqueeze(2).to_broadcast([P, HEADS, DK]),
                                      ALU.mult).then_inc(ao_ready, 1)

                def residual(g, b, psum, i):
                    t = g * GT + b
                    dve.wait_ge(o_psum, t + 1)
                    dve.wait_ge(xb_ready, g + 1)
                    arrived(dve, x2_stored, g - 2, i, 1, there(g - 2))
                    dve.scalar_tensor_tensor(out=x2[i][:, b, :], in0=psum[:, 0:D], scalar=tgx[:, 0:1],
                                             in1=xb[i][:, b, :], op0=ALU.mult, op1=ALU.add).then_inc(x2_ready, 1)
                    dve.wait_ge(x2_ready, t + 1)
                    variance(x2[i][:, b, :], bn[:, b, :], mv2[:, b, :], var2_ready)

                def norm2(g, b, i):
                    dve.wait_ge(rstd2_ready, g * GT + b + 1)
                    arrived(dve, scattered, g - 2, i, 4, there(g - 2))
                    dve.tensor_scalar(pay[i][:, b, 0:D], x2[i][:, b, :], mv2[:, b, 0:1], rs2[:, b:b + 1],
                                      ALU.subtract, ALU.mult).then_inc(xn2_ready, 1)

                def over_ranks(a):
                    return a.unsqueeze(2).to_broadcast([P, GT, 8, E])

                def it(g, par, half):
                    settled(dve)
                    step.restart()
                    g1, p1 = g + 1, 1 - par
                    for n in range(QUADS):
                        if there(g):
                            dve.wait_ge(s_psum, g * QUADS + n + 1)
                            when(dve, n >= 2 or there(g - 1), st_psum, g * QUADS + n - 1)
                            dve.tensor_reduce(rowmax[n % 2][:, :], SB[n % 2][:, :].rearrange("p (a k) -> p a k", a=4),
                                              AX, ALU.max).then_inc(max_ready, 1)
                        if n % 2 == 0 and there(g - 1):
                            c = slice(256 * n, 256 * n + 512)
                            if n == 0:
                                dve.wait_ge(w_high, g)
                            dve.scalar_tensor_tensor(out=split[p1][:, 1, c], in0=stage[p1][:, c],
                                                     scalar=wnow[:, p1:p1 + 1], in1=split[p1][:, 0, c],
                                                     op0=ALU.mult, op1=ALU.subtract).then_inc(w_low, 1)
                        if n == 0 and there(g1):
                            dve.wait_ge(rstd1_ready, g1 + 1)
                            when(dve, there(g), xT_psum, g + 1)
                            for b in range(GT):
                                last = dve.tensor_scalar(xn[:, b, :], xin[p1][:, b, :], mv1[:, b, 0:1],
                                                         rs1[:, b:b + 1], ALU.subtract, ALU.mult)
                            last.then_inc(xn_ready, 1)
                        if n == 0 and there(g - 1):
                            residual(g - 1, 0, PJA, p1)
                        if n in (1, 4) and there(g1):
                            rest(g1, n)
                        if n == 1 and there(g - 1):
                            norm2(g - 1, 0, p1)
                        if n == 1 and there(g - 2):
                            dve.wait_ge(ex_ready, g - 1)
                            step(dve.tensor_tensor(em[:, :, :], ex[:, :, :], msk[:, :, :], ALU.mult))
                            for b in range(GT):
                                step.later(dve.tensor_tensor_scan(cnt[:, b, :], ones8[:, :], msk[:, b, :], 0.0,
                                                                  ALU.mult, ALU.add))
                            step(dve.tensor_reduce(esum[:, :], em[:, :, :], AX, ALU.add))
                            step.later(dve.reciprocal(erec[:, :], esum[:, :]))
                            step.later(dve.tensor_tensor(cm[:, :, :], cnt[:, :, :], msk[:, :, :], ALU.mult))
                            step(dve.tensor_tensor(mostsel[:, :], mostsel[:, :], cnt[:, :, E - 1], ALU.max))
                            step.later(dve.scalar_tensor_tensor(
                                out=pay[par][:, :, D:D + E], in0=em[:, :, :], scalar=tgf[:, 0:1],
                                in1=erec[:, :].unsqueeze(2).to_broadcast([P, GT, E]), op0=ALU.mult, op1=ALU.mult))
                            if True:
                                numbers = pay[par][:, :, D + E:D + E + 1].bitcast(I32)
                                step.later(dve.tensor_scalar(numbers, numbers, float(2 * GT * P), None, ALU.add))
                            step.later(dve.tensor_tensor(inv[:, :, :], rank0[:, :].unsqueeze(1).to_broadcast([P, GT, 8]),
                                                         cnt[:, :, E - 1:E].to_broadcast([P, GT, 8]), ALU.is_ge))
                            step(dve.tensor_tensor(sel[:, :, :, :], over_ranks(cm[:, :, :]),
                                                   rank1[:, :].unsqueeze(1).unsqueeze(3).to_broadcast([P, GT, 8, E]),
                                                   ALU.is_equal))
                        if n == 2 and there(g - 2):
                            dve.wait_ge(pos_psum, g - 1)
                            step(dve.tensor_tensor(pos[:, :, :], PJA[:, 0:GT * E].rearrange("p (b e) -> p b e", b=GT),
                                                   base[:, :].unsqueeze(1).to_broadcast([P, GT, E]), ALU.add))
                            dve.tensor_tensor(base[:, :], base[:, :], PJA[:, GT * E:GT * E + E],
                                              ALU.add).then_inc(pos_read, 1)
                            step(dve.tensor_tensor(selpos[:, :, :, :], sel[:, :, :, :], over_ranks(pos[:, :, :]), ALU.mult))
                            step(dve.tensor_reduce(slotf[:, :, :], selpos[:, :, :, :], AX, ALU.add))
                            arrived(dve, scattered, g - 3, p1, 4, there(g - 3))
                            dve.scalar_tensor_tensor(out=slots[:, :, :], in0=inv[:, :, :], scalar=OFF_BIG,
                                                     in1=slotf[:, :, :], op0=ALU.mult,
                                                     op1=ALU.add).then_inc(slots_ready, 1)
                            dve.wait_ge(slots_ready, g - 1)
                            step.later(dve.tensor_copy(all_slots[:, bass.ds((g - 2) * GT, GT), :], slots[:, :, :]))
                        if n in (2, 5) and there(g1):
                            third(g1, p1, n)
                        if n == 3 and there(g1):
                            dve.wait_ge(v_psum, g1 + 1)
                            when(dve, there(g - 1), pv_psum, g * QUADS)
                            dve.tensor_tensor(va[p1][:, :, :, 0:DK],
                                              PJB[:, :].rearrange("p (b h v) -> p b h v", b=GT, h=HEADS),
                                              bv_all[:, :].rearrange("p (h v) -> p h v", h=HEADS).unsqueeze(1)
                                              .to_broadcast([P, GT, HEADS, DK]), ALU.add).then_inc(va_ready, 1)
                        if n == 3 and there(g - 1):
                            normalise(g - 1, 1)
                        if n == 4 and there(g - 1):
                            residual(g - 1, 1, PJB, p1)
                        if n == 5 and there(g - 1):
                            norm2(g - 1, 1, p1)
                        if n == 6 and there(g + 2):
                            arrived(dve, x_loaded, g + 2, par)
                            for b in range(GT):
                                step.later(dve.bn_stats(bn1[:, b, :], xin[par][:, b, :]))
                            when(dve, there(g1), xn_ready, g1 + 1)
                            step.wait()
                            settled(dve)
                            for b in range(GT):
                                step.later(dve.bn_aggr(mv1[:, b, :], bn1[:, b, :]))
                            step.wait()
                            dve.tensor_scalar_add(mv1[:, :, 1:2], mv1[:, :, 1:2], EPS).then_inc(var1_ready, 1)
                        if n == 6 and there(g):
                            dve.wait_ge(w_total, g + 1)
                            step(dve.tensor_scalar(ebits[:, :], wsum[:, par:par + 1].bitcast(I32), 24, None,
                                                   ALU.logical_shift_right))
                            dve.tensor_scalar(wnow[:, par:par + 1].bitcast(I32), ebits[:, :], -float(1 << 23),
                                              204.0 * (1 << 23), ALU.mult, ALU.add).then_inc(w_scaled, 1)
                            dve.wait_ge(w_scaled, g + 1)
                            e = half
                            dve.tensor_copy(wscale[:, par, bass.ds(e, 1)], wnow[:, par:par + 1])
                            step(dve.tensor_copy(wsquares[:, par, bass.ds(e, 1)], wsum[:, par:par + 1]))
                        if n == 7 and there(g):
                            normalise(g, 0)
                        if n == 7 and there(g - 1):
                            dve.wait_ge(r_psum, g)
                            dve.tensor_tensor(lg[:, :, :], PJA[:, 0:GT * E].rearrange("p (b e) -> p b e", b=GT),
                                              br_all[:, :].unsqueeze(1).to_broadcast([P, GT, E]),
                                              ALU.add).then_inc(logits_read, 1)
                            dve.wait_ge(logits_read, g)
                            settled(dve)
                            for b in range(GT):
                                last = dve.max(mx[:, b, :], lg[:, b, :])
                            step(last)
                            step.later(dve.tensor_tensor(msk[:, :, :], lg[:, :, :],
                                                         mx[:, :, 1:2].to_broadcast([P, GT, E]), ALU.is_ge))
                            dve.tensor_tensor(msk16[:, :, :], lg[:, :, :],
                                              mx[:, :, 1:2].to_broadcast([P, GT, E]), ALU.is_ge).then_inc(mask_ready, 1)
                            dve.tensor_tensor(lgs[:, :, :], lg[:, :, :], mx[:, :, 0:1].to_broadcast([P, GT, E]),
                                              ALU.subtract).then_inc(shifted_ready, 1)
                            dve.wait_ge(shifted_ready, g)

                loop_over_groups(dve, it)

            @block.tensor
            def _(pe):
                pe.wait_ge(dve_consts, 1)
                pe.wait_ge(params, 16 * 16)

                def transposes(parts, done):
                    for i, (src, n) in enumerate(parts):
                        last = pe.transpose(BT[:, i * P:(i + 1) * P], src, ident[:, :])
                    last.then_inc(done, 1)

                def product(psum, lhsT, rhs):
                    for k in range(KC):
                        last = pe.matmul(psum, lhsT(k), rhs(k), start=k == 0, stop=k == KC - 1)
                    return last

                def it(g, par, half):
                    g1, p1 = g + 1, 1 - par
                    for n in range(QUADS):
                        idx = g * QUADS + n
                        odd, pairs = n % 2, range(4 * ((n % 4) // 2), 4 * ((n % 4) // 2) + 4)
                        if there(g):
                            if n == 0:
                                arrived(pe, kst_ready, g, par, 6)
                                arrived(pe, qst_ready, g, par, 6)
                            when(pe, n >= 2 or there(g - 1), max_ready, idx - 1)
                            ps = SB[n % 2]
                            tok = slice((n // 4) * P, (n // 4) * P + P)
                            pe.matmul(ps[:, :], ident16[:, :], mask4[:, :, :].rearrange("p a k -> p (a k)"),
                                      start=True, stop=False)
                            for i, j in enumerate(pairs):
                                last = pe.matmul(ps[:, i * P:(i + 1) * P], qst[par][:, 2 * j + odd, tok],
                                                 kst[par][:, 2 * j + odd, tok], start=False, stop=i == 3)
                            last.then_inc(s_psum, 1)
                        if n == 0 and there(g - 1):
                            pe.wait_ge(aoT_ready, (g - 1) * GT + 1)
                            when(pe, there(g - 2), logits_read, g - 1)
                            product(PJA[:, 0:D], lambda k: aoT[0][:, k, :], lambda k: wo[:, k, :]).then_inc(o_psum, 1)
                        if n == 0 and there(g1):
                            arrived(pe, c_loaded, g1, p1)
                            free_bt(pe, g, 0)
                            transposes([(cin[p1][:, b, k * P:(k + 1) * P], 0) for k in range(KC) for b in range(GT)],
                                       cT_psum)
                        if n == 1 and there(g - 2):
                            pe.wait_ge(mask_ready, g - 1)
                            when(pe, there(g - 1), x2_ready, (g - 1) * GT + 1)
                            pe.matmul(PJA[:, 0:E], earlier[:, :], msk16[:, 0, :], start=True, stop=True)
                            pe.matmul(PJA[:, E:2 * E], earlier[:, :], msk16[:, 1, :], start=True, stop=False)
                            pe.matmul(PJA[:, E:2 * E], ones16[:, :], msk16[:, 0, :], start=False, stop=True)
                            pe.matmul(PJA[:, 2 * E:3 * E], ones16[:, :], msk16[:, 0, :], start=True, stop=False)
                            pe.matmul(PJA[:, 2 * E:3 * E], ones16[:, :], msk16[:, 1, :], start=False,
                                      stop=True).then_inc(pos_psum, 1)
                        if n == 1 and there(g1):
                            pe.wait_ge(cT_ready, g1 + 1)
                            when(pe, there(g), va_ready, g + 1)
                            when(pe, there(g - 2), x2_ready, (g - 1) * GT)
                            for o in range(2):
                                last = product(PJB[:, 256 * o:256 * o + 256], lambda k: wk[:, k, o * P:(o + 1) * P],
                                               lambda k: cT[:, k, :])
                            last.then_inc(k_psum, 1)
                            pe.wait_ge(xn_ready, g1 + 1)
                            free_bt(pe, g, 1)
                            transposes([(xn[:, b, k * P:(k + 1) * P], 0) for k in range(KC) for b in range(GT)],
                                       xT_psum)
                        if n == 2 and there(g1):
                            pe.wait_ge(k_left, g1 + 1)
                            for b in range(GT):
                                last = product(PJB[:, 256 * b:256 * b + 256], lambda k: cT[:, k, b * P:(b + 1) * P],
                                               lambda k: wv[:, k, :])
                            last.then_inc(v_psum, 1)
                        if n in (2, 6) and there(g - 1):
                            b = n // 4
                            pe.wait_ge(xn2_ready, (g - 1) * GT + b + 1)
                            free_bt(pe, g, 2 if n == 2 else 4)
                            transposes([(pay[p1][:, b, k * P:(k + 1) * P], 0) for k in range(KC)], x2T_psum)
                        if n == 3 and there(g1):
                            pe.wait_ge(xT_ready, g1 + 1)
                            when(pe, there(g - 1), x2_ready, (g - 1) * GT + 1)
                            when(pe, there(g - 2), pos_read, g - 1)
                            when(pe, there(g), q_left, g + 1)
                            for o in range(2):
                                last = product(PJA[:, 256 * o:256 * o + 256], lambda k: wq[:, k, o * P:(o + 1) * P],
                                               lambda k: xT[:, k, :])
                            last.then_inc(q_psum, 1)
                        if there(g if n >= 1 else g - 1):
                            tg, m, i = (g, n - 1, par) if n >= 1 else (g - 1, QUADS - 1, p1)
                            odd, pairs = m % 2, range(4 * ((m % 4) // 2), 4 * ((m % 4) // 2) + 4)
                            tok = slice((m // 4) * P, (m // 4) * P + P)
                            pe.wait_ge(max_ready, tg * QUADS + m + 1)
                            when(pe, m >= 2 or there(tg - 1), exp_ready, tg * QUADS + m - 1)
                            ps = TB[m % 2]
                            for a in range(4):
                                pe.matmul(ps[:, a * P:(a + 1) * P], rowmax[m % 2][:, a:a + 1].to_broadcast([P, P]),
                                          negident[:, :], start=a == 0, stop=False)
                            for a, j in enumerate(pairs):
                                last = pe.matmul(ps[:, a * P:(a + 1) * P], kst[i][:, 2 * j + odd, tok],
                                                 qst[i][:, 2 * j + odd, tok], start=False, stop=a == 3)
                            last.then_inc(st_psum, 1)
                        if there(g if n >= 3 else g - 1):
                            tg, m, i = (g, n - 3, par) if n >= 3 else (g - 1, n + 5, p1)
                            b, odd, pairs = m // 4, m % 2, range(4 * ((m % 4) // 2), 4 * ((m % 4) // 2) + 4)
                            pe.wait_ge(probs_ready, tg * QUADS + m + 1)
                            if m == 0:
                                pe.wait_ge(va_ready, tg + 1)
                            if m % 4 == 0:
                                when(pe, b == 1 or there(tg - 1), ao_ready, tg * GT + b)
                            for a, j in enumerate(pairs):
                                h = 2 * j + odd
                                last = pe.matmul(OB[:, h * VA:(h + 1) * VA], probs[m % 4][:, a, :],
                                                 va[i][:, b, h, :], start=True, stop=True)
                            last.then_inc(pv_psum, 1)
                        if (n == 3 and there(g - 1)) or (n == 7 and there(g)):
                            b, tg = (1, g - 1) if n == 3 else (0, g)
                            pe.wait_ge(ao_ready, tg * GT + b + 1)
                            free_bt(pe, g, 3 if n == 3 else 5)
                            flat = ao[b][:, :, :].rearrange("p h v -> p (h v)")
                            transposes([(flat[:, k * P:(k + 1) * P], 0) for k in range(KC)], aoT_psum)
                        if n == 4 and there(g - 1):
                            pe.wait_ge(aoT_ready, (g - 1) * GT + 2)
                            when(pe, there(g1), va_ready, g1 + 1)
                            when(pe, there(g - 2), x2_ready, (g - 1) * GT)
                            product(PJB[:, 0:D], lambda k: aoT[1][:, k, :], lambda k: wo[:, k, :]).then_inc(o_psum, 1)
                        if n == 7 and there(g - 1):
                            pe.wait_ge(x2T_ready, g * GT)
                            when(pe, there(g1), q_left, g1 + 1)
                            when(pe, there(g - 2), pos_read, g - 1)
                            pe.wait_ge(x2_ready, g * GT)
                            for b in range(GT):
                                last = product(PJA[:, b * E:(b + 1) * E], lambda k: x2T[:, k, b * P:(b + 1) * P],
                                               lambda k: wr[:, k, :])
                            last.then_inc(r_psum, 1)

                loop_over_groups(pe, it)


def experts(nc, env):
    (out, b2, xs_dram, w_dram, bank, wts, ident, region0, base, mostsel, wscale, wsquares, padrow,
     b1t, all_slots) = (env[k] for k in (
         "out", "b2", "xs_dram", "w_dram", "bank", "wts", "ident", "region0", "base", "mostsel",
         "wscale", "wsquares", "padrow", "b1t", "all_slots"))
    with ExitStack() as stack:
        def sb(name, shape, dt=F32):
            return stack.enter_context(nc.sbuf_tensor(name, shape, dt))

        def sem(name):
            return stack.enter_context(nc.semaphore(name))

        b2_all = sb("b2_all", [P, E, D])
        xs = [sb(f"xs{i}", [P, 2, ROW]) for i in range(4)]
        xh = [sb(f"xh{i}", [P, 2, KC, TILE], F16) for i in range(2)]
        hf = sb("hf", [P, HC, TILE])
        hh = [sb(f"hh{i}", [P, 2, HC, TILE], F16) for i in range(2)]
        yb = [sb(f"yb{i}", [P, 2, D]) for i in range(2)]
        yg = [sb(f"yg{i}", [P, 2, D]) for i in range(2)]
        gscale, hscale, yscale = sb("gscale", [P, E]), sb("hscale", [P, E]), sb("yscale", [P, E])
        small = sb("small", [P, 6, E])
        smallint = sb("smallint", [P, 3, E], I32)
        b1sq = sb("b1sq", [P, E, HC])
        pcol, minus_T = sb("pcol", [P, 1]), sb("minus_T", [P, 2, E])
        padidx = sb("padidx", [P, 2, E], I32)
        most = sb("most", [P, 2])
        mostint = sb("mostint", [P, 1], I32)
        tile_no_int, tile_no = sb("tile_no_int", [1, ALL_TILES], I32), sb("tile_no", [1, ALL_TILES])
        past, pastn = sb("past", [1, ALL_TILES, E]), sb("pastn", [1, ALL_TILES, E])
        te, ts = sb("te", [1, ALL_TILES]), sb("ts", [1, ALL_TILES])
        tile_expert, tile_row = sb("tile_expert", [1, ALL_TILES], I32), sb("tile_row", [1, ALL_TILES], I32)
        tie_idx = sb("tie_idx", [P, 8], I32)
        tie_row = sb("tie_row", [P, ROW])

        XT = bank[0]
        HB = bank[1:5]
        YB = [bank[5], bank[6]]

        weights_in, b2_in, pads_in, ties_in = sem("weights_in"), sem("b2_in"), sem("pads_in"), sem("ties_in")
        numbers_made, pad_rows_ready, table_ready = sem("numbers_made"), sem("pad_rows_ready"), sem("table_ready")
        b1_sums, b1_total, most_ready, most_total = sem("b1_sums"), sem("b1_total"), sem("most_ready"), sem("most_total")
        scales_ready, rows_placed = sem("scales_ready"), sem("rows_placed")
        row_in = [sem(f"row_in{i}") for i in range(4)]
        added = [sem(f"added{i}") for i in range(2)]
        xT_psum, xhi_ready, xlo_ready = sem("xT_psum"), sem("xhi_ready"), sem("xlo_ready")
        h_psum, gelu_ready, split_ready = sem("h_psum"), sem("gelu_ready"), sem("split_ready")
        y_psum, yb_ready, yg_ready = sem("y_psum"), sem("yb_ready"), sem("yg_ready")
        dve_steps, pool_steps, waits_taken = sem("dve_steps"), sem("pool_steps"), sem("waits_taken")

        def settled(eng):
            eng.sem_inc(waits_taken, 1)

        def pipeline(eng, it, lo, hi):
            def peeled(a, b):
                for i in range(a, b):
                    it(i, i % 4, lambda k, i=i: lo <= i + k < hi)

            first = -(-(lo + 1) // 4) * 4
            rounds = (hi - 3 - first) // 4
            peeled(lo - 2, first)
            with eng.Fori(0, rounds) as u:
                for m in range(4):
                    it(u * 4 + (first + m), m, lambda k: True)
            peeled(first + 4 * rounds, hi)

        def all_tiles(eng, it):
            pipeline(eng, it, 0, MAIN_TILES)
            ties = eng.value_load(mostint[0:1, 0:1], min_val=0, max_val=E)
            with eng.If(ties > 2):
                pipeline(eng, it, MAIN_TILES, ALL_TILES)

        def when(eng, ok, s, value):
            if ok:
                eng.wait_ge(s, value)

        def before(i, n):
            return i >= n if isinstance(i, int) else True

        def expert_of(eng, i):
            return eng.value_load(tile_expert[0:1, bass.ds(i, 1)], min_val=0, max_val=E - 1)

        def added_value(i):
            return i * 16 + 16

        with nc.Block() as block:

            @block.sync
            def _(sp):
                for e in range(EARLY, E):
                    sp.dma_start(wts[:, e, :].rearrange("p (a n) -> p a n", a=2),
                                 w_dram[e].rearrange("a p n -> p a n")).then_inc(weights_in, 16)
                sp.dma_start(b2_all[:, :, :].rearrange("p e d -> p (e d)"), b2.partition_broadcast(P)).then_inc(b2_in, 16)
                sp.wait_ge(rows_placed, 1)
                sp.wait_ge(table_ready, 1)

                def it(i, m, there):
                    if there(2):
                        j = i + 2
                        when(sp, before(j, 4), added[1], added_value(i - 2))
                        settled(sp)
                        row = sp.value_load(tile_row[0:1, bass.ds(j, 1)], min_val=0, max_val=E * REG)
                        sp.dma_start(xs[(m + 2) % 4][:, :, :],
                                     xs_dram[bass.ds(row, TILE), :].rearrange("(h p) r -> p h r", h=2)
                                     ).then_inc(row_in[(m + 2) % 4], 16)

                all_tiles(sp, it)
                sp.wait_ge(weights_in, 16 * (E - EARLY))
                sp.wait_ge(b2_in, 16)

            @block.gpsimd
            def _(pool):
                step = Links(pool, pool_steps)
                pool.iota(tile_no_int[:, :], pattern=[[1, ALL_TILES]], base=0, channel_multiplier=0).then_inc(numbers_made, 1)
                pool.wait_ge(most_ready, 1)
                pool.partition_all_reduce(most[:, 1:2], most[:, 0:1], P, MAX_ALL).then_inc(most_total, 1)
                pool.wait_ge(b1_sums, 1)
                pool.partition_all_reduce(small[:, 1, :], small[:, 0, :], P, ADD_ALL).then_inc(b1_total, 1)
                pool.wait_ge(pad_rows_ready, 2)
                for e in range(E):
                    for half in range(2):
                        pool.indirect_dma_start(
                            out=xs_dram[:, :],
                            out_offset=bass.IndirectOffsetOnAxis(ap=padidx[:, half, e:e + 1], axis=0),
                            in_=padrow[:, :], in_offset=None).then_inc(pads_in, 16)
                pool.wait_ge(pads_in, 16 * 2 * E)
                pool.wait_ge(table_ready, 1)
                ties = pool.value_load(mostint[0:1, 0:1], min_val=0, max_val=E)
                with pool.If(ties > 2):
                    with pool.Fori(0, B) as t:
                        step(pool.tensor_copy(tie_idx[:, :], all_slots[:, bass.ds(t, 1), :].rearrange("p a r -> p (a r)")))
                        pool.indirect_dma_start(out=tie_row[:, :], out_offset=None, in_=xs_dram[:, :],
                                                in_offset=bass.IndirectOffsetOnAxis(ap=tie_idx[:, 0:1], axis=0)
                                                ).then_inc(ties_in, 16)
                        pool.wait_ge(ties_in, t * (16 * 7) + 16)
                        settled(pool)
                        for r in range(2, 8):
                            pool.indirect_dma_start(out=xs_dram[:, :],
                                                    out_offset=bass.IndirectOffsetOnAxis(ap=tie_idx[:, r:r + 1], axis=0),
                                                    in_=tie_row[:, :], in_offset=None, bounds_check=E * REG - 1,
                                                    oob_is_err=False).then_inc(ties_in, 16)
                        pool.wait_ge(ties_in, t * (16 * 7) + 16 * 7)
                        settled(pool)
                        step.restart()
                pool.sem_inc(rows_placed, 1)

                def it(i, m, there):
                    if there(0):
                        for half in range(2):
                            pool.wait_ge(yg_ready, i * 2 + half + 1)
                            when(pool, half == 1 or before(i, 1), added[1 - half],
                                 added_value(i if half == 1 else i - 1))
                            settled(pool)
                            numbers = xs[m][:, half, D + E:D + E + 1].bitcast(I32)
                            pool.indirect_dma_start(
                                out=out[:, :], out_offset=bass.IndirectOffsetOnAxis(ap=numbers, axis=0),
                                in_=yg[m % 2][:, half, :], in_offset=None, compute_op=ALU.add
                                ).then_inc(added[half], 16)

                def last(tiles):
                    for half in range(2):
                        pool.wait_ge(added[half], added_value(tiles - 1))

                pipeline(pool, it, 0, MAIN_TILES)
                last(MAIN_TILES)
                ties = pool.value_load(mostint[0:1, 0:1], min_val=0, max_val=E)
                with pool.If(ties > 2):
                    pipeline(pool, it, MAIN_TILES, ALL_TILES)
                    last(ALL_TILES)

            @block.scalar
            def _(act):
                act.wait_ge(scales_ready, 1)
                act.wait_ge(table_ready, 1)

                def it(i, m, there):
                    if there(2):
                        act.wait_ge(xT_psum, i + 3)
                        when(act, before(i + 2, 2), h_psum, (i + 1) * 4)
                        act.activation(xh[m % 2][:, 0, :, :], XT[:, :].rearrange("p (k t) -> p k t", k=KC), ACT.Copy,
                                       scale=X_SCALE).then_inc(xhi_ready, 1)
                    if there(1):
                        e = expert_of(act, i + 1)
                        for quarter in range(4):
                            act.wait_ge(h_psum, (i + 1) * 4 + quarter + 1)
                            when(act, before(i + 1, 1), split_ready, i * 4 + quarter + 1)
                            for c in (2 * quarter, 2 * quarter + 1):
                                last = act.activation(
                                    hf[:, c, :], HB[quarter][:, c % 2 * TILE:(c % 2 + 1) * TILE],
                                    ACT.Gelu, bias=b1t[:, bass.ds(e, 1), c], scale=gscale[:, bass.ds(e, 1)])
                            last.then_inc(gelu_ready, 1)
                    if there(0):
                        e = expert_of(act, i)
                        act.wait_ge(yb_ready, i + 1)
                        when(act, before(i, 2), added[1], added_value(i - 2))
                        for half in range(2):
                            act.activation(yg[m % 2][:, half, :], yb[m % 2][:, half, :], ACT.Copy,
                                           scale=xs[m][:, half, bass.ds(e + D, 1)]).then_inc(yg_ready, 1)

                all_tiles(act, it)

            @block.vector
            def _(dve):
                step = Links(dve, dve_steps)
                dve.tensor_reduce(most[:, 0:1], mostsel[:, :], AX, ALU.max).then_inc(most_ready, 1)
                step.later(dve.tensor_copy(pcol[:, :], padrow[:, D + E:D + E + 1].bitcast(I32)))
                step(dve.tensor_tensor(b1sq[:, :, :], b1t[:, :, :], b1t[:, :, :], ALU.mult))
                dve.tensor_reduce(small[:, 0, :], b1sq[:, :, :], AX, ALU.add).then_inc(b1_sums, 1)
                for half in range(2):
                    step.later(dve.memset(minus_T[:, half, :], float(half * P - T)))
                step.wait()
                for half in range(2):
                    dve.scalar_tensor_tensor(out=padidx[:, half, :], in0=base[:, :], scalar=pcol[:, 0:1],
                                             in1=minus_T[:, half, :], op0=ALU.add, op1=ALU.add
                                             ).then_inc(pad_rows_ready, 1)
                step(dve.tensor_tensor(small[:, 2, :], base[:, :], region0[:, :], ALU.subtract))
                step(dve.tensor_scalar(smallint[:, 0, :], small[:, 2, :], float(TILE - 1), None, ALU.add))
                step(dve.tensor_scalar(smallint[:, 1, :], smallint[:, 0, :], TILE.bit_length() - 1, None, ALU.logical_shift_right))
                step.later(dve.memset(small[:, 4, :], 1.0))
                step(dve.tensor_copy(small[:, 3, :], smallint[:, 1, :]))
                step.later(dve.tensor_tensor_scan(small[:, 5, :], small[:, 4, :], small[:, 3, :], 0.0, ALU.mult, ALU.add))
                dve.wait_ge(numbers_made, 1)
                step(dve.tensor_copy(tile_no[:, :], tile_no_int[:, :]))

                def by_tile(a):
                    return a.unsqueeze(1).to_broadcast([1, ALL_TILES, E])

                step(dve.tensor_tensor(past[:, :, :], tile_no[:, :].unsqueeze(2).to_broadcast([1, ALL_TILES, E]),
                                       by_tile(small[0:1, 5, :]), ALU.is_ge))
                step.later(dve.tensor_tensor(pastn[:, :, :], past[:, :, :], by_tile(small[0:1, 3, :]), ALU.mult))
                step(dve.tensor_reduce(te[:, :], past[:, :, :], AX, ALU.add))
                step.later(dve.tensor_scalar(tile_expert[:, :], te[:, :], float(E - 1), None, ALU.min))
                step(dve.tensor_reduce(ts[:, :], pastn[:, :, :], AX, ALU.add))
                step(dve.tensor_tensor(ts[:, :], tile_no[:, :], ts[:, :], ALU.subtract))
                step.later(dve.tensor_scalar(te[:, :], te[:, :], float(REG), None, ALU.mult))
                step(dve.tensor_scalar(ts[:, :], ts[:, :], float(TILE), None, ALU.mult))
                step(dve.tensor_tensor(ts[:, :], ts[:, :], te[:, :], ALU.add))
                step(dve.tensor_scalar(tile_row[:, :], ts[:, :], float(E * REG), None, ALU.min))
                dve.wait_ge(most_total, 1)
                dve.tensor_copy(mostint[:, :], most[:, 1:2]).then_inc(table_ready, 1)

                one = float(1 << 23)
                dve.tensor_scalar(gscale[:, :].bitcast(I32), wscale[:, 0, :].bitcast(I32), -1.0, 244 * one,
                                  ALU.mult, ALU.add)
                dve.wait_ge(b1_total, 1)
                step(dve.scalar_tensor_tensor(out=small[:, 0, :], in0=wsquares[:, 0, :], scalar=256.0,
                                              in1=small[:, 1, :], op0=ALU.mult, op1=ALU.add))
                step(dve.tensor_scalar(small[:, 0, :], small[:, 0, :], 2.0, None, ALU.mult))
                step(dve.tensor_scalar(smallint[:, 0, :], small[:, 0, :].bitcast(I32), 24, None, ALU.logical_shift_right))
                step(dve.tensor_scalar(hscale[:, :].bitcast(I32), smallint[:, 0, :], -one, 204 * one,
                                       ALU.mult, ALU.add))
                step.later(dve.tensor_scalar(small[:, 0, :].bitcast(I32), hscale[:, :].bitcast(I32), -1.0, 254 * one,
                                             ALU.mult, ALU.add))
                step(dve.tensor_scalar(small[:, 1, :].bitcast(I32), wscale[:, 1, :].bitcast(I32), -1.0, 254 * one,
                                       ALU.mult, ALU.add))
                dve.tensor_tensor(yscale[:, :], small[:, 0, :], small[:, 1, :], ALU.mult).then_inc(scales_ready, 1)
                dve.wait_ge(scales_ready, 1)
                dve.wait_ge(b2_in, 16)

                def it(i, m, there):
                    if there(2):
                        dve.wait_ge(xhi_ready, i + 3)
                        dve.scalar_tensor_tensor(out=xh[m % 2][:, 1, :, :].rearrange("p k t -> p (k t)"),
                                                 in0=XT[:, :], scalar=X_SCALE,
                                                 in1=xh[m % 2][:, 0, :, :].rearrange("p k t -> p (k t)"),
                                                 op0=ALU.mult, op1=ALU.subtract).then_inc(xlo_ready, 1)
                    if there(1):
                        e = expert_of(dve, i + 1)
                        b = (m + 1) % 2
                        for quarter in range(4):
                            c = slice(2 * quarter, 2 * quarter + 2)
                            dve.wait_ge(gelu_ready, (i + 1) * 4 + quarter + 1)
                            when(dve, quarter == 0 and before(i + 1, 2), y_psum, i)
                            high = hh[b][:, 0, c, :].rearrange("p c t -> p (c t)")
                            full = hf[:, c, :].rearrange("p c t -> p (c t)")
                            step(dve.tensor_scalar(high, full, hscale[:, bass.ds(e, 1)], None, ALU.mult))
                            dve.scalar_tensor_tensor(out=hh[b][:, 1, c, :].rearrange("p c t -> p (c t)"), in0=full,
                                                     scalar=hscale[:, bass.ds(e, 1)], in1=high,
                                                     op0=ALU.mult, op1=ALU.subtract).then_inc(split_ready, 1)
                    if there(0):
                        e = expert_of(dve, i)
                        dve.wait_ge(y_psum, i + 1)
                        when(dve, before(i, 2), yg_ready, (i - 1) * 2)
                        dve.scalar_tensor_tensor(out=yb[m % 2][:, :, :],
                                                 in0=YB[m % 2][:, :].rearrange("p (h d) -> p h d", h=2),
                                                 scalar=yscale[:, bass.ds(e, 1)],
                                                 in1=b2_all[:, bass.ds(e, 1), :].to_broadcast([P, 2, D]),
                                                 op0=ALU.mult, op1=ALU.add).then_inc(yb_ready, 1)
                    settled(dve)
                    step.restart()

                settled(dve)
                step.restart()
                all_tiles(dve, it)

            @block.tensor
            def _(pe):
                pe.wait_ge(weights_in, 16 * (E - EARLY))
                pe.wait_ge(table_ready, 1)

                expert = {}

                def it(i, m, there):
                    if there(0):
                        expert[0] = expert[1] if m > 0 and not isinstance(i, int) else expert_of(pe, i)
                    if there(1):
                        expert[1] = expert_of(pe, i + 1)
                    if there(2):
                        pe.wait_ge(row_in[(m + 2) % 4], row_value(i + 2, (m + 2) % 4))
                        when(pe, before(i + 2, 1), xlo_ready, i + 2)
                        for k in range(KC):
                            for half in range(2):
                                at = k * TILE + half * P
                                last = pe.transpose(XT[:, at:at + P], xs[(m + 2) % 4][:, half, k * P:(k + 1) * P],
                                                    ident[:, :])
                        last.then_inc(xT_psum, 1)
                    if there(1):
                        b = (m + 1) % 2
                        terms = [(wp, xp, k) for wp, xp in ((0, 0), (0, 1), (1, 0)) for k in range(KC)]
                        pe.wait_ge(xlo_ready, i + 2)
                        for c in range(HC):
                            when(pe, c % 2 == 0 and before(i + 1, 1), gelu_ready, i * 4 + c // 2 + 1)
                            for q, (wp, xp, k) in enumerate(terms):
                                at = wp * 2048 + k * H + c * P
                                last = pe.matmul(HB[c // 2][:, c % 2 * TILE:(c % 2 + 1) * TILE],
                                                 wts[:, bass.ds(expert[1], 1), at:at + P], xh[b][:, xp, k, :],
                                                 start=q == 0, stop=q == 5)
                            if c % 2 == 1:
                                last.then_inc(h_psum, 1)
                    if there(0):
                        b = m % 2
                        when(pe, before(i, 2), yb_ready, i - 1)
                        terms = [(hp, wp, c) for quarter in range(4) for hp, wp in ((0, 0), (1, 0), (0, 1))
                                 for c in (2 * quarter, 2 * quarter + 1)]
                        for half in range(2):
                            for q, (hp, wp, c) in enumerate(terms):
                                if half == 0 and q % 6 == 0:
                                    pe.wait_ge(split_ready, i * 4 + q // 6 + 1)
                                at = 4096 + wp * 2048 + c * D
                                last = pe.matmul(YB[b][:, half * D:(half + 1) * D],
                                                 hh[b][:, hp, c, half * P:(half + 1) * P],
                                                 wts[:, bass.ds(expert[0], 1), at:at + D], start=q == 0, stop=q == 23)
                        last.then_inc(y_psum, 1)

                def row_value(i, m):
                    return (i - m) * 4 + 16

                all_tiles(pe, it)


def kernel(**inputs):
    import numpy as np
    import concourse.bacc as bacc
    from concourse.bass_utils import run_bass_kernel_spmd as run

    a = {k: np.asarray(v) for k, v in inputs.items()}
    order = np.arange(D).reshape(PAIRS, 2, DK).transpose(1, 2, 0).reshape(D)

    def w(name):
        return a["L0_xattn_w_" + name].T

    def bias(name):
        return a["L0_xattn_b_" + name]

    arrays = {
        "x": a["x"].reshape(T, D),
        "ctx_in": a["ctx_1024"].reshape(T, D),
        "g_xattn": a["g_xattn"], "g_ffn": a["g_ffn"],
        "w_q": w("q")[:, order], "b_q": bias("q")[order].reshape(2, P).T,
        "w_k": w("k")[:, order], "b_k": bias("k")[order].reshape(2, P).T,
        "w_v": w("v"), "b_v": bias("v"), "w_o": w("o"), "b_o": bias("o"),
        "W1": a["L0_ffn_W1"], "b1": a["L0_ffn_b1"].reshape(E, HC, P).transpose(2, 0, 1),
        "W2": a["L0_ffn_W2"], "b2": a["L0_ffn_b2"].reshape(E * D),
        "Wr": a["L0_ffn_Wr"], "br": a["L0_ffn_br"],
    }
    arrays = {k: np.ascontiguousarray(v) for k, v in arrays.items()}
    nc = bacc.Bacc("TRN2", target_bir_lowering=False, num_devices=1)
    aps = [nc.dram_tensor(f"in_{k}", v.shape, mybir.dt.from_np(v.dtype), kind="ExternalInput").ap()
           for k, v in arrays.items()]
    out = nc.dram_tensor("out_rows", [T + P, D], F32, kind="ExternalOutput").ap()
    bass_flamingo(nc, *aps, out)
    r = run(nc, [{f"in_{k}": v for k, v in arrays.items()}], core_ids=[0])
    return r.results[0]["out_rows"][:T].reshape(B, S, D)
```

```python
import concourse.bass as bass
from concourse import mybir
from contextlib import ExitStack

F32 = mybir.dt.float32
F32R = mybir.dt.float32r
F16 = mybir.dt.float16
BF16 = mybir.dt.bfloat16
I32 = mybir.dt.int32
ALU = mybir.AluOpType
ACT = mybir.ActivationFunctionType
AX = mybir.AxisListType.X
ADD_ALL = bass.bass_isa.ReduceOp.add
MAX_ALL = bass.bass_isa.ReduceOp.max

P = 128
B, S, D = 32, 128, 256
T = B * S
HEADS, DK = 16, 16
KC = D // P
H = 1024
HC = H // P
E = 8
GT = 2
NG = B // GT
PAIRS = HEADS // 2
VA = DK + 1
PRODUCTS = ((0, 0), (0, 1), (1, 0), (0, 2), (2, 0), (1, 1))
STACK = len(PRODUCTS) * DK
QUADS = 4 * GT
EPS = 1e-5
MASKED = -1e30

TILE = 2 * P
REG = T + TILE
ROW = D + E + 8
MAIN_TILES = (2 * T + E * (TILE - 1)) // TILE
ALL_TILES = E * T // TILE
EARLY = 4
X_SCALE = 1024.0
OFF_BIG = 1.0e6


def padding(eng, env, experts):
    eng.wait_ge(env["pad_rows_ready"], 1)
    for e in experts:
        place = eng.value_load(env["padplace"][0:1, e:e + 1], min_val=0, max_val=E * REG)
        eng.dma_start(env["xs_dram"][bass.ds(place, TILE), :].rearrange("(h p) r -> p h r", h=2),
                      env["padrow"][:, :].unsqueeze(1).to_broadcast([P, 2, ROW])).then_inc(env["pads_in"], 16)


def load_weights(sp, wts, w_dram, e, done):
    for layer in range(2):
        sp.dma_start(wts[:, e, 4096 * layer:4096 * (layer + 1)], w_dram[e, layer]).then_inc(done, 16)


class Links:

    def __init__(self, eng, sem):
        self.eng, self.sem, self.k = eng, sem, 0

    def __call__(self, ins):
        self.k += 1
        ins.then_inc(self.sem, 1)
        self.eng.wait_ge(self.sem, self.k)

    def later(self, ins):
        self.k += 1
        ins.then_inc(self.sem, 1)

    def wait(self):
        self.eng.wait_ge(self.sem, self.k)

    def restart(self):
        if self.k:
            self.eng.sem_clear(self.sem)
        self.k = 0


def there(g):
    return 0 <= g < NG if isinstance(g, int) else True


def bass_flamingo(nc, x, ctx_in, g_xattn, g_ffn, w_q, b_q, w_k, b_k, w_v, b_v, w_o, b_o,
                  W1, b1, W2, b2, Wr, br, out):
    xs_dram = nc.dram_tensor("token_rows", [E * REG + TILE, ROW], F32, kind="Internal").ap()
    w_dram = nc.dram_tensor("split_weights", [E, 2, P, 2 * 2048], F16, kind="Internal").ap()

    with ExitStack() as stack:
        def sb(name, shape, dt=F32):
            return stack.enter_context(nc.sbuf_tensor(name, shape, dt))

        def sem(name):
            return stack.enter_context(nc.semaphore(name))

        wts = sb("wts", [P, E, 4 * 2048], F16)
        stacked = wts[:, E - 2:E, :].rearrange("p e n -> p (e n)").bitcast(BF16)
        stacked = stacked.rearrange("p (w a h t) -> p w a h t", w=2, a=2, h=HEADS)
        qst = [stacked[0:STACK, 0, i] for i in range(2)]
        kst = [stacked[0:STACK, 1, i] for i in range(2)]
        passing = wts[:, E - 4:E - 2, :].rearrange("p e n -> p (e n)")
        stage = [passing[:, 4096 * i:4096 * (i + 1)].bitcast(F32) for i in range(2)]
        split = [passing[:, 8192 + 4096 * i:8192 + 4096 * (i + 1)].rearrange("p (a n) -> p a n", a=2)
                 for i in range(2)]

        ident = sb("ident", [P, P])
        negident = sb("negident", [P, P], F32R)
        ident16 = sb("ident16", [P, P], BF16)
        mask4 = sb("mask4", [P, 4, P], BF16)
        earlier = sb("earlier", [P, P], BF16)
        ones16 = sb("ones16", [P, P], BF16)
        rank1 = sb("rank1", [P, 8])
        rank0 = sb("rank0", [P, 8])
        ones8 = sb("ones8", [P, 8])
        region0 = sb("region0", [P, 8])
        base = sb("base", [P, 8])
        mostsel = sb("mostsel", [P, GT])
        tgx = sb("tgx", [P, 1])
        tgf = sb("tgf", [P, 1])
        gates_in = sb("gates_in", [P, 2])
        power = sb("power", [P, GT])
        wscale = sb("wscale", [P, 2, 8])
        wsquares = sb("wsquares", [P, 2, 8])
        padrow = sb("padrow", [P, ROW])
        all_slots = sb("all_slots", [P, B, 8], I32)
        b1t = sb("b1t", [P, E, HC])
        gscale, hscale, yscale = sb("gscale", [P, E]), sb("hscale", [P, E]), sb("yscale", [P, E])
        small = sb("small", [P, 6, E])
        smallint = sb("smallint", [P, 3, E], I32)
        b1sq = sb("b1sq", [P, E, HC])
        padplace = sb("padplace", [1, E], I32)
        most = sb("most", [P, 2])
        mostint = sb("mostint", [P, 1], I32)
        tile_no = sb("tile_no", [1, ALL_TILES])
        past = sb("past", [1, ALL_TILES, E])
        te, ts = sb("te", [1, ALL_TILES]), sb("ts", [1, ALL_TILES])
        tile_no_int = te[:, :].bitcast(I32)
        tile_expert, tile_row = sb("tile_expert", [1, ALL_TILES], I32), sb("tile_row", [1, ALL_TILES], I32)
        numbers_made, pad_rows_ready, table_ready = sem("numbers_made"), sem("pad_rows_ready"), sem("table_ready")
        b1_sums, b1_total, most_ready, most_total = sem("b1_sums"), sem("b1_total"), sem("most_ready"), sem("most_total")
        scales_ready, weights_in, pads_in = sem("scales_ready"), sem("weights_in"), sem("pads_in")
        bank = [stack.enter_context(nc.psum_tensor(f"bank{i}", [P, 512], F32)) for i in range(8)]

        env = dict(locals())
        attention_and_routing(nc, env)
        experts(nc, env)


def attention_and_routing(nc, env):
    (x, ctx_in, g_xattn, g_ffn, w_q, b_q, w_k, b_k, w_v, b_v, w_o, b_o, W1, b1, W2, Wr, br, out,
     xs_dram, w_dram, bank, qst, kst, ident, negident, ident16, mask4, earlier, ones16, rank1,
     rank0, ones8, region0, base, mostsel, tgx, tgf, gates_in, power, wscale, wsquares, padrow,
     b1t, stage, split, all_slots, wts, tile_no_int, numbers_made, weights_in) = (env[k] for k in (
         "x", "ctx_in", "g_xattn", "g_ffn", "w_q", "b_q", "w_k", "b_k", "w_v", "b_v", "w_o", "b_o",
         "W1", "b1", "W2", "Wr", "br", "out", "xs_dram", "w_dram", "bank", "qst", "kst", "ident",
         "negident", "ident16", "mask4", "earlier", "ones16", "rank1", "rank0", "ones8", "region0",
         "base", "mostsel", "tgx", "tgf", "gates_in", "power", "wscale", "wsquares", "padrow",
         "b1t", "stage", "split", "all_slots", "wts", "tile_no_int", "numbers_made", "weights_in"))
    with ExitStack() as stack:
        def sb(name, shape, dt=F32):
            return stack.enter_context(nc.sbuf_tensor(name, shape, dt))

        def sem(name):
            return stack.enter_context(nc.semaphore(name))

        wq, wk, wv, wo = (sb(f"w{c}_sb", [P, KC, D]) for c in "qkvo")
        wr = sb("wr_sb", [P, KC, E])
        bqk = sb("bqk", [P, 2, 2])
        bv_all, bo_all = sb("bv_all", [P, D]), sb("bo_all", [P, D])
        br_all = sb("br_all", [P, E])
        xin = [sb(f"xin{i}", [P, GT, D]) for i in range(2)]
        cin = [sb(f"cin{i}", [P, GT, D]) for i in range(2)]
        xn = sb("xn", [P, GT, D])
        xT, cT = sb("xT", [P, KC, GT * P]), sb("cT", [P, KC, GT * P])
        xb = [sb(f"xb{i}", [P, GT, D]) for i in range(2)]
        queries, keys = (sb(name, [P, 3, 2, GT * P], BF16) for name in ("queries", "keys"))
        q_rest, k_rest = (sb(name, [P, 2, GT * P]) for name in ("q_rest", "k_rest"))
        va = [sb(f"va{i}", [P, GT, HEADS, VA]) for i in range(2)]
        rowmax = [sb(f"rowmax{i}", [P, 4], F32R) for i in range(2)]
        probs = [sb(f"probs{i}", [P, 4, P]) for i in range(4)]
        rden = sb("rden", [P, HEADS])
        ao = [sb(f"ao{i}", [P, HEADS, DK]) for i in range(2)]
        aoT = [sb(f"aoT{i}", [P, KC, P]) for i in range(2)]
        x2 = [sb(f"x2_{i}", [P, GT, D]) for i in range(2)]
        pay = [sb(f"pay{i}", [P, GT, ROW]) for i in range(2)]
        x2T = sb("x2T", [P, KC, GT * P])
        bn, bn1 = sb("bn", [P, GT, 6]), sb("bn1", [P, GT, 6])
        mv1, mv2 = sb("mv1", [P, GT, 2]), sb("mv2", [P, GT, 2])
        rs1, rs2 = sb("rs1", [P, GT]), sb("rs2", [P, GT])
        partsum, allsum = sb("partsum", [P, 4]), sb("allsum", [P, 2, 4])
        ebits = sb("ebits", [P, 1], I32)
        wsum, wnow = sb("wsum", [P, 2]), sb("wnow", [P, 2])
        ints = sb("ints", [P, 3, 8], I32)
        lg, mx, lgs = sb("lg", [P, GT, E]), sb("mx", [P, GT, 8]), sb("lgs", [P, GT, E])
        msk, msk16 = sb("msk", [P, GT, E]), sb("msk16", [P, GT, E], BF16)
        ex, em, esum, erec = sb("ex", [P, GT, E]), sb("em", [P, GT, E]), sb("esum", [P, GT]), sb("erec", [P, GT])
        cnt, cm, inv = sb("cnt", [P, GT, E]), sb("cm", [P, GT, E]), sb("inv", [P, GT, E])
        pos, slotf = sb("pos", [P, GT, E]), sb("slotf", [P, GT, E])
        sel = sb("sel", [P, GT, 8, E])
        slots = [sb(f"slots{i}", [P, GT, 8], I32) for i in range(2)]

        BT = bank[0]
        PJA, PJB = bank[1], bank[2]
        SB = [bank[3], bank[4]]
        TB = [bank[5], bank[6]]
        OB = bank[7]

        consts = sem("consts")
        first_params, params = sem("first_params"), sem("params")
        tanh_ready, bias_ready = sem("tanh_ready"), sem("bias_ready")
        x_loaded, c_loaded, kst_ready, qst_ready, x2_stored, scattered, w_staged, w_stored = (
            [sem(f"{name}{i}") for i in range(2)] for name in (
                "x_loaded", "c_loaded", "kst_ready", "qst_ready", "x2_stored", "scattered",
                "w_staged", "w_stored"))
        var1_ready, rstd1_ready, xn_ready = sem("var1_ready"), sem("rstd1_ready"), sem("xn_ready")
        cT_psum, cT_ready = sem("cT_psum"), sem("cT_ready")
        xT_psum, xT_ready = sem("xT_psum"), sem("xT_ready")
        k_psum, keys_ready = sem("k_psum"), sem("keys_ready")
        k_first, k_left, k_second = sem("k_first"), sem("k_left"), sem("k_second")
        q_first, q_left, q_second = sem("q_first"), sem("q_left"), sem("q_second")
        q_psum, queries_ready = sem("q_psum"), sem("queries_ready")
        v_psum, va_ready = sem("v_psum"), sem("va_ready")
        s_psum, max_ready = sem("s_psum"), sem("max_ready")
        st_psum, exp_ready, probs_ready = sem("st_psum"), sem("exp_ready"), sem("probs_ready")
        pv_psum, ao_ready = sem("pv_psum"), sem("ao_ready")
        aoT_psum, aoT_ready = sem("aoT_psum"), sem("aoT_ready")
        o_psum, x2_ready = sem("o_psum"), sem("x2_ready")
        xb_ready = sem("xb_ready")
        var2_ready, rstd2_ready, xn2_ready = sem("var2_ready"), sem("rstd2_ready"), sem("xn2_ready")
        x2T_psum, x2T_ready = sem("x2T_psum"), sem("x2T_ready")
        r_psum, logits_read, shifted_ready = sem("r_psum"), sem("logits_read"), sem("shifted_ready")
        ex_ready, pos_psum, pos_read = sem("ex_ready"), sem("pos_psum"), sem("pos_read")
        slots_ready = sem("slots_ready")
        w_sums, w_total, w_scaled = sem("w_sums"), sem("w_total"), sem("w_scaled")
        w_high, w_low = sem("w_high"), sem("w_low")
        mask_ready = sem("mask_ready")
        dve_consts, waits_taken = sem("dve_consts"), sem("waits_taken")
        dve_steps, pool_steps = sem("dve_steps"), sem("pool_steps")


        def bt_before(g, k):
            order = [(cT_ready, 1, lambda i: i + 1), (xT_ready, 1, lambda i: i + 1),
                     (x2T_ready, -1, lambda i: 2 * i + 1), (aoT_ready, -1, lambda i: 2 * i + 2),
                     (x2T_ready, -1, lambda i: 2 * i + 2), (aoT_ready, 0, lambda i: 2 * i + 1)]
            while True:
                k -= 1
                if k < 0:
                    g, k = g - 1, 5
                s, d, count = order[k]
                if there(g + d):
                    return s, count(g + d)
                if isinstance(g, int) and g < -2:
                    return None

        def free_bt(pe, g, k):
            w = bt_before(g, k)
            if w:
                pe.wait_ge(*w)

        def loop_over_groups(eng, it):
            for g in (-2, -1, 0, 1):
                it(g, g % 2, g // 2)
            with eng.Fori(0, (NG - 4) // 2) as u:
                it(u * 2 + 2, 0, u + 1)
                it(u * 2 + 3, 1, u + 1)
            for g in range(NG - 2, NG + 2):
                it(g, g % 2, g // 2)

        def arrived(eng, sems, g, par, dmas=1, ok=True):
            if ok:
                eng.wait_ge(sems[par], (g - par) * (8 * dmas) + 16 * dmas)

        def settled(eng):
            eng.sem_inc(waits_taken, 1)

        def when(eng, ok, s, value):
            if ok:
                eng.wait_ge(s, value)

        with nc.Block() as block:

            @block.sync
            def _(sp):
                def load(dst, src, done=params):
                    sp.dma_start(dst, src).then_inc(done, 16)

                def group_rows(a, g):
                    return a[bass.ds(g * (GT * P), GT * P), :].rearrange("(b p) d -> p b d", p=P)

                def it(g, par, half):
                    if there(g + 2):
                        when(sp, there(g), xn_ready, g + 1)
                        settled(sp)
                        when(sp, there(g), xb_ready, g + 1)
                        settled(sp)
                        when(sp, there(g), cT_psum, g + 1)
                        settled(sp)
                        sp.dma_start(xin[par][:, :, :], group_rows(x, g + 2)).then_inc(x_loaded[par], 16)
                        sp.dma_start(cin[par][:, :, :], group_rows(ctx_in, g + 2)).then_inc(c_loaded[par], 16)
                    if isinstance(g, int) and g == -2:
                        load(wk[:, :, :], w_k.rearrange("(k p) n -> p k n", p=P), first_params)
                        load(bqk[:, 0, :], b_q, first_params)
                        load(bqk[:, 1, :], b_k, first_params)
                        load(wv[:, :, :], w_v.rearrange("(k p) n -> p k n", p=P), first_params)
                        load(wq[:, :, :], w_q.rearrange("(k p) n -> p k n", p=P), first_params)
                        load(bv_all[:, :], b_v.partition_broadcast(P), first_params)
                        load(wo[:, :, :], w_o.rearrange("(k p) n -> p k n", p=P))
                        load(bo_all[:, :], b_o.partition_broadcast(P))
                        load(wr[:, :, :], Wr.rearrange("(k p) n -> p k n", p=P))
                        load(br_all[:, :], br.partition_broadcast(P))
                        load(gates_in[:, 0:1], g_xattn.partition_broadcast(P))
                        load(gates_in[:, 1:2], g_ffn.partition_broadcast(P))
                        load(b1t[:, :, :], b1)
                        sp.wait_ge(consts, 2)
                        load(out[T:T + P, :], padrow[:, 0:D])
                        for half in range(2):
                            at = E * REG + half * P
                            load(xs_dram[at:at + P, :], padrow[:, :])
                    if there(g):
                        when(sp, there(g - 2), w_low, (g - 1) * 4)
                        settled(sp)
                        e = half
                        if par == 0:
                            src = W1[bass.ds(e, 1), :, :].rearrange("a (k p) n -> p (a k) n", p=P)
                            dst = stage[0].rearrange("p (k n) -> p k n", k=KC)
                        else:
                            src = W2[bass.ds(e, 1), :, :].rearrange("a (k p) n -> p (a k) n", p=P)
                            dst = stage[1].rearrange("p (k n) -> p k n", k=HC)
                        sp.dma_start(dst, src).then_inc(w_staged[par], 16)
                    if there(g + 1):
                        for w, src, st, made, dst_ready in (
                                (1, keys, kst, (k_first, k_second, keys_ready), kst_ready),
                                (0, queries, qst, (q_first, q_second, queries_ready), qst_ready)):
                            when(sp, there(g - 1), st_psum, g * QUADS)
                            settled(sp)
                            for part in range(3):
                                sp.wait_ge(made[part], g + 2)
                                settled(sp)
                                for at, parts in enumerate(PRODUCTS):
                                    if parts[w] == part:
                                        sp.dma_start(st[1 - par][DK * at:DK * at + DK, :, :],
                                                     src[:, part, :, :]).then_inc(dst_ready[1 - par], 16)
                    if there(g - 1):
                        sp.wait_ge(x2_ready, g * GT)
                        settled(sp)
                        sp.dma_start(group_rows(out, g - 1), x2[1 - par][:, :, :]).then_inc(x2_stored[1 - par], 16)
                        sp.wait_ge(w_low, g * 4)
                        settled(sp)
                        e = half - (1 - par)
                        rows = w_dram[bass.ds(e, 1), 1 - par, :, :].rearrange("a p n -> p (a n)")
                        sp.dma_start(rows, split[1 - par].rearrange("p a n -> p (a n)")).then_inc(w_stored[1 - par], 16)
                    if isinstance(g, int) and NG - 2 <= g <= NG:
                        e = g - (NG - 2)
                        if e == 0:
                            for i in range(2):
                                arrived(sp, w_stored, 2 * (EARLY - 1) + i, i)
                                settled(sp)
                        else:
                            sp.wait_ge(weights_in, 16 * 2 * e)
                        load_weights(sp, wts, w_dram, e, weights_in)

                loop_over_groups(sp, it)
                padding(sp, env, range(E // 2))
                sp.wait_ge(weights_in, 16 * 2 * (EARLY - 1))
                load_weights(sp, wts, w_dram, EARLY - 1, weights_in)
                for i in range(2):
                    arrived(sp, x2_stored, NG - 2 + i, i)
                    settled(sp)
                    arrived(sp, w_stored, NG - 2 + i, i)
                    settled(sp)
                sp.wait_ge(params, 16 * 10)

            @block.gpsimd
            def _(pool):
                step = Links(pool, pool_steps)
                step.later(pool.memset(ident[:, :], 0.0))
                step.later(pool.memset(mask4[:, :, :], 0.0))
                step.later(pool.memset(earlier[:, :], 1.0))
                step.later(pool.memset(padrow[:, :], 0.0))
                for i in range(2):
                    step.later(pool.memset(pay[i][:, :, D + E:], 0.0))
                step(pool.memset(power[:, :], -0.5))
                pool.iota(padrow[:, D + E:D + E + 1].bitcast(I32), pattern=[[0, 1]], base=T,
                          channel_multiplier=1).then_inc(consts, 1)
                pool.affine_select(out=ident[:, :], in_=ident[:, :], compare_op=ALU.not_equal,
                                   fill=1.0, base=0, pattern=[[-1, P]], channel_multiplier=1).then_inc(consts, 1)
                pool.affine_select(out=mask4[:, :, :], in_=mask4[:, :, :], compare_op=ALU.is_ge,
                                   fill=MASKED, base=0, pattern=[[0, 4], [-1, P]],
                                   channel_multiplier=1).then_inc(consts, 1)
                pool.affine_select(out=earlier[:, :], in_=earlier[:, :], compare_op=ALU.is_gt,
                                   fill=0.0, base=0, pattern=[[1, P]], channel_multiplier=-1).then_inc(consts, 1)
                pool.iota(ints[:, 0, :], pattern=[[1, 8]], base=0, channel_multiplier=0).then_inc(consts, 1)
                pool.iota(ints[:, 1, :], pattern=[[1, 8]], base=1, channel_multiplier=0).then_inc(consts, 1)
                pool.iota(ints[:, 2, :], pattern=[[REG, 8]], base=0, channel_multiplier=0).then_inc(consts, 1)
                for i in range(2):
                    pool.iota(pay[i][:, :, D + E:D + E + 1].bitcast(I32), pattern=[[P, GT], [0, 1]],
                              base=(i - 2) * GT * P, channel_multiplier=1).then_inc(consts, 1)

                pool.iota(tile_no_int, pattern=[[1, ALL_TILES]], base=0, channel_multiplier=0
                          ).then_inc(numbers_made, 1)

                def it(g, par, half):
                    for n in range(QUADS):
                        q, pg = (QUADS - 1, g - 1) if n == 0 else (n - 1, g)
                        if n in (1, 5) and there(g - 1):
                            b = n // 4
                            pool.wait_ge(var2_ready, (g - 1) * GT + b + 1)
                            pool.tensor_tensor(rs2[:, b:b + 1], mv2[:, b, 1:2], power[:, 0:1],
                                               ALU.pow).then_inc(rstd2_ready, 1)
                        if there(pg):
                            pool.wait_ge(exp_ready, pg * QUADS + q + 1)
                            settled(pool)
                            pool.affine_select(out=probs[q % 4][:, :, :], in_=probs[q % 4][:, :, :],
                                               compare_op=ALU.is_ge, fill=0.0, base=0,
                                               pattern=[[0, 4], [1, P]],
                                               channel_multiplier=-1).then_inc(probs_ready, 1)
                        if n == 5 and there(g + 1):
                            arrived(pool, x_loaded, g + 1, 1 - par)
                            when(pool, there(g - 1), x2_ready, g * GT)
                            pool.wait_ge(bias_ready, 1)
                            pool.tensor_tensor(xb[1 - par][:, :, :], xin[1 - par][:, :, :],
                                               bo_all[:, :].unsqueeze(1).to_broadcast([P, GT, D]),
                                               ALU.add).then_inc(xb_ready, 1)
                        if n >= 4 and there(g - 2):
                            b, r = (n - 4) // 2, n % 2
                            if n == 4:
                                pool.wait_ge(slots_ready, g - 1)
                                settled(pool)
                            pool.indirect_dma_start(
                                out=xs_dram[:, :],
                                out_offset=bass.IndirectOffsetOnAxis(ap=slots[par][:, b, r:r + 1], axis=0),
                                in_=pay[par][:, b, :], in_offset=None,
                                bounds_check=E * REG - 1, oob_is_err=False).then_inc(scattered[par], 16)
                        if n == 7 and there(g):
                            pool.wait_ge(w_sums, g * 4 + 4)
                            when(pool, there(g - 1), w_scaled, g)
                            settled(pool)
                            pool.partition_all_reduce(allsum[:, par, :], partsum[:, :], P, ADD_ALL).then_inc(w_total, 1)
                        if n == 7 and there(g + 2):
                            pool.wait_ge(var1_ready, g + 3)
                            when(pool, there(g + 1), xn_ready, g + 2)
                            pool.tensor_tensor(rs1[:, :], mv1[:, :, 1], power[:, 0:GT],
                                               ALU.pow).then_inc(rstd1_ready, 1)

                loop_over_groups(pool, it)
                pool.wait_ge(env["most_ready"], 1)
                pool.partition_all_reduce(env["most"][:, 1:2], env["most"][:, 0:1], P,
                                          MAX_ALL).then_inc(env["most_total"], 1)
                pool.wait_ge(env["b1_sums"], 1)
                pool.partition_all_reduce(env["small"][:, 1, :], env["small"][:, 0, :], P,
                                          ADD_ALL).then_inc(env["b1_total"], 1)
                for i in range(2):
                    arrived(pool, scattered, NG - 2 + i, i, 4)

            @block.scalar
            def _(act):
                def first_part(g, g1, par, n):
                    w, dst, ps, psum, done, restacked = (
                        (1, keys, k_psum, PJB, k_first, kst_ready) if n == 1 else
                        (0, queries, q_psum, PJA, q_first, qst_ready))
                    act.wait_ge(ps, g1 + 1)
                    arrived(act, restacked, g, par, 6, there(g))
                    for odd in range(2):
                        last = act.activation(dst[:, 0, odd, :], psum[:, 256 * odd:256 * odd + 256],
                                              ACT.Identity, bias=bqk[:, w, odd:odd + 1])
                    last.then_inc(done, 1)

                def it(g, par, half):
                    g1, p1 = g + 1, 1 - par
                    for n in range(QUADS):
                        if isinstance(g, int) and g == -1 and n == 1:
                            act.wait_ge(first_params, 16 * 6)
                        if isinstance(g, int) and g == -1 and n == 2:
                            act.wait_ge(params, 16 * 10)
                            act.activation(tgx[:, :], gates_in[:, 0:1], ACT.Tanh).then_inc(tanh_ready, 1)
                            act.activation(tgf[:, :], gates_in[:, 1:2], ACT.Tanh).then_inc(tanh_ready, 1)
                        if n == 1 and there(g1):
                            first_part(g, g1, par, n)
                        q, pg = (QUADS - 1, g - 1) if n == 0 else (n - 1, g)
                        if there(pg):
                            act.wait_ge(st_psum, pg * QUADS + q + 1)
                            before = there(pg - 1) if q < 4 else True
                            when(act, before, pv_psum, pg * QUADS + q - 3)
                            act.activation(probs[q % 4][:, :, :].rearrange("p a q -> p (a q)"), TB[q % 2][:, :],
                                           ACT.Exp, scale=float(DK) ** -0.5).then_inc(exp_ready, 1)
                        if n == 0 and there(g1):
                            act.wait_ge(cT_psum, g1 + 1)
                            when(act, there(g), v_psum, g + 1)
                            act.activation(cT[:, :, :].rearrange("p k t -> p (k t)"), BT[:, :],
                                           ACT.Copy).then_inc(cT_ready, 1)
                        if n == 0 and there(g - 2):
                            act.wait_ge(shifted_ready, g - 1)
                            when(act, there(g - 3), slots_ready, g - 2)
                            act.activation(ex[:, :, :], lgs[:, :, :], ACT.Exp).then_inc(ex_ready, 1)
                        if n == 3 and there(g1):
                            first_part(g, g1, par, n)
                        if n in (2, 4) and there(g1):
                            dst, rest, left, done = ((keys, k_rest, k_left, k_second) if n == 2 else
                                                     (queries, q_rest, q_left, q_second))
                            act.wait_ge(left, g1 + 1)
                            act.activation(dst[:, 1, :, :], rest[:, :, :], ACT.Copy).then_inc(done, 1)
                        if n == 1 and there(g1):
                            act.wait_ge(xT_psum, g1 + 1)
                            when(act, there(g), q_psum, g + 1)
                            act.activation(xT[:, :, :].rearrange("p k t -> p (k t)"), BT[:, :],
                                           ACT.Copy).then_inc(xT_ready, 1)
                        if n in (2, 6) and there(g - 1):
                            b = n // 4
                            act.wait_ge(x2T_psum, (g - 1) * GT + b + 1)
                            when(act, there(g - 2), r_psum, g - 1)
                            act.activation(x2T[:, :, b * P:(b + 1) * P],
                                           BT[:, 0:D].rearrange("p (k t) -> p k t", k=KC),
                                           ACT.Copy).then_inc(x2T_ready, 1)
                        if (n == 3 and there(g - 1)) or (n == 7 and there(g)):
                            b, tg = (1, g - 1) if n == 3 else (0, g)
                            act.wait_ge(aoT_psum, tg * GT + b + 1)
                            when(act, there(tg - 1), o_psum, (tg - 1) * GT + b + 1)
                            act.activation(aoT[b][:, :, :].rearrange("p k t -> p (k t)"), BT[:, 0:D],
                                           ACT.Copy).then_inc(aoT_ready, 1)
                        if 3 <= n <= 6 and there(g):
                            k = n - 3
                            c = slice(512 * k, 512 * k + 512)
                            if k == 0:
                                arrived(act, w_staged, g, par)
                                when(act, there(g - 1), w_total, g)
                                arrived(act, w_stored, g - 2, par, 1, there(g - 2))
                            act.activation(split[par][:, 1, c].bitcast(BF16), stage[par][:, c], ACT.Square,
                                           accum_out=partsum[:, k:k + 1]).then_inc(w_sums, 1)
                        if 1 <= n <= 4 and there(g - 1):
                            k = n - 1
                            c = slice(512 * k, 512 * k + 512)
                            act.wait_ge(w_scaled, g)
                            act.activation(split[p1][:, 0, c], stage[p1][:, c], ACT.Copy,
                                           scale=wnow[:, p1:p1 + 1]).then_inc(w_high, 1)

                loop_over_groups(act, it)
                padding(act, env, range(E // 2, E))

            @block.vector
            def _(dve):
                step = Links(dve, dve_steps)
                for i in range(2):
                    step.later(dve.memset(va[i][:, :, :, DK:DK + 1], 1.0))
                step.later(dve.memset(mostsel[:, :], 0.0))
                step.later(dve.memset(ones8[:, :], 1.0))
                step.later(dve.memset(ones16[:, :], 1.0))
                dve.wait_ge(consts, 9)
                step.later(dve.tensor_copy(rank0[:, :], ints[:, 0, :]))
                step.later(dve.tensor_copy(rank1[:, :], ints[:, 1, :]))
                step.later(dve.tensor_copy(region0[:, :], ints[:, 2, :]))
                step.later(dve.tensor_copy(base[:, :], ints[:, 2, :]))
                step.later(dve.tensor_scalar(negident[:, :], ident[:, :], -1.0, None, ALU.mult))
                dve.tensor_copy(ident16[:, :], ident[:, :]).then_inc(dve_consts, 1)
                step.wait()

                def variance(src, bn_, mv, done):
                    step(dve.bn_stats(bn_, src))
                    step(dve.bn_aggr(mv, bn_))
                    dve.tensor_scalar_add(mv[:, 1:2], mv[:, 1:2], EPS).then_inc(done, 1)

                def rest(g1, n):
                    w, dst, left, psum, first, done = ((1, keys, k_rest, PJB, k_first, k_left) if n == 1 else
                                                       (0, queries, q_rest, PJA, q_first, q_left))
                    dve.wait_ge(first, g1 + 1)
                    when(dve, there(g1 - 1), queries_ready if w == 0 else keys_ready, g1)
                    for odd in range(2):
                        last = dve.scalar_tensor_tensor(
                            out=left[:, odd, :], in0=psum[:, 256 * odd:256 * odd + 256],
                            scalar=bqk[:, w, odd:odd + 1], in1=dst[:, 0, odd, :], op0=ALU.add, op1=ALU.subtract)
                    last.then_inc(done, 1)

                def third(g1, p1, n):
                    dst, left, second, done, restacked = (
                        (keys, k_rest, k_second, keys_ready, kst_ready) if n == 2 else
                        (queries, q_rest, q_second, queries_ready, qst_ready))
                    dve.wait_ge(second, g1 + 1)
                    arrived(dve, restacked, g1 - 1, 1 - p1, 6, there(g1 - 1))
                    dve.tensor_tensor(dst[:, 2, :, :], left[:, :, :], dst[:, 1, :, :], ALU.subtract).then_inc(done, 1)

                def normalise(g, b):
                    t = g * GT + b
                    dve.wait_ge(pv_psum, (t + 1) * 4)
                    when(dve, there(g - 1), aoT_psum, t - 1)
                    o = OB[:, 0:HEADS * VA].rearrange("p (h v) -> p h v", h=HEADS)
                    step(dve.reciprocal(rden[:, :], o[:, :, DK]))
                    dve.tensor_tensor(ao[b][:, :, :], o[:, :, 0:DK],
                                      rden[:, :].unsqueeze(2).to_broadcast([P, HEADS, DK]),
                                      ALU.mult).then_inc(ao_ready, 1)

                def residual(g, b, psum, i):
                    t = g * GT + b
                    dve.wait_ge(o_psum, t + 1)
                    dve.wait_ge(xb_ready, g + 1)
                    arrived(dve, x2_stored, g - 2, i, 1, there(g - 2))
                    dve.scalar_tensor_tensor(out=x2[i][:, b, :], in0=psum[:, 0:D], scalar=tgx[:, 0:1],
                                             in1=xb[i][:, b, :], op0=ALU.mult, op1=ALU.add).then_inc(x2_ready, 1)
                    dve.wait_ge(x2_ready, t + 1)
                    variance(x2[i][:, b, :], bn[:, b, :], mv2[:, b, :], var2_ready)

                def norm2(g, b, i):
                    dve.wait_ge(rstd2_ready, g * GT + b + 1)
                    arrived(dve, scattered, g - 2, i, 4, there(g - 2))
                    dve.tensor_scalar(pay[i][:, b, 0:D], x2[i][:, b, :], mv2[:, b, 0:1], rs2[:, b:b + 1],
                                      ALU.subtract, ALU.mult).then_inc(xn2_ready, 1)

                def over_ranks(a):
                    return a.unsqueeze(2).to_broadcast([P, GT, 8, E])

                def it(g, par, half):
                    settled(dve)
                    step.restart()
                    g1, p1 = g + 1, 1 - par
                    for n in range(QUADS):
                        if isinstance(g, int) and g == -1 and n == 4:
                            dve.wait_ge(tanh_ready, 2)
                            dve.tensor_scalar(bo_all[:, :], bo_all[:, :], tgx[:, 0:1], None,
                                              ALU.mult).then_inc(bias_ready, 1)
                        if n == 3 and there(g - 1):
                            normalise(g - 1, 1)
                        if n == 7 and there(g):
                            normalise(g, 0)
                        if n == 2 and there(g - 2):
                            dve.wait_ge(pos_psum, g - 1)
                            step(dve.tensor_tensor(pos[:, :, :], PJA[:, 0:GT * E].rearrange("p (b e) -> p b e", b=GT),
                                                   base[:, :].unsqueeze(1).to_broadcast([P, GT, E]), ALU.add))
                            dve.tensor_tensor(base[:, :], base[:, :], PJA[:, GT * E:GT * E + E],
                                              ALU.add).then_inc(pos_read, 1)
                        if there(g):
                            dve.wait_ge(s_psum, g * QUADS + n + 1)
                            when(dve, n >= 2 or there(g - 1), st_psum, g * QUADS + n - 1)
                            dve.tensor_reduce(rowmax[n % 2][:, :], SB[n % 2][:, :].rearrange("p (a k) -> p a k", a=4),
                                              AX, ALU.max).then_inc(max_ready, 1)
                        if n == 5 and there(g - 1):
                            norm2(g - 1, 1, p1)
                        if n in (2, 3, 6, 7) and there(g - 1):
                            k = (2, 3, 6, 7).index(n)
                            c = slice(512 * k, 512 * k + 512)
                            dve.wait_ge(w_high, g * 4 - 3 + k)
                            dve.scalar_tensor_tensor(out=split[p1][:, 1, c], in0=stage[p1][:, c],
                                                     scalar=wnow[:, p1:p1 + 1], in1=split[p1][:, 0, c],
                                                     op0=ALU.mult, op1=ALU.subtract).then_inc(w_low, 1)
                        if n == 0 and there(g1):
                            dve.wait_ge(rstd1_ready, g1 + 1)
                            when(dve, there(g), xT_psum, g + 1)
                            for b in range(GT):
                                last = dve.tensor_scalar(xn[:, b, :], xin[p1][:, b, :], mv1[:, b, 0:1],
                                                         rs1[:, b:b + 1], ALU.subtract, ALU.mult)
                            last.then_inc(xn_ready, 1)
                        if n == 0 and there(g - 1):
                            residual(g - 1, 0, PJA, p1)
                        if n == 0 and there(g - 1):
                            dve.wait_ge(w_total, g)
                            step(dve.tensor_reduce(wsum[:, p1:p1 + 1], allsum[:, p1, :], AX, ALU.add))
                            step(dve.tensor_scalar(ebits[:, :], wsum[:, p1:p1 + 1].bitcast(I32), 24, None,
                                                   ALU.logical_shift_right))
                            dve.tensor_scalar(wnow[:, p1:p1 + 1].bitcast(I32), ebits[:, :], -float(1 << 23),
                                              204.0 * (1 << 23), ALU.mult, ALU.add).then_inc(w_scaled, 1)
                            dve.wait_ge(w_scaled, g)
                            e = half - (1 - par)
                            dve.tensor_copy(wscale[:, p1, bass.ds(e, 1)], wnow[:, p1:p1 + 1])
                            step(dve.tensor_copy(wsquares[:, p1, bass.ds(e, 1)], wsum[:, p1:p1 + 1]))
                        if n == 1 and there(g1):
                            rest(g1, n)
                        if n == 1 and there(g - 1):
                            norm2(g - 1, 0, p1)
                        if n == 1 and there(g - 2):
                            dve.wait_ge(ex_ready, g - 1)
                            step(dve.tensor_tensor(em[:, :, :], ex[:, :, :], msk[:, :, :], ALU.mult))
                            for b in range(GT):
                                step.later(dve.tensor_tensor_scan(cnt[:, b, :], ones8[:, :], msk[:, b, :], 0.0,
                                                                  ALU.mult, ALU.add))
                            step(dve.tensor_reduce(esum[:, :], em[:, :, :], AX, ALU.add))
                            step.later(dve.reciprocal(erec[:, :], esum[:, :]))
                            step.later(dve.tensor_tensor(cm[:, :, :], cnt[:, :, :], msk[:, :, :], ALU.mult))
                            step(dve.tensor_tensor(mostsel[:, :], mostsel[:, :], cnt[:, :, E - 1], ALU.max))
                            step.later(dve.scalar_tensor_tensor(
                                out=pay[par][:, :, D:D + E], in0=em[:, :, :], scalar=tgf[:, 0:1],
                                in1=erec[:, :].unsqueeze(2).to_broadcast([P, GT, E]), op0=ALU.mult, op1=ALU.mult))
                            numbers = pay[par][:, :, D + E:D + E + 1].bitcast(I32)
                            step.later(dve.tensor_scalar(numbers, numbers, float(2 * GT * P), None, ALU.add))
                            step.later(dve.tensor_tensor(inv[:, :, :], rank0[:, :].unsqueeze(1).to_broadcast([P, GT, 8]),
                                                         cnt[:, :, E - 1:E].to_broadcast([P, GT, 8]), ALU.is_ge))
                            step(dve.tensor_tensor(sel[:, :, :, :], over_ranks(cm[:, :, :]),
                                                   rank1[:, :].unsqueeze(1).unsqueeze(3).to_broadcast([P, GT, 8, E]),
                                                   ALU.is_equal))
                        if n == 2 and there(g - 2):
                            step(dve.tensor_tensor(sel[:, :, :, :], sel[:, :, :, :], over_ranks(pos[:, :, :]), ALU.mult))
                            step(dve.tensor_reduce(slotf[:, :, :], sel[:, :, :, :], AX, ALU.add))
                            arrived(dve, scattered, g - 4, par, 4, there(g - 4))
                            dve.scalar_tensor_tensor(out=slots[par][:, :, :], in0=inv[:, :, :], scalar=OFF_BIG,
                                                     in1=slotf[:, :, :], op0=ALU.mult,
                                                     op1=ALU.add).then_inc(slots_ready, 1)
                            dve.wait_ge(slots_ready, g - 1)
                            step.later(dve.tensor_copy(all_slots[:, bass.ds((g - 2) * GT, GT), :], slots[par][:, :, :]))
                        if n in (2, 5) and there(g1):
                            third(g1, p1, n)
                        if n == 3 and there(g1):
                            dve.wait_ge(v_psum, g1 + 1)
                            when(dve, there(g - 1), pv_psum, g * QUADS)
                            dve.tensor_tensor(va[p1][:, :, :, 0:DK],
                                              PJB[:, :].rearrange("p (b h v) -> p b h v", b=GT, h=HEADS),
                                              bv_all[:, :].rearrange("p (h v) -> p h v", h=HEADS).unsqueeze(1)
                                              .to_broadcast([P, GT, HEADS, DK]), ALU.add).then_inc(va_ready, 1)
                        if n == 3 and there(g1):
                            rest(g1, n)
                        if n == 4 and there(g - 1):
                            residual(g - 1, 1, PJB, p1)
                        if n == 7 and there(g + 2):
                            arrived(dve, x_loaded, g + 2, par)
                            for b in range(GT):
                                step.later(dve.bn_stats(bn1[:, b, :], xin[par][:, b, :]))
                            when(dve, there(g1), xn_ready, g1 + 1)
                            step.wait()
                            settled(dve)
                            for b in range(GT):
                                step.later(dve.bn_aggr(mv1[:, b, :], bn1[:, b, :]))
                            step.wait()
                            dve.tensor_scalar_add(mv1[:, :, 1:2], mv1[:, :, 1:2], EPS).then_inc(var1_ready, 1)
                        if n == 7 and there(g - 1):
                            dve.wait_ge(r_psum, g)
                            dve.tensor_tensor(lg[:, :, :], PJA[:, 0:GT * E].rearrange("p (b e) -> p b e", b=GT),
                                              br_all[:, :].unsqueeze(1).to_broadcast([P, GT, E]),
                                              ALU.add).then_inc(logits_read, 1)
                            dve.wait_ge(logits_read, g)
                            settled(dve)
                            for b in range(GT):
                                last = dve.max(mx[:, b, :], lg[:, b, :])
                            step(last)
                            step.later(dve.tensor_tensor(msk[:, :, :], lg[:, :, :],
                                                         mx[:, :, 1:2].to_broadcast([P, GT, E]), ALU.is_ge))
                            dve.tensor_tensor(msk16[:, :, :], lg[:, :, :],
                                              mx[:, :, 1:2].to_broadcast([P, GT, E]), ALU.is_ge).then_inc(mask_ready, 1)
                            dve.tensor_tensor(lgs[:, :, :], lg[:, :, :], mx[:, :, 0:1].to_broadcast([P, GT, E]),
                                              ALU.subtract).then_inc(shifted_ready, 1)
                            dve.wait_ge(shifted_ready, g)

                loop_over_groups(dve, it)
                tile_table(dve, step, env)

            @block.tensor
            def _(pe):
                pe.wait_ge(dve_consts, 1)

                def transposes(parts, done):
                    for i, (src, n) in enumerate(parts):
                        last = pe.transpose(BT[:, i * P:(i + 1) * P], src, ident[:, :])
                    last.then_inc(done, 1)

                def product(psum, lhsT, rhs):
                    for k in range(KC):
                        last = pe.matmul(psum, lhsT(k), rhs(k), start=k == 0, stop=k == KC - 1)
                    return last

                def it(g, par, half):
                    g1, p1 = g + 1, 1 - par
                    for n in range(QUADS):
                        idx = g * QUADS + n
                        odd, pairs = n % 2, range(4 * ((n % 4) // 2), 4 * ((n % 4) // 2) + 4)
                        if there(g):
                            if n == 0:
                                arrived(pe, kst_ready, g, par, 6)
                                arrived(pe, qst_ready, g, par, 6)
                            when(pe, n >= 2 or there(g - 1), max_ready, idx - 1)
                            ps = SB[n % 2]
                            tok = slice((n // 4) * P, (n // 4) * P + P)
                            pe.matmul(ps[:, :], ident16[:, :], mask4[:, :, :].rearrange("p a k -> p (a k)"),
                                      start=True, stop=False)
                            for i, j in enumerate(pairs):
                                last = pe.matmul(ps[:, i * P:(i + 1) * P], qst[par][:, 2 * j + odd, tok],
                                                 kst[par][:, 2 * j + odd, tok], start=False, stop=i == 3)
                            last.then_inc(s_psum, 1)
                        if n == 0 and there(g1):
                            arrived(pe, c_loaded, g1, p1)
                            free_bt(pe, g, 0)
                            transposes([(cin[p1][:, b, k * P:(k + 1) * P], 0) for k in range(KC) for b in range(GT)],
                                       cT_psum)
                        if isinstance(g, int) and g == 0 and n == 0:
                            pe.wait_ge(params, 16 * 10)
                        if n == 0 and there(g - 1):
                            pe.wait_ge(aoT_ready, (g - 1) * GT + 1)
                            when(pe, there(g - 2), logits_read, g - 1)
                            product(PJA[:, 0:D], lambda k: aoT[0][:, k, :], lambda k: wo[:, k, :]).then_inc(o_psum, 1)
                        if isinstance(g, int) and g == -1 and n == 1:
                            pe.wait_ge(first_params, 16 * 6)
                        if n == 1 and there(g1):
                            pe.wait_ge(cT_ready, g1 + 1)
                            when(pe, there(g), va_ready, g + 1)
                            when(pe, there(g - 2), x2_ready, (g - 1) * GT)
                            for o in range(2):
                                last = product(PJB[:, 256 * o:256 * o + 256], lambda k: wk[:, k, o * P:(o + 1) * P],
                                               lambda k: cT[:, k, :])
                            last.then_inc(k_psum, 1)
                            pe.wait_ge(xn_ready, g1 + 1)
                            free_bt(pe, g, 1)
                            transposes([(xn[:, b, k * P:(k + 1) * P], 0) for k in range(KC) for b in range(GT)],
                                       xT_psum)
                        if n == 1 and there(g - 2):
                            pe.wait_ge(mask_ready, g - 1)
                            when(pe, there(g - 1), x2_ready, (g - 1) * GT + 1)
                            pe.matmul(PJA[:, 0:E], earlier[:, :], msk16[:, 0, :], start=True, stop=True)
                            pe.matmul(PJA[:, E:2 * E], earlier[:, :], msk16[:, 1, :], start=True, stop=False)
                            pe.matmul(PJA[:, E:2 * E], ones16[:, :], msk16[:, 0, :], start=False, stop=True)
                            pe.matmul(PJA[:, 2 * E:3 * E], ones16[:, :], msk16[:, 0, :], start=True, stop=False)
                            pe.matmul(PJA[:, 2 * E:3 * E], ones16[:, :], msk16[:, 1, :], start=False,
                                      stop=True).then_inc(pos_psum, 1)
                        if n == 3 and there(g1):
                            pe.wait_ge(xT_ready, g1 + 1)
                            when(pe, there(g - 1), x2_ready, (g - 1) * GT + 1)
                            when(pe, there(g - 2), pos_read, g - 1)
                            when(pe, there(g), q_left, g + 1)
                            for o in range(2):
                                last = product(PJA[:, 256 * o:256 * o + 256], lambda k: wq[:, k, o * P:(o + 1) * P],
                                               lambda k: xT[:, k, :])
                            last.then_inc(q_psum, 1)
                        if there(g if n >= 1 else g - 1):
                            tg, m, i = (g, n - 1, par) if n >= 1 else (g - 1, QUADS - 1, p1)
                            odd, pairs = m % 2, range(4 * ((m % 4) // 2), 4 * ((m % 4) // 2) + 4)
                            tok = slice((m // 4) * P, (m // 4) * P + P)
                            pe.wait_ge(max_ready, tg * QUADS + m + 1)
                            when(pe, m >= 2 or there(tg - 1), exp_ready, tg * QUADS + m - 1)
                            ps = TB[m % 2]
                            for a in range(4):
                                pe.matmul(ps[:, a * P:(a + 1) * P], rowmax[m % 2][:, a:a + 1].to_broadcast([P, P]),
                                          negident[:, :], start=a == 0, stop=False)
                            for a, j in enumerate(pairs):
                                last = pe.matmul(ps[:, a * P:(a + 1) * P], kst[i][:, 2 * j + odd, tok],
                                                 qst[i][:, 2 * j + odd, tok], start=False, stop=a == 3)
                            last.then_inc(st_psum, 1)
                        if there(g if n >= 3 else g - 1):
                            tg, m, i = (g, n - 3, par) if n >= 3 else (g - 1, n + 5, p1)
                            b, odd, pairs = m // 4, m % 2, range(4 * ((m % 4) // 2), 4 * ((m % 4) // 2) + 4)
                            pe.wait_ge(probs_ready, tg * QUADS + m + 1)
                            if m == 0:
                                pe.wait_ge(va_ready, tg + 1)
                            if m % 4 == 0:
                                when(pe, b == 1 or there(tg - 1), ao_ready, tg * GT + b)
                            for a, j in enumerate(pairs):
                                h = 2 * j + odd
                                last = pe.matmul(OB[:, h * VA:(h + 1) * VA], probs[m % 4][:, a, :],
                                                 va[i][:, b, h, :], start=True, stop=True)
                            last.then_inc(pv_psum, 1)
                        if n == 2 and there(g1):
                            pe.wait_ge(k_left, g1 + 1)
                            for b in range(GT):
                                last = product(PJB[:, 256 * b:256 * b + 256], lambda k: cT[:, k, b * P:(b + 1) * P],
                                               lambda k: wv[:, k, :])
                            last.then_inc(v_psum, 1)
                        if n in (2, 6) and there(g - 1):
                            b = n // 4
                            pe.wait_ge(xn2_ready, (g - 1) * GT + b + 1)
                            free_bt(pe, g, 2 if n == 2 else 4)
                            transposes([(pay[p1][:, b, k * P:(k + 1) * P], 0) for k in range(KC)], x2T_psum)
                        if (n == 3 and there(g - 1)) or (n == 7 and there(g)):
                            b, tg = (1, g - 1) if n == 3 else (0, g)
                            pe.wait_ge(ao_ready, tg * GT + b + 1)
                            free_bt(pe, g, 3 if n == 3 else 5)
                            flat = ao[b][:, :, :].rearrange("p h v -> p (h v)")
                            transposes([(flat[:, k * P:(k + 1) * P], 0) for k in range(KC)], aoT_psum)
                        if n == 4 and there(g - 1):
                            pe.wait_ge(aoT_ready, (g - 1) * GT + 2)
                            when(pe, there(g1), va_ready, g1 + 1)
                            when(pe, there(g - 2), x2_ready, (g - 1) * GT)
                            product(PJB[:, 0:D], lambda k: aoT[1][:, k, :], lambda k: wo[:, k, :]).then_inc(o_psum, 1)
                        if n == 7 and there(g - 1):
                            pe.wait_ge(x2T_ready, g * GT)
                            when(pe, there(g1), q_left, g1 + 1)
                            when(pe, there(g - 2), pos_read, g - 1)
                            pe.wait_ge(x2_ready, g * GT)
                            for b in range(GT):
                                last = product(PJA[:, b * E:(b + 1) * E], lambda k: x2T[:, k, b * P:(b + 1) * P],
                                               lambda k: wr[:, k, :])
                            last.then_inc(r_psum, 1)

                loop_over_groups(pe, it)


def tile_table(dve, step, env):
    (region0, base, mostsel, wscale, wsquares, padrow, b1t, gscale, hscale, yscale, small, smallint,
     b1sq, padplace, most, mostint, tile_no_int, tile_no, past, te, ts, tile_expert,
     tile_row, numbers_made, pad_rows_ready, table_ready, b1_sums, b1_total, most_ready, most_total,
     scales_ready) = (env[k] for k in (
         "region0", "base", "mostsel", "wscale", "wsquares", "padrow", "b1t", "gscale", "hscale",
         "yscale", "small", "smallint", "b1sq", "padplace", "most", "mostint",
         "tile_no_int", "tile_no", "past", "te", "ts", "tile_expert", "tile_row", "numbers_made",
         "pad_rows_ready", "table_ready", "b1_sums", "b1_total", "most_ready", "most_total",
         "scales_ready"))
    dve.tensor_reduce(most[:, 0:1], mostsel[:, :], AX, ALU.max).then_inc(most_ready, 1)
    dve.tensor_copy(padplace[:, :], base[0:1, :]).then_inc(pad_rows_ready, 1)
    step(dve.tensor_tensor(b1sq[:, :, :], b1t[:, :, :], b1t[:, :, :], ALU.mult))
    dve.tensor_reduce(small[:, 0, :], b1sq[:, :, :], AX, ALU.add).then_inc(b1_sums, 1)
    step(dve.tensor_tensor(small[:, 2, :], base[:, :], region0[:, :], ALU.subtract))
    step(dve.tensor_scalar(smallint[:, 0, :], small[:, 2, :], float(TILE - 1), None, ALU.add))
    step(dve.tensor_scalar(smallint[:, 1, :], smallint[:, 0, :], TILE.bit_length() - 1, None, ALU.logical_shift_right))
    step.later(dve.memset(small[:, 4, :], 1.0))
    step(dve.tensor_copy(small[:, 3, :], smallint[:, 1, :]))
    step.later(dve.tensor_tensor_scan(small[:, 5, :], small[:, 4, :], small[:, 3, :], 0.0, ALU.mult, ALU.add))
    dve.wait_ge(numbers_made, 1)
    step(dve.tensor_copy(tile_no[:, :], tile_no_int))

    def by_tile(a):
        return a.unsqueeze(1).to_broadcast([1, ALL_TILES, E])

    step(dve.tensor_tensor(past[:, :, :], tile_no[:, :].unsqueeze(2).to_broadcast([1, ALL_TILES, E]),
                           by_tile(small[0:1, 5, :]), ALU.is_ge))
    step(dve.tensor_reduce(te[:, :], past[:, :, :], AX, ALU.add))
    step(dve.tensor_tensor(past[:, :, :], past[:, :, :], by_tile(small[0:1, 3, :]), ALU.mult))
    step.later(dve.tensor_scalar(tile_expert[:, :], te[:, :], float(E - 1), None, ALU.min))
    step(dve.tensor_reduce(ts[:, :], past[:, :, :], AX, ALU.add))
    step(dve.tensor_tensor(ts[:, :], tile_no[:, :], ts[:, :], ALU.subtract))
    step.later(dve.tensor_scalar(te[:, :], te[:, :], float(REG), None, ALU.mult))
    step(dve.tensor_scalar(ts[:, :], ts[:, :], float(TILE), None, ALU.mult))
    step(dve.tensor_tensor(ts[:, :], ts[:, :], te[:, :], ALU.add))
    step(dve.tensor_scalar(tile_row[:, :], ts[:, :], float(E * REG), None, ALU.min))
    dve.wait_ge(most_total, 1)
    dve.tensor_copy(mostint[:, :], most[:, 1:2]).then_inc(table_ready, 1)

    one = float(1 << 23)
    dve.tensor_scalar(gscale[:, :].bitcast(I32), wscale[:, 0, :].bitcast(I32), -1.0, 244 * one,
                      ALU.mult, ALU.add)
    dve.wait_ge(b1_total, 1)
    step(dve.scalar_tensor_tensor(out=small[:, 0, :], in0=wsquares[:, 0, :], scalar=256.0,
                                  in1=small[:, 1, :], op0=ALU.mult, op1=ALU.add))
    step(dve.tensor_scalar(small[:, 0, :], small[:, 0, :], 2.0, None, ALU.mult))
    step(dve.tensor_scalar(smallint[:, 0, :], small[:, 0, :].bitcast(I32), 24, None, ALU.logical_shift_right))
    step(dve.tensor_scalar(hscale[:, :].bitcast(I32), smallint[:, 0, :], -one, 204 * one,
                           ALU.mult, ALU.add))
    step.later(dve.tensor_scalar(small[:, 0, :].bitcast(I32), hscale[:, :].bitcast(I32), -1.0, 254 * one,
                                 ALU.mult, ALU.add))
    step(dve.tensor_scalar(small[:, 1, :].bitcast(I32), wscale[:, 1, :].bitcast(I32), -1.0, 254 * one,
                           ALU.mult, ALU.add))
    dve.tensor_tensor(yscale[:, :], small[:, 0, :], small[:, 1, :], ALU.mult).then_inc(scales_ready, 1)


def experts(nc, env):
    (out, b2, xs_dram, w_dram, bank, wts, ident, region0, base, mostsel, wscale, wsquares, padrow,
     b1t, all_slots, gscale, hscale, yscale, mostint, tile_expert, tile_row, weights_in, pads_in) = (
         env[k] for k in (
             "out", "b2", "xs_dram", "w_dram", "bank", "wts", "ident", "region0", "base", "mostsel",
             "wscale", "wsquares", "padrow", "b1t", "all_slots", "gscale", "hscale", "yscale",
             "mostint", "tile_expert", "tile_row", "weights_in", "pads_in"))
    with ExitStack() as stack:
        def sb(name, shape, dt=F32):
            return stack.enter_context(nc.sbuf_tensor(name, shape, dt))

        def sem(name):
            return stack.enter_context(nc.semaphore(name))

        b2_all = sb("b2_all", [P, E, D])
        xs = [sb(f"xs{i}", [P, 2, ROW]) for i in range(4)]
        xh = [sb(f"xh{i}", [P, 2, KC, TILE], F16) for i in range(2)]
        hf = sb("hf", [P, HC, TILE])
        hh = [sb(f"hh{i}", [P, 2, HC, TILE], F16) for i in range(2)]
        yb = [sb(f"yb{i}", [P, 2, D]) for i in range(2)]
        yg = [sb(f"yg{i}", [P, 2, D]) for i in range(2)]
        tie_idx = sb("tie_idx", [P, 8], I32)
        tie_row = sb("tie_row", [P, ROW])

        XT = bank[0]
        HB = bank[1:5]
        YB = [bank[5], bank[6]]

        b2_in, ties_in = sem("b2_in"), sem("ties_in")
        rows_placed = sem("rows_placed")
        row_in = [sem(f"row_in{i}") for i in range(4)]
        added = [sem(f"added{i}") for i in range(2)]
        xT_psum, xhi_ready, xlo_ready = sem("xT_psum"), sem("xhi_ready"), sem("xlo_ready")
        h_psum, gelu_ready, split_ready = sem("h_psum"), sem("gelu_ready"), sem("split_ready")
        y_psum, yb_ready, yg_ready = sem("y_psum"), sem("yb_ready"), sem("yg_ready")
        dve_steps, pool_steps, waits_taken = sem("dve_steps"), sem("pool_steps"), sem("waits_taken")

        def settled(eng):
            eng.sem_inc(waits_taken, 1)

        def pipeline(eng, it, lo, hi):
            def peeled(a, b):
                for i in range(a, b):
                    it(i, i % 4, lambda k, i=i: lo <= i + k < hi)

            first = -(-(lo + 1) // 4) * 4
            rounds = (hi - 3 - first) // 4
            peeled(lo - 2, first)
            with eng.Fori(0, rounds) as u:
                for m in range(4):
                    it(u * 4 + (first + m), m, lambda k: True)
            peeled(first + 4 * rounds, hi)

        def all_tiles(eng, it):
            pipeline(eng, it, 0, MAIN_TILES)
            ties = eng.value_load(mostint[0:1, 0:1], min_val=0, max_val=E)
            with eng.If(ties > 2):
                pipeline(eng, it, MAIN_TILES, ALL_TILES)

        def when(eng, ok, s, value):
            if ok:
                eng.wait_ge(s, value)

        def before(i, n):
            return i >= n if isinstance(i, int) else True

        def expert_of(eng, i):
            return eng.value_load(tile_expert[0:1, bass.ds(i, 1)], min_val=0, max_val=E - 1)

        def added_value(i):
            return i * 16 + 16

        with nc.Block() as block:

            @block.sync
            def _(sp):
                sp.wait_ge(rows_placed, 1)
                sp.wait_ge(pads_in, 16 * E)

                def it(i, m, there):
                    if there(2):
                        j = i + 2
                        when(sp, before(j, 4), added[1], added_value(i - 2))
                        settled(sp)
                        row = sp.value_load(tile_row[0:1, bass.ds(j, 1)], min_val=0, max_val=E * REG)
                        sp.dma_start(xs[(m + 2) % 4][:, :, :],
                                     xs_dram[bass.ds(row, TILE), :].rearrange("(h p) r -> p h r", h=2)
                                     ).then_inc(row_in[(m + 2) % 4], 16)
                    if isinstance(i, int) and i == -1:
                        sp.dma_start(b2_all[:, :, :].rearrange("p e d -> p (e d)"), b2.partition_broadcast(P)).then_inc(b2_in, 16)
                    if isinstance(i, int) and -1 <= i <= 1:
                        for e in {-1: (EARLY,), 0: (EARLY + 1,), 1: range(EARLY + 2, E)}[i]:
                            sp.wait_ge(weights_in, 16 * 2 * e)
                            load_weights(sp, wts, w_dram, e, weights_in)

                all_tiles(sp, it)
                sp.wait_ge(weights_in, 16 * 2 * E)
                sp.wait_ge(b2_in, 16)

            @block.gpsimd
            def _(pool):
                step = Links(pool, pool_steps)
                ties = pool.value_load(mostint[0:1, 0:1], min_val=0, max_val=E)
                with pool.If(ties > 2):
                    with pool.Fori(0, B) as t:
                        step(pool.tensor_copy(tie_idx[:, :], all_slots[:, bass.ds(t, 1), :].rearrange("p a r -> p (a r)")))
                        pool.indirect_dma_start(out=tie_row[:, :], out_offset=None, in_=xs_dram[:, :],
                                                in_offset=bass.IndirectOffsetOnAxis(ap=tie_idx[:, 0:1], axis=0)
                                                ).then_inc(ties_in, 16)
                        pool.wait_ge(ties_in, t * (16 * 7) + 16)
                        settled(pool)
                        for r in range(2, 8):
                            pool.indirect_dma_start(out=xs_dram[:, :],
                                                    out_offset=bass.IndirectOffsetOnAxis(ap=tie_idx[:, r:r + 1], axis=0),
                                                    in_=tie_row[:, :], in_offset=None, bounds_check=E * REG - 1,
                                                    oob_is_err=False).then_inc(ties_in, 16)
                        pool.wait_ge(ties_in, t * (16 * 7) + 16 * 7)
                        settled(pool)
                        step.restart()
                pool.sem_inc(rows_placed, 1)

                def it(i, m, there):
                    if there(0):
                        for half in range(2):
                            pool.wait_ge(yg_ready, i * 2 + half + 1)
                            when(pool, half == 1 or before(i, 1), added[1 - half],
                                 added_value(i if half == 1 else i - 1))
                            settled(pool)
                            numbers = xs[m][:, half, D + E:D + E + 1].bitcast(I32)
                            pool.indirect_dma_start(
                                out=out[:, :], out_offset=bass.IndirectOffsetOnAxis(ap=numbers, axis=0),
                                in_=yg[m % 2][:, half, :], in_offset=None, compute_op=ALU.add
                                ).then_inc(added[half], 16)

                def last(tiles):
                    for half in range(2):
                        pool.wait_ge(added[half], added_value(tiles - 1))

                pipeline(pool, it, 0, MAIN_TILES)
                last(MAIN_TILES)
                ties = pool.value_load(mostint[0:1, 0:1], min_val=0, max_val=E)
                with pool.If(ties > 2):
                    pipeline(pool, it, MAIN_TILES, ALL_TILES)
                    last(ALL_TILES)

            @block.scalar
            def _(act):
                def it(i, m, there):
                    if there(2):
                        act.wait_ge(xT_psum, i + 3)
                        when(act, before(i + 2, 2), h_psum, (i + 1) * 4)
                        act.activation(xh[m % 2][:, 0, :, :], XT[:, :].rearrange("p (k t) -> p k t", k=KC), ACT.Copy,
                                       scale=X_SCALE).then_inc(xhi_ready, 1)
                    if there(1):
                        e = expert_of(act, i + 1)
                        for quarter in range(4):
                            act.wait_ge(h_psum, (i + 1) * 4 + quarter + 1)
                            when(act, before(i + 1, 1), split_ready, i * 4 + quarter + 1)
                            for c in (2 * quarter, 2 * quarter + 1):
                                last = act.activation(
                                    hf[:, c, :], HB[quarter][:, c % 2 * TILE:(c % 2 + 1) * TILE],
                                    ACT.Gelu, bias=b1t[:, bass.ds(e, 1), c], scale=gscale[:, bass.ds(e, 1)])
                            last.then_inc(gelu_ready, 1)
                    if there(0):
                        e = expert_of(act, i)
                        act.wait_ge(yb_ready, i + 1)
                        when(act, before(i, 2), added[1], added_value(i - 2))
                        for half in range(2):
                            act.activation(yg[m % 2][:, half, :], yb[m % 2][:, half, :], ACT.Copy,
                                           scale=xs[m][:, half, bass.ds(e + D, 1)]).then_inc(yg_ready, 1)

                all_tiles(act, it)

            @block.vector
            def _(dve):
                step = Links(dve, dve_steps)

                def it(i, m, there):
                    if there(2):
                        dve.wait_ge(xhi_ready, i + 3)
                        dve.scalar_tensor_tensor(out=xh[m % 2][:, 1, :, :].rearrange("p k t -> p (k t)"),
                                                 in0=XT[:, :], scalar=X_SCALE,
                                                 in1=xh[m % 2][:, 0, :, :].rearrange("p k t -> p (k t)"),
                                                 op0=ALU.mult, op1=ALU.subtract).then_inc(xlo_ready, 1)
                    if there(1):
                        e = expert_of(dve, i + 1)
                        b = (m + 1) % 2
                        for quarter in range(4):
                            c = slice(2 * quarter, 2 * quarter + 2)
                            dve.wait_ge(gelu_ready, (i + 1) * 4 + quarter + 1)
                            when(dve, quarter == 0 and before(i + 1, 2), y_psum, i)
                            high = hh[b][:, 0, c, :].rearrange("p c t -> p (c t)")
                            full = hf[:, c, :].rearrange("p c t -> p (c t)")
                            step(dve.tensor_scalar(high, full, hscale[:, bass.ds(e, 1)], None, ALU.mult))
                            dve.scalar_tensor_tensor(out=hh[b][:, 1, c, :].rearrange("p c t -> p (c t)"), in0=full,
                                                     scalar=hscale[:, bass.ds(e, 1)], in1=high,
                                                     op0=ALU.mult, op1=ALU.subtract).then_inc(split_ready, 1)
                    if there(0):
                        e = expert_of(dve, i)
                        if isinstance(i, int) and i == 0:
                            dve.wait_ge(b2_in, 16)
                        dve.wait_ge(y_psum, i + 1)
                        when(dve, before(i, 2), yg_ready, (i - 1) * 2)
                        dve.scalar_tensor_tensor(out=yb[m % 2][:, :, :],
                                                 in0=YB[m % 2][:, :].rearrange("p (h d) -> p h d", h=2),
                                                 scalar=yscale[:, bass.ds(e, 1)],
                                                 in1=b2_all[:, bass.ds(e, 1), :].to_broadcast([P, 2, D]),
                                                 op0=ALU.mult, op1=ALU.add).then_inc(yb_ready, 1)
                    settled(dve)
                    step.restart()

                settled(dve)
                step.restart()
                all_tiles(dve, it)

            @block.tensor
            def _(pe):
                expert = {}

                def it(i, m, there):
                    if there(0):
                        expert[0] = expert[1] if m > 0 and not isinstance(i, int) else expert_of(pe, i)
                    if there(1):
                        expert[1] = expert_of(pe, i + 1)
                    if there(2):
                        pe.wait_ge(row_in[(m + 2) % 4], row_value(i + 2, (m + 2) % 4))
                        when(pe, before(i + 2, 1), xlo_ready, i + 2)
                        for k in range(KC):
                            for half in range(2):
                                at = k * TILE + half * P
                                last = pe.transpose(XT[:, at:at + P], xs[(m + 2) % 4][:, half, k * P:(k + 1) * P],
                                                    ident[:, :])
                        last.then_inc(xT_psum, 1)
                    if there(1):
                        b = (m + 1) % 2
                        terms = [(wp, xp, k) for wp, xp in ((0, 0), (0, 1), (1, 0)) for k in range(KC)]
                        pe.wait_ge(xlo_ready, i + 2)
                        pe.wait_ge(weights_in, expert[1] * (16 * 2) + 16 * 2)
                        settled(pe)
                        for c in range(HC):
                            when(pe, c % 2 == 0 and before(i + 1, 1), gelu_ready, i * 4 + c // 2 + 1)
                            for q, (wp, xp, k) in enumerate(terms):
                                at = wp * 2048 + k * H + c * P
                                last = pe.matmul(HB[c // 2][:, c % 2 * TILE:(c % 2 + 1) * TILE],
                                                 wts[:, bass.ds(expert[1], 1), at:at + P], xh[b][:, xp, k, :],
                                                 start=q == 0, stop=q == 5)
                            if c % 2 == 1:
                                last.then_inc(h_psum, 1)
                    if there(0):
                        b = m % 2
                        when(pe, before(i, 2), yb_ready, i - 1)
                        terms = [(hp, wp, c) for quarter in range(4) for hp, wp in ((0, 0), (1, 0), (0, 1))
                                 for c in (2 * quarter, 2 * quarter + 1)]
                        for half in range(2):
                            for q, (hp, wp, c) in enumerate(terms):
                                if half == 0 and q % 6 == 0:
                                    pe.wait_ge(split_ready, i * 4 + q // 6 + 1)
                                at = 4096 + wp * 2048 + c * D
                                last = pe.matmul(YB[b][:, half * D:(half + 1) * D],
                                                 hh[b][:, hp, c, half * P:(half + 1) * P],
                                                 wts[:, bass.ds(expert[0], 1), at:at + D], start=q == 0, stop=q == 23)
                        last.then_inc(y_psum, 1)

                def row_value(i, m):
                    return (i - m) * 4 + 16

                all_tiles(pe, it)


def kernel(**inputs):
    import numpy as np
    import concourse.bacc as bacc
    from concourse.bass_utils import run_bass_kernel_spmd as run

    a = {k: np.asarray(v) for k, v in inputs.items()}
    order = np.arange(D).reshape(PAIRS, 2, DK).transpose(1, 2, 0).reshape(D)

    def w(name):
        return a["L0_xattn_w_" + name].T

    def bias(name):
        return a["L0_xattn_b_" + name]

    arrays = {
        "x": a["x"].reshape(T, D),
        "ctx_in": a["ctx_1024"].reshape(T, D),
        "g_xattn": a["g_xattn"], "g_ffn": a["g_ffn"],
        "w_q": w("q")[:, order], "b_q": bias("q")[order].reshape(2, P).T,
        "w_k": w("k")[:, order], "b_k": bias("k")[order].reshape(2, P).T,
        "w_v": w("v"), "b_v": bias("v"), "w_o": w("o"), "b_o": bias("o"),
        "W1": a["L0_ffn_W1"], "b1": a["L0_ffn_b1"].reshape(E, HC, P).transpose(2, 0, 1),
        "W2": a["L0_ffn_W2"], "b2": a["L0_ffn_b2"].reshape(E * D),
        "Wr": a["L0_ffn_Wr"], "br": a["L0_ffn_br"],
    }
    arrays = {k: np.ascontiguousarray(v) for k, v in arrays.items()}
    nc = bacc.Bacc("TRN2", target_bir_lowering=False, num_devices=1)
    aps = [nc.dram_tensor(f"in_{k}", v.shape, mybir.dt.from_np(v.dtype), kind="ExternalInput").ap()
           for k, v in arrays.items()]
    out = nc.dram_tensor("out_rows", [T + P, D], F32, kind="ExternalOutput").ap()
    bass_flamingo(nc, *aps, out)
    r = run(nc, [{f"in_{k}": v for k, v in arrays.items()}], core_ids=[0])
    return r.results[0]["out_rows"][:T].reshape(B, S, D)
```
